# Optimizing a Trainium2 kernel written in Bass

```python
import numpy as np
import jax
import jax.numpy as jnp

def _softmax(x, axis=-1):
    return jax.nn.softmax(x, axis=axis)

def _gelu(x):
    return jax.nn.gelu(x, approximate=True)

def _silu(x):
    return jax.nn.silu(x)

def _sigmoid(x):
    return jax.nn.sigmoid(x)

def _layernorm(x, axis=-1, eps=1e-05):
    m = jnp.mean(x, axis=axis, keepdims=True)
    v = jnp.var(x, axis=axis, keepdims=True)
    return (x - m) / jnp.sqrt(v + eps)

def _scatter_add(tgt, idx, src, axis=0):
    return tgt.at[idx].add(src)

def _segment_sum(src, seg, n):
    return jax.ops.segment_sum(src, seg, n)
kernel_name = 'mk_gnn_ffn_d2_gnn_r8_2780ec'

def setup_inputs(seed: int=0):
    np.random.seed(seed)
    _w = jnp.asarray

    def _rec_inputs():
        import jax
        import jax.numpy as jnp
        _gk = jax.random.key(seed)
        x = -0.0001126 + 1 * jax.random.normal(jax.random.fold_in(_gk, 1), (1250, 768), jnp.float32)
        src = jax.random.randint(jax.random.fold_in(_gk, 2), (40000,), 0, 1250, jnp.int32)
        dst = jax.random.randint(jax.random.fold_in(_gk, 3), (40000,), 0, 1250, jnp.int32)
        _o = jnp.argsort(dst, stable=True)
        src = src[_o]
        dst = dst[_o]
        edge_type_3 = jax.random.randint(jax.random.fold_in(_gk, 12), (40000,), 0, 3, jnp.int32)
        node_type_3 = jax.random.randint(jax.random.fold_in(_gk, 13), (1250,), 0, 3, jnp.int32)
        return (x, src, dst, edge_type_3, node_type_3)
    x, src, dst, edge_type_3, node_type_3 = _rec_inputs()

    def _L0_gnn_setup():
        import jax, jax.numpy as jnp
        import numpy as np
        NUM_NODES = 1250
        NUM_EDGES = 20000
        IN_CH = 768
        TYPE_DIM = 128
        HID = 768
        OUT = 768
        NUM_REL = 3
        NUM_NODE_TYPE = 3

        def _glorot(key, shape):
            fan_in, fan_out = (shape[-2], shape[-1])
            lim = (6.0 / (fan_in + fan_out)) ** 0.5
            return jax.random.uniform(key, shape, jnp.float32, -lim, lim)

        def rgcn_conv(h, src, dst, edge_type, w_rel, w_root, bias):
            num_nodes = h.shape[0]
            xw = jnp.einsum('nd,rde->rne', h, w_rel)
            msg = xw[edge_type, src]
            onehot = jax.nn.one_hot(edge_type, NUM_REL, dtype=h.dtype)
            count = jax.ops.segment_sum(onehot, dst, num_segments=num_nodes)
            inv = jnp.where(count > 0, 1.0 / jnp.maximum(count, 1.0), 0.0)
            msg = msg * inv[dst, edge_type][:, None]
            agg = jax.ops.segment_sum(msg, dst, num_segments=num_nodes)
            return agg + h @ w_root + bias
        key = jax.random.key(seed)
        ks = jax.random.split(key, 16)
        d1 = IN_CH + TYPE_DIM
        inp = {'x': jax.random.normal(ks[0], (NUM_NODES, IN_CH), jnp.float32), 'node_type': jax.random.randint(ks[1], (NUM_NODES,), 0, NUM_NODE_TYPE, jnp.int32), 'edge_index': jax.random.randint(ks[2], (2, NUM_EDGES), 0, NUM_NODES, jnp.int32), 'edge_type': jax.random.randint(ks[3], (NUM_EDGES,), 0, NUM_REL, jnp.int32), 'node_emb': jax.random.normal(ks[4], (NUM_NODE_TYPE, TYPE_DIM), jnp.float32), 'w_rel1': _glorot(ks[5], (NUM_REL, d1, d1)), 'w_root1': _glorot(ks[6], (d1, d1)), 'b1': jnp.zeros((d1,), jnp.float32), 'w_rel2': _glorot(ks[7], (NUM_REL, d1, HID)), 'w_root2': _glorot(ks[8], (d1, HID)), 'b2': jnp.zeros((HID,), jnp.float32), 'w_rel3': _glorot(ks[9], (NUM_REL, HID, OUT)), 'w_root3': _glorot(ks[10], (HID, OUT)), 'b3': jnp.zeros((OUT,), jnp.float32)}
        return inp
    _L0_gnn_all = _L0_gnn_setup()
    _L0_gnn_in = {k: v for k, v in _L0_gnn_all.items() if k in ('node_emb', 'w_rel1', 'w_root1', 'b1', 'w_rel2', 'w_root2', 'b2', 'w_rel3', 'w_root3', 'b3')}
    del _L0_gnn_all

    def _L0_ffn_setup():
        import jax, jax.numpy as jnp
        import numpy as np
        D_MODEL = 768
        D_FF = 384
        NUM_EXPERTS = 8
        EXPERT_CAPACITY = 1024
        key = jax.random.key(seed)
        k0, k1, k2, k3 = jax.random.split(key, 4)
        hidden_states = jax.random.normal(k0, (2, 1024, D_MODEL), dtype=jnp.float32)
        router_w = jax.random.normal(k1, (D_MODEL, NUM_EXPERTS), dtype=jnp.float32) * D_MODEL ** (-0.5)
        wi = jax.random.normal(k2, (NUM_EXPERTS, D_MODEL, D_FF), dtype=jnp.float32) * D_MODEL ** (-0.5)
        wo = jax.random.normal(k3, (NUM_EXPERTS, D_FF, D_MODEL), dtype=jnp.float32) * D_FF ** (-0.5)
        return {'hidden_states': hidden_states, 'router_w': router_w, 'wi': wi, 'wo': wo}
    _L0_ffn_all = _L0_ffn_setup()
    _L0_ffn_in = {k: v for k, v in _L0_ffn_all.items() if k in ('router_w', 'wi', 'wo')}
    del _L0_ffn_all

    def _L1_gnn_setup():
        import jax, jax.numpy as jnp
        import numpy as np
        N_NODES = 1250
        N_EDGES = 12500
        DIM = 768
        key = jax.random.key(seed)
        k1, k2, k3, k4 = jax.random.split(key, 4)
        x = jax.random.normal(k1, (N_NODES, DIM), dtype=jnp.float32)
        edge_index = jax.random.randint(k2, (2, N_EDGES), 0, N_NODES, dtype=jnp.int32)
        W = jax.random.normal(k3, (DIM, DIM), dtype=jnp.float32) / np.sqrt(DIM)
        b = jnp.zeros((DIM,), dtype=jnp.float32)
        return {'x': x, 'edge_index': edge_index, 'W': W, 'b': b}
    _L1_gnn_all = _L1_gnn_setup()
    _L1_gnn_in = {k: v for k, v in _L1_gnn_all.items() if k in ('W', 'b')}
    del _L1_gnn_all

    def _L1_ffn_setup():
        import jax, jax.numpy as jnp
        import numpy as np
        B, N, D, H, E, HID, TOPK = (8, 197, 768, 12, 8, 384, 2)

        def _layernorm(x, w, b, eps=1e-05):
            mu = jnp.mean(x, axis=-1, keepdims=True)
            var = jnp.mean((x - mu) ** 2, axis=-1, keepdims=True)
            return (x - mu) * jax.lax.rsqrt(var + eps) * w + b
        key = jax.random.key(seed)
        ks = jax.random.split(key, 8)
        s = 0.02
        return {'x': jax.random.normal(ks[0], (B, N, D), jnp.float32), 'norm1_w': jnp.ones((D,), jnp.float32), 'norm1_b': jnp.zeros((D,), jnp.float32), 'qkv_w': jax.random.normal(ks[1], (3 * D, D), jnp.float32) * s, 'qkv_b': jnp.zeros((3 * D,), jnp.float32), 'proj_w': jax.random.normal(ks[2], (D, D), jnp.float32) * s, 'proj_b': jnp.zeros((D,), jnp.float32), 'norm2_w': jnp.ones((D,), jnp.float32), 'norm2_b': jnp.zeros((D,), jnp.float32), 'w_gate': jax.random.normal(ks[3], (D, E), jnp.float32) * s, 'W1': jax.random.normal(ks[4], (E, D, HID), jnp.float32) * s, 'b1': jnp.zeros((E, HID), jnp.float32), 'W2': jax.random.normal(ks[5], (E, HID, D), jnp.float32) * s, 'b2': jnp.zeros((E, D), jnp.float32)}
    _L1_ffn_all = _L1_ffn_setup()
    _L1_ffn_in = {k: v for k, v in _L1_ffn_all.items() if k in ('norm1_w', 'norm1_b', 'qkv_w', 'qkv_b', 'proj_w', 'proj_b', 'norm2_w', 'norm2_b', 'w_gate', 'W1', 'b1', 'W2', 'b2')}
    del _L1_ffn_all
    return {'x': x, 'src': src, 'dst': dst, 'edge_type_3': edge_type_3, 'node_type_3': node_type_3, 'L0_gnn_node_emb': _L0_gnn_in['node_emb'], 'L0_gnn_w_rel1': _L0_gnn_in['w_rel1'], 'L0_gnn_w_root1': _L0_gnn_in['w_root1'], 'L0_gnn_b1': _L0_gnn_in['b1'], 'L0_gnn_w_rel2': _L0_gnn_in['w_rel2'], 'L0_gnn_w_root2': _L0_gnn_in['w_root2'], 'L0_gnn_b2': _L0_gnn_in['b2'], 'L0_gnn_w_rel3': _L0_gnn_in['w_rel3'], 'L0_gnn_w_root3': _L0_gnn_in['w_root3'], 'L0_gnn_b3': _L0_gnn_in['b3'], 'L0_ffn_router_w': _L0_ffn_in['router_w'], 'L0_ffn_wi': _L0_ffn_in['wi'], 'L0_ffn_wo': _L0_ffn_in['wo'], 'L1_gnn_W': _L1_gnn_in['W'], 'L1_gnn_b': _L1_gnn_in['b'], 'L1_ffn_norm1_w': _L1_ffn_in['norm1_w'], 'L1_ffn_norm1_b': _L1_ffn_in['norm1_b'], 'L1_ffn_qkv_w': _L1_ffn_in['qkv_w'], 'L1_ffn_qkv_b': _L1_ffn_in['qkv_b'], 'L1_ffn_proj_w': _L1_ffn_in['proj_w'], 'L1_ffn_proj_b': _L1_ffn_in['proj_b'], 'L1_ffn_norm2_w': _L1_ffn_in['norm2_w'], 'L1_ffn_norm2_b': _L1_ffn_in['norm2_b'], 'L1_ffn_w_gate': _L1_ffn_in['w_gate'], 'L1_ffn_W1': _L1_ffn_in['W1'], 'L1_ffn_b1': _L1_ffn_in['b1'], 'L1_ffn_W2': _L1_ffn_in['W2'], 'L1_ffn_b2': _L1_ffn_in['b2']}

def reference(x, src, dst, edge_type_3, node_type_3, L0_gnn_node_emb, L0_gnn_w_rel1, L0_gnn_w_root1, L0_gnn_b1, L0_gnn_w_rel2, L0_gnn_w_root2, L0_gnn_b2, L0_gnn_w_rel3, L0_gnn_w_root3, L0_gnn_b3, L0_ffn_router_w, L0_ffn_wi, L0_ffn_wo, L1_gnn_W, L1_gnn_b, L1_ffn_norm1_w, L1_ffn_norm1_b, L1_ffn_qkv_w, L1_ffn_qkv_b, L1_ffn_proj_w, L1_ffn_proj_b, L1_ffn_norm2_w, L1_ffn_norm2_b, L1_ffn_w_gate, L1_ffn_W1, L1_ffn_b1, L1_ffn_W2, L1_ffn_b2):
    import jax
    import jax.numpy as jnp

    def _L0_gnn_ref(x, node_type, edge_index, edge_type, node_emb, w_rel1, w_root1, b1, w_rel2, w_root2, b2, w_rel3, w_root3, b3):
        import jax, jax.numpy as jnp
        import numpy as np
        NUM_NODES = 1250
        NUM_EDGES = 20000
        IN_CH = 768
        TYPE_DIM = 128
        HID = 768
        OUT = 768
        NUM_REL = 3
        NUM_NODE_TYPE = 3

        def _glorot(key, shape):
            fan_in, fan_out = (shape[-2], shape[-1])
            lim = (6.0 / (fan_in + fan_out)) ** 0.5
            return jax.random.uniform(key, shape, jnp.float32, -lim, lim)

        def rgcn_conv(h, src, dst, edge_type, w_rel, w_root, bias):
            num_nodes = h.shape[0]
            xw = jnp.einsum('nd,rde->rne', h, w_rel)
            msg = xw[edge_type, src]
            onehot = jax.nn.one_hot(edge_type, NUM_REL, dtype=h.dtype)
            count = jax.ops.segment_sum(onehot, dst, num_segments=num_nodes)
            inv = jnp.where(count > 0, 1.0 / jnp.maximum(count, 1.0), 0.0)
            msg = msg * inv[dst, edge_type][:, None]
            agg = jax.ops.segment_sum(msg, dst, num_segments=num_nodes)
            return agg + h @ w_root + bias
        src, dst = (edge_index[0], edge_index[1])
        h = jnp.concatenate([x, node_emb[node_type]], axis=-1)
        h = jax.nn.relu(rgcn_conv(h, src, dst, edge_type, w_rel1, w_root1, b1))
        h = jax.nn.relu(rgcn_conv(h, src, dst, edge_type, w_rel2, w_root2, b2))
        h = jax.nn.relu(rgcn_conv(h, src, dst, edge_type, w_rel3, w_root3, b3))
        return h

    def _L0_ffn_ref(hidden_states, router_w, wi, wo):
        import jax, jax.numpy as jnp
        import numpy as np
        D_MODEL = 768
        D_FF = 384
        NUM_EXPERTS = 8
        EXPERT_CAPACITY = 1024
        B, S, d = hidden_states.shape
        E = router_w.shape[1]
        x = hidden_states.reshape(-1, d)
        logits = x.astype(jnp.float32) @ router_w.astype(jnp.float32)
        probs = jax.nn.softmax(logits, axis=-1).astype(x.dtype)
        p = jnp.max(probs, axis=-1)
        e_idx = jnp.argmax(probs, axis=-1)
        mask = jax.nn.one_hot(e_idx, E, dtype=x.dtype)
        token_priority = jnp.cumsum(mask[:, None, :], axis=-2)[:, 0, :]
        mask = mask * (token_priority <= EXPERT_CAPACITY).astype(x.dtype)
        combine = mask * p[:, None]

        def body(acc, ew):
            Wi_e, Wo_e, w_e = ew
            h = jax.nn.relu(x @ Wi_e) @ Wo_e
            return (acc + w_e[:, None] * h, None)
        out, _ = jax.lax.scan(body, jnp.zeros_like(x), (wi, wo, combine.T))
        return out.reshape(B, S, d)

    def _L1_gnn_ref(x, edge_index, W, b):
        import jax, jax.numpy as jnp
        import numpy as np
        N_NODES = 1250
        N_EDGES = 12500
        DIM = 768
        n = x.shape[0]
        loop = jnp.arange(n, dtype=edge_index.dtype)
        src = jnp.concatenate([edge_index[0], loop])
        dst = jnp.concatenate([edge_index[1], loop])
        deg = jax.ops.segment_sum(jnp.ones_like(dst, dtype=x.dtype), dst, num_segments=n)
        deg_inv_sqrt = jnp.where(deg > 0, jax.lax.rsqrt(deg), 0.0)
        norm = deg_inv_sqrt[src] * deg_inv_sqrt[dst]
        h = x @ W
        msg = h[src] * norm[:, None]
        out = jax.ops.segment_sum(msg, dst, num_segments=n)
        return out + b

    def _L1_ffn_ref(x, norm1_w, norm1_b, qkv_w, qkv_b, proj_w, proj_b, norm2_w, norm2_b, w_gate, W1, b1, W2, b2):
        import jax, jax.numpy as jnp
        import numpy as np
        B, N, D, H, E, HID, TOPK = (8, 197, 768, 12, 8, 384, 2)

        def _layernorm(x, w, b, eps=1e-05):
            mu = jnp.mean(x, axis=-1, keepdims=True)
            var = jnp.mean((x - mu) ** 2, axis=-1, keepdims=True)
            return (x - mu) * jax.lax.rsqrt(var + eps) * w + b
        Bx, Nx, C = x.shape
        hd = C // H
        scale = hd ** (-0.5)
        xn = _layernorm(x, norm1_w, norm1_b)
        qkv = (xn @ qkv_w.T + qkv_b).reshape(Bx, Nx, 3, H, hd).transpose(2, 0, 3, 1, 4)
        q, k, v = (qkv[0], qkv[1], qkv[2])
        attn = jax.nn.softmax(jnp.einsum('bhqd,bhkd->bhqk', q, k) * scale, axis=-1)
        o = jnp.einsum('bhqk,bhkd->bqhd', attn, v).reshape(Bx, Nx, C)
        x = x + (o @ proj_w.T + proj_b)
        xn2 = _layernorm(x, norm2_w, norm2_b).reshape(-1, C)
        T = xn2.shape[0]
        logits = xn2 @ w_gate
        top_vals, top_idx = jax.lax.top_k(logits, TOPK)
        gates = jax.nn.softmax(top_vals, axis=-1)
        gates_full = jnp.zeros((T, E), xn2.dtype).at[jnp.arange(T)[:, None], top_idx].add(gates)

        def body(acc, p):
            w1, bb1, w2, bb2, g = p
            h = jax.nn.gelu(xn2 @ w1 + bb1, approximate=False)
            return (acc + g[:, None] * (h @ w2 + bb2), None)
        moe_out, _ = jax.lax.scan(body, jnp.zeros_like(xn2), (W1, b1, W2, b2, gates_full.T))
        return x + moe_out.reshape(Bx, Nx, C)
    edge_index = jnp.stack([src, dst])
    x = x + _L0_gnn_ref(_layernorm(x, axis=-1), node_type_3, edge_index, edge_type_3, L0_gnn_node_emb, L0_gnn_w_rel1, L0_gnn_w_root1, L0_gnn_b1, L0_gnn_w_rel2, L0_gnn_w_root2, L0_gnn_b2, L0_gnn_w_rel3, L0_gnn_w_root3, L0_gnn_b3)
    x = x + _L0_ffn_ref(_layernorm(x, axis=-1)[None], L0_ffn_router_w, L0_ffn_wi, L0_ffn_wo)[0]
    x = x + _L1_gnn_ref(_layernorm(x, axis=-1), edge_index, L1_gnn_W, L1_gnn_b)
    x = x + _L1_ffn_ref(_layernorm(x, axis=-1)[None], L1_ffn_norm1_w, L1_ffn_norm1_b, L1_ffn_qkv_w, L1_ffn_qkv_b, L1_ffn_proj_w, L1_ffn_proj_b, L1_ffn_norm2_w, L1_ffn_norm2_b, L1_ffn_w_gate, L1_ffn_W1, L1_ffn_b1, L1_ffn_W2, L1_ffn_b2)[0]
    return x

_drawn_inputs = setup_inputs


def setup_inputs(seed=0):
    import zlib

    import numpy as np

    out = dict(_drawn_inputs(seed))
    spreads = {'L0_gnn_b1': (0.0, 0.1),
     'L0_gnn_b2': (0.0, 0.1),
     'L0_gnn_b3': (0.0, 0.1),
     'L1_gnn_b': (0.0, 0.1),
     'L1_ffn_norm1_w': (1.0, 0.6),
     'L1_ffn_norm1_b': (0.0, 0.588),
     'L1_ffn_qkv_b': (0.0, 0.322),
     'L1_ffn_proj_b': (0.0, 0.1),
     'L1_ffn_norm2_w': (1.0, 0.6),
     'L1_ffn_norm2_b': (0.0, 0.605),
     'L1_ffn_b1': (0.0, 0.8),
     'L1_ffn_b2': (0.0, 0.304)}
    factors = {}
    for name, (base, spread) in spreads.items():
        noise = np.random.default_rng([zlib.crc32(name.encode()), seed]).standard_normal(out[name].shape)
        drawn = base * np.exp(spread * noise) if base else spread * noise
        out[name] = jnp.asarray(drawn.astype(out[name].dtype))
    for name, factor in factors.items():
        out[name] = (out[name] * factor).astype(out[name].dtype)
    return out
```

```python
from contextlib import ExitStack

import concourse.bass as bass
from concourse import mybir

F32, F16 = mybir.dt.float32, mybir.dt.float16
I32, U32 = mybir.dt.int32, mybir.dt.uint32
ALU = mybir.AluOpType
ACT = mybir.ActivationFunctionType
AX_X = mybir.AxisListType.X

N = 1250
TP = 125
NT = N // TP
D = 768
KD = D // 128
NREL = 3
EP = 125
NBUCKET = NREL * NT
EXPERTS = 8
HID = 384
KH = HID // 128
HEADS = 12
HD = 64
QC = 2 * TP
LAYERS = ((7, 896, "1"), (7, 768, "2"), (6, 768, "3"))
WMAX = 7 * 448
NODE_COLS = ((0, 418), (418, 416), (834, 416))
BANKS3 = ((0, 512), (512, 512), (1024, 226))
RING = 4
UNIT = 2


def build(nc, a, out):
    E = a["src"].shape[0]
    EJ = E // EP
    UNITS = E // (UNIT * 128) + NBUCKET + 1
    ETILES = UNIT * UNITS
    PAD_EDGE = (N + 50) * 128 + 127

    ctx = ExitStack()
    with ctx:
        sems = {}

        def sem(name):
            if name not in sems:
                sems[name] = ctx.enter_context(nc.semaphore(name))
            return sems[name]

        def sb(name, shape, dt=F32, scope=ctx):
            return scope.enter_context(nc.sbuf_tensor(name, shape, dt))

        ident = sb("ident", [128, 128])
        bias_b = sb("bias_b", [128, 896])
        inv_cnt = sb("inv_cnt", [128, NT, NREL])
        dinv = sb("dinv", [128, NT])
        stats = sb("stats", [128, NT, 2, 6])
        meanvar = sb("meanvar", [128, NT, 2])
        rstd = sb("rstd", [128, NT])
        minus_half = sb("minus_half", [128, NT])
        gates = sb("gates", [128, NT, EXPERTS])
        ones_col = sb("ones_col", [128, 2], F16)
        eye8 = sb("eye8", [128, EXPERTS])
        node_type = sb("node_type", [128, NT], I32)
        type_f = sb("type_f", [128, NT])
        top_val = sb("top_val", [128, NT, 8])
        top_idx = sb("top_idx", [128, NT, 8], U32)
        top_idx_f = sb("top_idx_f", [128, NT, 8])
        logit = sb("logit", [128, NT, EXPERTS])
        soft = sb("soft", [128, NT, EXPERTS])
        share = sb("share", [128, 4, NT])
        recip = sb("recip", [128, 2])
        router32 = sb("router32", [128, KD, EXPERTS])
        router_hi = sb("router_hi", [128, KD, EXPERTS], F16)
        router_lo = sb("router_lo", [128, KD, EXPERTS], F16)
        pidx = sb("pidx", [128, 4])
        tstart_i = sb("tstart_i", [128, NBUCKET + 1], I32)
        wraw = sb("wraw", [128, WMAX])
        whi = sb("whi", [128, 2, WMAX], F16)
        wlo = sb("wlo", [128, 2, WMAX], F16)
        qk_bias = sb("qk_bias", [128, 12])
        b1_cols = sb("b1_cols", [128, EXPERTS * KH])

        edge = ExitStack()
        iota_n = sb("iota_n", [128, N], F16, edge)
        ones16 = sb("ones16", [128, 128], F16, edge)
        e_src = sb("e_src", [128, EJ], I32, edge)
        e_dst = sb("e_dst", [128, EJ], I32, edge)
        e_typ = sb("e_typ", [128, EJ], I32, edge)
        src_tile = sb("src_tile", [128, EJ], F32, edge)
        bucket = sb("bucket", [128, EJ], F32, edge)
        src_loc = sb("src_loc", [128, EJ], F32, edge)
        packed_f = sb("packed_f", [128, EJ], F32, edge)
        packed = sb("packed", [128, EJ], I32, edge)
        mask = sb("mask", [128, NBUCKET, EJ], F16, edge)
        below = sb("below", [128, 4, EJ], F16, edge)
        col_cnt = sb("col_cnt", [128, 3, NBUCKET], F16, edge)
        row_cnt = sb("row_cnt", [128, NBUCKET], F16, edge)
        tiles_f = sb("tiles_f", [128, NBUCKET], F32, edge)
        tiles_i = sb("tiles_i", [128, NBUCKET], I32, edge)
        tstart = sb("tstart", [128, NBUCKET + 1], F32, edge)
        first_slot = sb("first_slot", [128, NBUCKET], F32, edge)
        slot = sb("slot", [128, EJ], F32, edge)
        slot_part = sb("slot_part", [128, 2, EJ], F32, edge)
        slot_i = sb("slot_i", [128, EJ], I32, edge)
        lane_i = sb("lane_i", [128, EJ], I32, edge)
        tile_i = sb("tile_i", [128, EJ], I32, edge)
        lane_f = sb("lane_f", [128, EJ], F32, edge)
        addr_f = sb("addr_f", [128, EJ], F32, edge)
        addr = sb("addr", [128, EJ], U32, edge)
        pad_fill = sb("pad_fill", [128, ETILES], I32, edge)
        sorted_p = sb("sorted_p", [128, ETILES], I32, edge)
        sorted_i = sb("sorted_i", [128, 2, ETILES], I32, edge)
        sorted_f = sb("sorted_f", [128, 2, ETILES], F32, edge)
        oh_dst = sb("oh_dst", [128, RING, N], F16, edge)
        oh_src = sb("oh_src", [128, RING, TP], F16, edge)
        zeros = sb("zeros", [128, 512], F16, edge)
        edge.close()

        hT_hi = sb("hT_hi", [128, 7, N], F16)
        hT_lo = sb("hT_lo", [128, 7, N], F16)
        hT_hi_flat, hT_lo_flat = (t[:, :, :].rearrange("p k n -> p (k n)") for t in (hT_hi, hT_lo))
        acc = sb("acc", [128, NT, 896])
        y = ExitStack()
        y_hi = sb("y_hi", [128, NT, 448], F16, y)
        y_lo = sb("y_lo", [128, NT, 448], F16, y)
        adj_all = sb("adj", [128, NBUCKET * N + 4], F16, y)
        adj = adj_all[:, 0:NBUCKET * N].rearrange("p (b n) -> p b n", n=N)
        y.close()
        e0 = ExitStack()
        stage = sb("stage", [128, 2, D], F32, e0)
        again = sb("again", [128, 2, D], F32, e0)
        ln_w = sb("ln_w", [128, D], F32, e0)
        ln_b = sb("ln_b", [128, D], F32, e0)
        e0.close()
        e1 = ExitStack()
        ht_hi = sb("ht_hi", [128, KH, N], F16, e1)
        ht_lo = sb("ht_lo", [128, KH, N], F16, e1)
        gelu32 = sb("gelu32", [128, 2, 418], F32, e1)
        gate_t = sb("gate_t", [EXPERTS, N], F32, e1)
        b2_rows = sb("b2_rows", [EXPERTS, D], F32, e1)
        e1.close()
        at = ExitStack()
        v_parts = sb("v_parts", [128, NT, HEADS, 129], F16, at)
        qk32 = sb("qk32", [128, 2, 418], F32, at)
        q_a = sb("q_a", [128, 2, N], F16, at)
        k_a = sb("k_a", [128, 2, N], F16, at)
        q_b = sb("q_b", [128, 2, N], F16, at)
        k_b = sb("k_b", [128, 2, N], F16, at)
        p32 = sb("p32", [128, 2, 2 * QC], F32, at)
        p_hi = sb("p_hi", [128, 2, NT, QC + 6], F16, at)
        p_lo = sb("p_lo", [128, 2, NT, QC + 6], F16, at)
        o_pair = sb("o_pair", [128, NT, 128], F32, at)
        ot_hi = sb("ot_hi", [128, N], F16, at)
        ot_lo = sb("ot_lo", [128, N], F16, at)
        row_max = sb("row_max", [128, 2, NT], F32, at)
        at.close()

        ps = ctx.enter_context(nc.psum_tensor("ps", [128, 8, 512], F32))
        x3_dram = nc.dram_tensor("x3_dram", [N, D], F32, kind="Internal").ap()
        edge_dram = nc.dram_tensor("edge_slots", [128 * ETILES, 1], I32, kind="Internal").ap()

        pieces = []

        def piece(src, k, cols, done, value):
            pieces.append((src, k, cols, done, value))
            return len(pieces) - 1

        steps = []
        for L, (K, O, nm) in enumerate(LAYERS):
            Oc = O // 2
            for c in range(2):
                for r in (None, 0, 1, 2):
                    w = a[f"root{nm}"] if r is None else a[f"rel{nm}"][r]
                    v = w.rearrange("(k p) n -> p k n", p=128)[:, :, c * Oc:(c + 1) * Oc]
                    n = sum(1 for s in steps if s[0] == L)
                    steps.append((L, c, r, piece(v, K, Oc, f"y{L}_full", NT * (n + 1))))
        moe_pieces = {}

        def moe_weights(tag, w1, w2):
            got = []
            for x in range(EXPERTS):
                p1 = piece(w1[x].rearrange("(k p) n -> p k n", p=128), KD, HID, f"{tag}_h_full", 9 * (x + 1))
                p2 = piece(w2[x].rearrange("(k p) n -> p k n", p=128), KH, D, f"{tag}_o_full", 2 * NT * (x + 1))
                got.append((p1, p2))
            moe_pieces[tag] = got
        moe_weights("m0", a["wi"], a["wo"])
        gcn_pieces = [piece(a["gcn_w"].rearrange("(k p) n -> p k n", p=128)[:, :, c * 384:(c + 1) * 384],
                            KD, 384, "gy_full", NT * (c + 1)) for c in range(2)]
        v_pieces = [piece(a["w_v"].rearrange("(k p) n -> p k n", p=128)[:, :, c * 384:(c + 1) * 384],
                          KD, 384, "v_full", NT * (c + 1)) for c in range(2)]
        qk_pieces, proj_pieces = [], []
        for j in range(HEADS // 2):
            qk_pieces.append(piece(a["w_qk"][j].rearrange("(k p) n -> p k n", p=128), KD, 256, "qk_full", 6 * (j + 1)))
            proj_pieces.append(piece(a["w_proj"][128 * j:128 * (j + 1), :].rearrange("(k p) n -> p k n", p=128),
                                     1, D, "pr_full", 2 * NT * (j + 1)))
        moe_weights("m1", a["w1"], a["w2"])

        def w_of(g):
            _, k, cols, _, _ = pieces[g]
            v = lambda t: t[:, g % 2, 0:k * cols].rearrange("p (k n) -> p k n", k=k)
            return v(whi), v(wlo)

        def row(reg3, i, lo, hi, parts=TP):
            return reg3[:parts, bass.ds(i, 1), lo:hi].rearrange("p o n -> p (o n)")

        def cols(t2, start, n, parts=128):
            return t2[:parts, bass.ds(start, n)]

        def row_bias(name):
            v = a[name].rearrange("(o d) -> o d", o=1)
            return v.broadcast_to([TP, v.shape[1]])

        p32_flat = p32[:, :, :].rearrange("p a b -> p (a b)")
        block = ctx.enter_context(nc.Block())


        @block.sync
        def _(sp):
            for t, n in ((e_src, "src"), (e_dst, "dst"), (e_typ, "typ")):
                sp.dma_start(t[:EP, :], a[n].rearrange("(p j) -> p j", p=EP)).then_inc(sem("edges_in"), 16)
            for g, (src, k, n, _, _) in enumerate(pieces):
                if g >= 1:
                    sp.wait_ge(sem("w_split"), g)
                sp.dma_start(wraw[:, 0:k * n].rearrange("p (k n) -> p k n", k=k), src).then_inc(sem("w_in"), 16)

        @block.gpsimd
        def _(pool):
            pool.iota(pidx[:, 0:1], [[0, 1]], base=0, channel_multiplier=1,
                      allow_small_or_imprecise_dtypes=True).then_inc(sem("iota_ready"), 1)
            pool.iota(iota_n[:, :], [[1, N]], base=0, channel_multiplier=0,
                      allow_small_or_imprecise_dtypes=True).then_inc(sem("iota_ready"), 1)
            pool.iota(eye8[:, :], [[1, EXPERTS]], base=0, channel_multiplier=0,
                      allow_small_or_imprecise_dtypes=True).then_inc(sem("iota_ready"), 1)
            pool.memset(pad_fill[:, :], PAD_EDGE).then_inc(sem("pad_ready"), 1)
            pool.memset(minus_half[:, :], -0.5).then_inc(sem("half_ready"), 1)
            split = [0]

            def split_to(last):
                while split[0] <= min(last, len(pieces) - 1):
                    g = split[0]
                    _, k, n, _, _ = pieces[g]
                    raw, hi, lo = wraw[:, 0:k * n], whi[:, g % 2, 0:k * n], wlo[:, g % 2, 0:k * n]
                    pool.wait_ge(sem("w_in"), 16 * (g + 1))
                    if g >= 2:
                        pool.wait_ge(sem(pieces[g - 2][3]), pieces[g - 2][4])
                    pool.tensor_copy(hi, raw).then_inc(sem("w_high"), 1)
                    pool.wait_ge(sem("w_high"), g + 1)
                    pool.tensor_tensor(lo, raw, hi, ALU.subtract).then_inc(sem("w_split"), 1)
                    split[0] += 1

            def power(tag, t):
                pool.wait_ge(sem("half_ready"), 1)
                pool.wait_ge(sem(f"{tag}_var"), 1)
                pool.tensor_tensor(t[:TP, :], t[:TP, :], minus_half[:TP, :], ALU.pow).then_inc(sem(f"{tag}_rstd"), 1)

            split_to(1)
            pool.wait_ge(sem("padded"), 16)
            pool.wait_ge(sem("addr_ready"), 1)
            for j in range(EJ):
                pool.indirect_dma_start(edge_dram[:, :], bass.IndirectOffsetOnAxis(ap=addr[:EP, j:j + 1], axis=0),
                                        packed[:EP, j:j + 1], None).then_inc(sem("scattered"), 16)
            power("deg", dinv)
            power("n0", rstd)
            split_to(moe_pieces["m0"][0][1])
            power("n1", rstd)
            split_to(gcn_pieces[1])
            power("n2", rstd)
            split_to(v_pieces[1])
            power("n3", rstd)
            power("n4", rstd)
            split_to(proj_pieces[0])
            for j in range(HEADS // 2):
                split_to(qk_pieces[j + 1] if j < 5 else moe_pieces["m1"][0][0])
                if j < 5:
                    split_to(proj_pieces[j + 1])
            split_to(moe_pieces["m1"][0][1])
            power("n5", rstd)
            split_to(len(pieces))

        @block.scalar
        def _(act):
            act.dma_start(qk_bias[:, :], a["qk_b"]).then_inc(sem("consts_in"), 16)
            act.dma_start(b1_cols[:, :], a["b1x"]).then_inc(sem("consts_in"), 16)
            act.dma_start(node_type[:TP, :], a["node_type"]).then_inc(sem("consts_in"), 16)
            act.dma_start(router32[:, :, :], a["router"].rearrange("(k p) n -> p k n", p=128)).then_inc(sem("consts_in"), 16)
            act.wait_ge(sem("pad_ready"), 1)
            act.dma_start(edge_dram.rearrange("(p t) o -> p (t o)", p=128), pad_fill[:, :]).then_inc(sem("padded"), 16)
            act.wait_ge(sem("scattered"), 16 * EJ)
            act.dma_start(sorted_p[:, :], edge_dram.rearrange("(p t) o -> p (t o)", p=128)).then_inc(sem("sorted_in"), 16)
            act.nop().then_inc(sem("adj_free"), 2)
            with act.Fori(0, NBUCKET // 2) as bh:
                for u in range(2):
                    act.wait_ge(sem("adj_full"), 2 * bh + u + 1)
                    act.activation(row(adj, 2 * bh + u, 0, N), ps[:TP, 3 * u:3 * u + 3, :].rearrange("p a b -> p (a b)")[:, :N],
                                   ACT.Copy).then_inc(sem("adj_free"), 1)
            act.wait_ge(sem("adj_full"), NBUCKET)
            act.dma_start(acc[:TP, :, 0:D], a["x"].rearrange("(t p) d -> p t d", p=TP)).then_inc(sem("x_in"), 16)
            for t in range(3):
                act.dma_start(bias_b[:TP, 128 * t:128 * (t + 1)], a["emb"][t:t + 1, :].broadcast_to([TP, 128])
                              ).then_inc(sem("x_in"), 16)

            def transposed(tag, K, func):
                job = 0
                for m in range(NT):
                    for k0, k1 in ((0, 4), (4, K)):
                        act.wait_ge(sem(f"{tag}_t_full"), job + 1)
                        act.activation(hT_hi[:, k0:k1, m * TP:(m + 1) * TP],
                                       ps[:, 4 + job % 4, 0:(k1 - k0) * TP].rearrange("p (k n) -> p k n", n=TP),
                                       func).then_inc(sem(f"{tag}_t_high"), 1)
                        job += 1

            def relational(L):
                K, O, nm = LAYERS[L]
                Oc = O // 2
                yj = 0
                for n, (_, c, r, g) in enumerate(s for s in steps if s[0] == L):
                    if r is not None:
                        done = NT * (3 * c + r)
                        if done:
                            act.wait_ge(sem(f"z{L}_full"), done)
                        with act.Fori(0, NT // 2) as i:
                            for u in range(2):
                                act.wait_ge(sem(f"y{L}_full"), NT * n + 2 * i + u + 1)
                                act.activation(row(y_hi, 2 * i + u, 0, Oc), ps[:TP, u, 0:Oc], ACT.Copy
                                               ).then_inc(sem(f"y{L}_high"), 1)

            act.wait_ge(sem("h0_ready"), 1)
            act.dma_start(bias_b[:TP, 0:896], row_bias("b1")).then_inc(sem("bias_in"), 16)
            transposed("t0", 7, ACT.Copy)
            relational(0)
            for L in (1, 2):
                act.wait_ge(sem(f"z{L - 1}_free"), 2 + 6 * NT)
                act.wait_ge(sem(f"y{L - 1}_free"), 2 + 8 * NT)
                act.dma_start(bias_b[:TP, 0:D], row_bias(f"b{L + 1}")).then_inc(sem("bias_in"), 16)
                transposed(f"t{L}", LAYERS[L][0], ACT.Relu)
                relational(L)

            def read_again(tag, src):
                for m in range(NT):
                    if m >= 2:
                        act.wait_ge(sem(f"{tag}_sum"), m - 1)
                    act.dma_start(again[:TP, m % 2, :], src[m * TP:(m + 1) * TP, :]).then_inc(sem(f"{tag}_in{m % 2}"), 16)

            act.wait_ge(sem("z2_free"), 2 + 6 * NT)
            read_again("res", a["x"])

            def hidden(tag, x):
                if x:
                    act.wait_ge(sem(f"{tag}_o_full"), 2 * NT * x)
                for job in range(9):
                    hc, (c0, w) = job // 3, NODE_COLS[job % 3]
                    n = 9 * x + job
                    act.wait_ge(sem(f"{tag}_h_full"), n + 1)
                    p = ps[:, job % 2, 0:w]
                    if tag == "m0":
                        act.activation(ht_hi[:, hc, c0:c0 + w], p, ACT.Relu).then_inc(sem("m0_h_high"), 1)
                    else:
                        b = b1_cols[:, x * KH + hc:x * KH + hc + 1]
                        if n >= 2:
                            act.wait_ge(sem("m1_h_low"), n - 1)
                        act.activation(gelu32[:, n % 2, 0:w], p, ACT.Gelu, bias=b)
                        act.activation(ht_hi[:, hc, c0:c0 + w], p, ACT.Gelu, bias=b).then_inc(sem("m1_h_high"), 1)

            transposed("n1", KD, ACT.Copy)
            act.wait_ge(sem("m0_soft_in"), 1)
            act.activation(soft[:TP, :, :], logit[:TP, :, :], ACT.Exp).then_inc(sem("m0_exp"), 1)
            for x in range(EXPERTS):
                hidden("m0", x)
            transposed("n2", KD, ACT.Copy)
            act.wait_ge(sem("n2_t_high"), 2 * NT)
            act.dma_start(bias_b[:TP, 0:D], row_bias("gcn_b")).then_inc(sem("bias_in"), 16)
            for c in range(2):
                if c:
                    act.wait_ge(sem("gz_full"), NT)
                with act.Fori(0, NT // 2) as i:
                    for u in range(2):
                        m = 2 * i + u
                        act.wait_ge(sem("gy_full"), NT * c + m + 1)
                        act.activation(row(y_hi, m, 0, 384), ps[:TP, u, 0:384], ACT.Copy,
                                       scale=dinv[:TP, bass.ds(m, 1)]).then_inc(sem("gy_high"), 1)
            act.wait_ge(sem("gz_free"), 2 + 2 * NT)
            act.dma_start(x3_dram.rearrange("(t p) d -> p t d", p=TP), acc[:TP, :, 0:D]).then_inc(sem("x3_out"), 16)
            act.dma_start(bias_b[:TP, 0:D], row_bias("v_b")).then_inc(sem("bias_in"), 16)
            act.dma_start(ln_w[:TP, :], row_bias("n1_w")).then_inc(sem("affine_in"), 16)
            act.dma_start(ln_b[:TP, :], row_bias("n1_b")).then_inc(sem("affine_in"), 16)
            transposed("n4", KD, ACT.Copy)
            for c in range(2):
                with act.Fori(0, NT // 2) as i:
                    for u in range(2):
                        m = 2 * i + u
                        act.wait_ge(sem("v_biased"), NT * c + m + 1)
                        act.activation(v_parts[:TP, bass.ds(m, 1), 6 * c:6 * c + 6, 0:HD].rearrange("p o h d -> p (o h) d"),
                                       p32_flat[:TP, 384 * u:384 * (u + 1)].rearrange("p (h d) -> p h d", d=HD),
                                       ACT.Copy).then_inc(sem("v_high"), 1)
            job = 0
            act.nop().then_inc(sem("exp_done"), 5)
            for j in range(HEADS // 2):
                for which in range(2):
                    for c0, w in NODE_COLS:
                        job += 1
                        act.wait_ge(sem("qk_full"), job)
                        if job > 1:
                            act.wait_ge(sem("qk_parts"), job - 1)
                        for hh in range(2):
                            P0 = slice(64 * hh, 64 * hh + 64)
                            p, b = ps[P0, (job - 1) % 2, 0:w], qk_bias[P0, 6 * which + j:6 * which + j + 1]
                            act.activation((q_a, k_a)[which][0:64, hh, c0:c0 + w], p, ACT.Identity, bias=b)
                            act.activation(qk32[0:64, hh, 0:w], p, ACT.Identity, bias=b).then_inc(sem("qk_moved"), 1)
                for h2 in range(2):
                    act.wait_ge(sem("max_rows"), 2 * j + h2 + 1)
                    act.activation(q_b[64:65, h2, 0:1000].rearrange("p (a b) -> p a b", b=500),
                                   ps[64:65, 3 * h2:3 * h2 + 2, 0:500], ACT.Copy, scale=-1.0)
                    act.activation(q_b[64:65, h2, 1000:N], ps[64:65, 3 * h2 + 2, 0:250], ACT.Copy,
                                   scale=-1.0).then_inc(sem("max_set"), 1)
                with act.Fori(0, NT // 2) as qc:
                    for h2 in range(2):
                        n = 10 * j + 2 * qc + h2
                        act.wait_ge(sem("pv_full"), 2 * n + 2)
                        for kp in range(5):
                            p = ps[:TP, kp, 0:2 * QC]
                            act.wait_ge(sem("s_full"), 5 * n + kp + 1)
                            act.activation(p_hi[:TP, h2, 2 * kp:2 * kp + 2, 0:QC], p.rearrange("p (a b) -> p a b", b=QC),
                                           ACT.Exp, scale=HD ** -0.5).then_inc(sem("p_high"), 1)
                            act.wait_ge(sem("p_low"), 5 * n + kp + 1)
                            act.activation(p32[:TP, (5 * h2 + kp) % 2, :], p,
                                           ACT.Exp, scale=HD ** -0.5).then_inc(sem("exp_done"), 1)
                for t, (c0, w) in enumerate(((0, 500), (500, 500), (1000, 250))):
                    act.wait_ge(sem("ot_full"), 3 * j + t + 1)
                    if j:
                        act.wait_ge(sem("pr_full"), 2 * NT * j)
                    act.activation(ot_hi[:, c0:c0 + w], ps[:, t, 0:w], ACT.Copy).then_inc(sem("ot_high"), 1)
            act.wait_ge(sem("pr_free"), 4 + 2 * NT * 6)
            act.dma_start(bias_b[:TP, 0:D], row_bias("proj_b")).then_inc(sem("bias_in"), 16)
            act.dma_start(ln_w[:TP, :], row_bias("n2_w")).then_inc(sem("affine_in"), 16)
            act.dma_start(ln_b[:TP, :], row_bias("n2_b")).then_inc(sem("affine_in"), 16)
            act.dma_start(router32[:, :, :], a["w_gate"].rearrange("(k p) n -> p k n", p=128)).then_inc(sem("gate_in"), 16)
            transposed("n5", KD, ACT.Copy)
            act.wait_ge(sem("m1_soft_in"), 1)
            act.activation(share[:TP, 1, :], share[:TP, 0, :], ACT.Exp).then_inc(sem("m1_exp"), 1)
            act.dma_start(b2_rows[:, :], a["b2x"]).then_inc(sem("b2_in"), 16)
            for q in range(3):
                act.wait_ge(sem("gt_full"), q + 1)
                w = 500 if q < 2 else 250
                act.activation(gate_t[:, 500 * q:500 * q + w], ps[0:EXPERTS, 4 + q, 0:w], ACT.Copy).then_inc(sem("gt_done"), 1)
            for x in range(EXPERTS):
                hidden("m1", x)
            act.wait_ge(sem("m1_o_full"), 2 * NT * EXPERTS)
            read_again("last", x3_dram)
            act.wait_ge(sem("last_sum"), NT)
            act.dma_start(out.rearrange("(t p) d -> p t d", p=TP), acc[:TP, :, 0:D]).then_inc(sem("stored"), 16)
            act.wait_ge(sem("stored"), 16)

        @block.vector
        def _(dve):
            count = [0]

            def then(ins):
                count[0] += 1
                ins.then_inc(sem("dve_step"), 1)
                dve.wait_ge(sem("dve_step"), count[0])

            def signal(ins, name, value):
                ins.then_inc(sem(name), 1)
                dve.wait_ge(sem(name), value)

            def bcast(col, n):
                return col.to_broadcast([TP, NT, n])

            dve.memset(zeros[:, :], 0.0)
            dve.memset(ones16[:, :], 1.0)
            dve.memset(slot[:EP, :], 0.0)
            dve.wait_ge(sem("iota_ready"), 3)
            for c in range(1, 3):
                dve.tensor_scalar(pidx[:, c:c + 1], pidx[:, 0:1], float(128 * c), None, ALU.add)
            then(dve.tensor_scalar(ident[:, :], iota_n[:, :128], pidx[:, 0:1], None, ALU.is_equal))
            dve.tensor_scalar(below[:, 0, :128], iota_n[:, :128], pidx[:, 0:1], None, ALU.is_gt)
            for c in range(3):
                dve.tensor_scalar(below[:, 1 + c, :], iota_n[:, :EJ], pidx[:, c:c + 1], None, ALU.is_gt)
            dve.wait_ge(sem("edges_in"), 48)
            then(dve.tensor_scalar(src_tile[:EP, :], e_src[:EP, :], float(TP), None, ALU.is_ge))
            for k in range(2, NT):
                then(dve.scalar_tensor_tensor(src_tile[:EP, :], e_src[:EP, :], float(TP * k), src_tile[:EP, :],
                                              ALU.is_ge, ALU.add))
            dve.scalar_tensor_tensor(bucket[:EP, :], e_typ[:EP, :], float(NT), src_tile[:EP, :], ALU.mult, ALU.add)
            then(dve.scalar_tensor_tensor(src_loc[:EP, :], src_tile[:EP, :], float(-TP), e_src[:EP, :], ALU.mult, ALU.add))
            then(dve.scalar_tensor_tensor(packed_f[:EP, :], e_dst[:EP, :], 128.0, src_loc[:EP, :], ALU.mult, ALU.add))
            dve.tensor_copy(packed[:EP, :], packed_f[:EP, :])
            for b in range(NBUCKET):
                ins = dve.tensor_scalar(mask[:EP, b, :], bucket[:EP, :], float(b), None, ALU.is_equal)
            then(ins)
            then(dve.tensor_reduce(tiles_f[:EP, :], mask[:EP, :, :], AX_X, ALU.add))
            signal(dve.tensor_copy(row_cnt[:EP, :], tiles_f[:EP, :]), "row_counts", 1)
            dve.wait_ge(sem("col_counts"), 1)
            dve.tensor_copy(col_cnt[:, :2, :], ps[:, 0, 0:2 * NBUCKET].rearrange("p (c b) -> p c b", c=2))
            dve.tensor_copy(col_cnt[:64, 2, :], ps[:64, 0, 2 * NBUCKET:3 * NBUCKET])
            signal(dve.tensor_scalar(tiles_f[:, :], ps[:, 1, 0:NBUCKET], 128.0 * UNIT - 1, None, ALU.add), "col_counts_in", 1)
            then(dve.tensor_copy(tiles_i[:, :], tiles_f[:, :]))
            then(dve.tensor_scalar(tiles_i[:, :], tiles_i[:, :], 8, None, ALU.arith_shift_right))
            dve.tensor_scalar(tiles_f[:, :], tiles_i[:, :], 1.0, None, ALU.max)
            then(dve.memset(tstart[:, 0:1], 0.0))
            for b in range(NBUCKET):
                then(dve.tensor_tensor(tstart[:, b + 1:b + 2], tstart[:, b:b + 1], tiles_f[:, b:b + 1], ALU.add))
            dve.tensor_copy(tstart_i[:, :], tstart[:, :]).then_inc(sem("starts_ready"), 1)
            then(dve.tensor_scalar(first_slot[:, :], tstart[:, :NBUCKET], 128.0 * UNIT, None, ALU.mult))
            for b in range(NBUCKET):
                dve.wait_ge(sem("ranks"), b + 1)
                then(dve.scalar_tensor_tensor(slot_part[:EP, b % 2, :], ps[:EP, 2 + b % 4, :EJ], first_slot[:EP, b:b + 1],
                                              mask[:EP, b, :], ALU.add, ALU.mult))
                signal(dve.tensor_tensor(slot[:EP, :], slot[:EP, :], slot_part[:EP, b % 2, :], ALU.add), "rank_used", b + 1)
            then(dve.tensor_copy(slot_i[:EP, :], slot[:EP, :]))
            dve.tensor_scalar(tile_i[:EP, :], slot_i[:EP, :], 7, None, ALU.arith_shift_right)
            then(dve.tensor_scalar(lane_i[:EP, :], slot_i[:EP, :], 127, None, ALU.bitwise_and))
            then(dve.tensor_scalar(lane_f[:EP, :], lane_i[:EP, :], float(ETILES), None, ALU.mult))
            then(dve.tensor_tensor(addr_f[:EP, :], lane_f[:EP, :], tile_i[:EP, :], ALU.add))
            dve.tensor_copy(addr[:EP, :], addr_f[:EP, :]).then_inc(sem("addr_ready"), 1)
            dve.wait_ge(sem("sorted_in"), 16)
            dve.tensor_scalar(sorted_i[:, 0, :], sorted_p[:, :], 7, None, ALU.arith_shift_right)
            then(dve.tensor_scalar(sorted_i[:, 1, :], sorted_p[:, :], 127, None, ALU.bitwise_and))
            then(dve.tensor_copy(sorted_f[:, :, :], sorted_i[:, :, :]))
            with dve.Fori(0, NBUCKET) as b:
                lo = dve.value_load(tstart_i[0:1, bass.ds(b, 1)], min_val=0, max_val=UNITS - 1)
                hi = dve.value_load(tstart_i[0:1, bass.ds(b + 1, 1)], min_val=1, max_val=UNITS)
                with dve.Fori(lo, hi) as t:
                    ring = UNIT * (t % (RING // UNIT))
                    for u in range(UNIT):
                        dve.wait_ge(sem("onehot_free"), UNIT * t + u + 1)
                        dve.tensor_scalar(row(oh_src, ring + u, 0, TP, 128), iota_n[:, :TP],
                                          sorted_f[:, 1, bass.ds(UNIT * t + u, 1)], None, ALU.is_equal)
                        dve.tensor_scalar(row(oh_dst, ring + u, 0, N, 128), iota_n[:, :],
                                          sorted_f[:, 0, bass.ds(UNIT * t + u, 1)], None, ALU.is_equal
                                          ).then_inc(sem("onehot_ready"), 1)

            dve.wait_ge(sem("adj_full"), NBUCKET)
            dve.memset(adj_all[:, NBUCKET * N:], 0.0)
            then(dve.memset(ones_col[:, :], 1.0))
            dve.nop().then_inc(sem("ones_ready"), 1)
            dve.wait_ge(sem("counts"), 1)
            cnt = ps[:TP, 7, 0:NBUCKET].rearrange("p (m r) -> p m r", r=NREL)
            then(dve.tensor_scalar(inv_cnt[:TP, :, :], cnt, 1.0, None, ALU.max))
            then(dve.reciprocal(inv_cnt[:TP, :, :], inv_cnt[:TP, :, :]))
            then(dve.scalar_tensor_tensor(inv_cnt[:TP, :, :], cnt, 1.0, inv_cnt[:TP, :, :], ALU.min, ALU.mult))
            then(dve.tensor_reduce(dinv[:TP, :], cnt, AX_X, ALU.add))
            dve.tensor_scalar(dinv[:TP, :], dinv[:TP, :], 1.0, None, ALU.add).then_inc(sem("deg_var"), 1)

            def normalize_stats(tag):
                for m in range(NT):
                    for h in range(2):
                        ins = dve.bn_stats(stats[:TP, m, h, :], acc[:TP, m, 384 * h:384 * (h + 1)])
                then(ins)
                for m in range(NT):
                    ins = dve.bn_aggr(meanvar[:TP, m, :], stats[:TP, m, :, :])
                then(ins)
                dve.tensor_scalar(rstd[:TP, :], meanvar[:TP, :, 1:2].rearrange("p m o -> p (m o)"), 1e-5, None, ALU.add
                                  ).then_inc(sem(f"{tag}_var"), 1)
                dve.wait_ge(sem(f"{tag}_rstd"), 1)

            def normalized(dst, m):
                return dve.tensor_scalar(dst, acc[:TP, m, 0:D], meanvar[:TP, m, 0:1], rstd[:TP, m:m + 1],
                                         ALU.subtract, ALU.mult)

            def low_parts(tag, m, K, relu):
                for q, (k0, k1) in enumerate(((0, 4), (4, K))):
                    job = 2 * m + q
                    dve.wait_ge(sem(f"{tag}_t_high"), job + 1)
                    p = ps[:, 4 + job % 4, 0:(k1 - k0) * TP].rearrange("p (k n) -> p k n", n=TP)
                    hi = hT_hi[:, k0:k1, m * TP:(m + 1) * TP]
                    lo = hT_lo[:, k0:k1, m * TP:(m + 1) * TP]
                    if relu:
                        ins = dve.scalar_tensor_tensor(lo, p, 0.0, hi, ALU.max, ALU.subtract)
                    else:
                        ins = dve.tensor_tensor(lo, p, hi, ALU.subtract)
                    ins.then_inc(sem(f"{tag}_t_free"), 1)

            def normalized_transposed(tag, affine=False):
                normalize_stats(tag)
                if affine:
                    dve.wait_ge(sem("affine_in"), 32 if tag == "n4" else 64)
                for m in range(NT + 1):
                    if m < NT:
                        if m >= 2:
                            dve.wait_ge(sem(f"{tag}_t_full"), 2 * (m - 1))
                        s = stage[:TP, m % 2, :]
                        ins = normalized(s, m)
                        if affine:
                            then(ins)
                            then(dve.tensor_tensor(s, s, ln_w[:TP, :], ALU.mult))
                            ins = dve.tensor_tensor(s, s, ln_b[:TP, :], ALU.add)
                        ins.then_inc(sem(f"{tag}_staged"), 1)
                    if m:
                        low_parts(tag, m - 1, KD, False)

            dve.wait_ge(sem("x_in"), 64)
            dve.wait_ge(sem("consts_in"), 64)
            normalize_stats("n0")
            for m in range(NT):
                normalized(acc[:TP, m, 0:D], m)
            then(dve.tensor_copy(type_f[:TP, :], node_type[:TP, :]))
            for t in range(3):
                then(dve.tensor_scalar(share[:TP, t, :], type_f[:TP, :], float(t), None, ALU.is_equal))
            for m in range(NT):
                e = acc[:TP, m, D:896]
                then(dve.tensor_scalar(e, bias_b[:TP, 0:128], share[:TP, 0, m:m + 1], None, ALU.mult))
                for t in (1, 2):
                    then(dve.scalar_tensor_tensor(e, bias_b[:TP, 128 * t:128 * (t + 1)], share[:TP, t, m:m + 1], e,
                                                  ALU.mult, ALU.add))
            dve.nop().then_inc(sem("h0_ready"), 1)
            for m in range(NT):
                low_parts("t0", m, 7, False)

            def relational(L):
                K, O, nm = LAYERS[L]
                Oc = O // 2
                dve.nop().then_inc(sem(f"y{L}_free"), 2)
                dve.nop().then_inc(sem(f"z{L}_free"), 2)
                dve.wait_ge(sem("bias_in"), 16 * (L + 1))
                for n, (_, c, r, g) in enumerate(s for s in steps if s[0] == L):
                    c0, c1 = c * Oc, (c + 1) * Oc
                    with dve.Fori(0, NT // 2) as i:
                        for u in range(2):
                            m = 2 * i + u
                            if r is None:
                                dve.wait_ge(sem(f"y{L}_full"), NT * n + m + 1)
                                dve.tensor_tensor(row(acc, m, c0, c1), ps[:TP, u, 0:Oc], bias_b[:TP, c0:c1], ALU.add
                                                  ).then_inc(sem(f"y{L}_free"), 1)
                            else:
                                dve.wait_ge(sem(f"y{L}_high"), NT * (3 * c + r) + m + 1)
                                dve.tensor_tensor(row(y_lo, m, 0, Oc), ps[:TP, u, 0:Oc], row(y_hi, m, 0, Oc), ALU.subtract
                                                  ).then_inc(sem(f"y{L}_free"), 1)
                    if r is not None:
                        z = 3 * c + r
                        dve.wait_ge(sem(f"y{L}_free"), 2 + NT * (n + 1))
                        dve.wait_ge(sem(f"z{L}_free"), 2 + NT * z)
                        with dve.Fori(0, NT // 2) as i:
                            for u in range(2):
                                m = 2 * i + u
                                dve.wait_ge(sem(f"z{L}_full"), NT * z + m + 1)
                                dve.scalar_tensor_tensor(row(acc, m, c0, c1), ps[:TP, 2 + u, 0:Oc],
                                                         row(inv_cnt, m, r, r + 1), row(acc, m, c0, c1),
                                                         ALU.mult, ALU.add).then_inc(sem(f"z{L}_free"), 1)
                dve.wait_ge(sem(f"z{L}_free"), 2 + 6 * NT)

            relational(0)
            for L in (1, 2):
                for m in range(NT):
                    low_parts(f"t{L}", m, LAYERS[L][0], True)
                relational(L)
            for m in range(NT):
                dve.wait_ge(sem(f"res_in{m % 2}"), 16 * (m // 2 + 1))
                dve.scalar_tensor_tensor(acc[:TP, m, 0:D], acc[:TP, m, 0:D], 0.0, again[:TP, m % 2, :], ALU.max, ALU.add
                                         ).then_inc(sem("res_sum"), 1)
            dve.wait_ge(sem("res_sum"), NT)

            def logits_in(tag):
                dve.wait_ge(sem(f"{tag}_logits"), NT)
                then(dve.tensor_copy(logit[:TP, :, :], ps[:TP, 3, 0:NT * EXPERTS].rearrange("p (m e) -> p m e", e=EXPERTS)))
                for m in range(NT):
                    ins = dve.max(top_val[:TP, m, :], logit[:TP, m, :])
                then(ins)
                for m in range(NT):
                    ins = dve.max_index(top_idx[:TP, m, :], top_val[:TP, m, :], logit[:TP, m, :])
                then(ins)
                then(dve.tensor_copy(top_idx_f[:TP, :, :], top_idx[:TP, :, :]))

            def router_parts(tag, name, value):
                dve.wait_ge(sem(name), value)
                then(dve.tensor_copy(router_hi[:, :, :], router32[:, :, :]))
                dve.tensor_tensor(router_lo[:, :, :], router32[:, :, :], router_hi[:, :, :], ALU.subtract
                                  ).then_inc(sem(f"{tag}_router"), 1)

            def experts(tag):
                dve.nop().then_inc(sem(f"{tag}_o_free"), 2)
                for x in range(EXPERTS):
                    for job in range(9):
                        hc, (c0, w) = job // 3, NODE_COLS[job % 3]
                        n = 9 * x + job
                        dve.wait_ge(sem(f"{tag}_h_high"), n + 1)
                        hi, lo = ht_hi[:, hc, c0:c0 + w], ht_lo[:, hc, c0:c0 + w]
                        if tag == "m0":
                            ins = dve.scalar_tensor_tensor(lo, ps[:, job % 2, 0:w], 0.0, hi, ALU.max, ALU.subtract)
                        else:
                            ins = dve.tensor_tensor(lo, gelu32[:, n % 2, 0:w], hi, ALU.subtract)
                        ins.then_inc(sem(f"{tag}_h_low"), 1)
                    if x:
                        dve.wait_ge(sem(f"{tag}_o_free"), 2 + NT * x)
                    with dve.Fori(0, NT // 2) as i:
                        for u in range(2):
                            m = 2 * i + u
                            for c in range(2):
                                dve.wait_ge(sem(f"{tag}_o_full"), 2 * NT * x + 2 * m + c + 1)
                                av = row(acc, m, 384 * c, 384 * (c + 1))
                                ins = dve.scalar_tensor_tensor(av, ps[:TP, 2 + 2 * u + c, 0:384], row(gates, m, x, x + 1), av,
                                                               ALU.mult, ALU.add)
                            ins.then_inc(sem(f"{tag}_o_free"), 1)
                dve.wait_ge(sem(f"{tag}_o_free"), 2 + NT * EXPERTS)

            normalized_transposed("n1")
            router_parts("m0", "consts_in", 64)
            logits_in("m0")
            dve.tensor_tensor(logit[:TP, :, :], logit[:TP, :, :], top_val[:TP, :, 0:1].to_broadcast([TP, NT, EXPERTS]),
                              ALU.subtract).then_inc(sem("m0_soft_in"), 1)
            dve.wait_ge(sem("m0_exp"), 1)
            then(dve.tensor_reduce(share[:TP, 0, :], soft[:TP, :, :], AX_X, ALU.add))
            then(dve.reciprocal(share[:TP, 0, :], share[:TP, 0, :]))
            for m in range(NT):
                ins = dve.tensor_scalar(gates[:TP, m, :], eye8[:TP, :], top_idx_f[:TP, m, 0:1], share[:TP, 0, m:m + 1],
                                        ALU.is_equal, ALU.mult)
            then(ins)
            experts("m0")

            for s in range(NT):
                then(dve.tensor_tensor(adj[:TP, s, :], adj[:TP, s, :], adj[:TP, NT + s, :], ALU.add))
                then(dve.tensor_tensor(adj[:TP, s, :], adj[:TP, s, :], adj[:TP, 2 * NT + s, :], ALU.add))
                dg = adj[:TP, s, s * TP:(s + 1) * TP]
                ins = dve.tensor_tensor(dg, dg, ident[:TP, :TP], ALU.add)
            ins.then_inc(sem("adj_sum"), 1)
            normalized_transposed("n2")
            dve.wait_ge(sem("bias_in"), 16 * 4)
            for m in range(NT):
                ins = dve.tensor_tensor(acc[:TP, m, 0:D], acc[:TP, m, 0:D], bias_b[:TP, 0:D], ALU.add)
            then(ins)
            dve.nop().then_inc(sem("gy_free"), 2)
            dve.nop().then_inc(sem("gz_free"), 2)
            for c in range(2):
                c0, c1 = 384 * c, 384 * (c + 1)
                with dve.Fori(0, NT // 2) as i:
                    for u in range(2):
                        m = 2 * i + u
                        dve.wait_ge(sem("gy_high"), NT * c + m + 1)
                        dve.scalar_tensor_tensor(row(y_lo, m, 0, 384), ps[:TP, u, 0:384], dinv[:TP, bass.ds(m, 1)],
                                                 row(y_hi, m, 0, 384), ALU.mult, ALU.subtract).then_inc(sem("gy_free"), 1)
                with dve.Fori(0, NT // 2) as i:
                    for u in range(2):
                        m = 2 * i + u
                        dve.wait_ge(sem("gz_full"), NT * c + m + 1)
                        dve.scalar_tensor_tensor(row(acc, m, c0, c1), ps[:TP, 2 + u, 0:384], dinv[:TP, bass.ds(m, 1)],
                                                 row(acc, m, c0, c1), ALU.mult, ALU.add).then_inc(sem("gz_free"), 1)
            dve.wait_ge(sem("gz_free"), 2 + 2 * NT)

            normalize_stats("n3")
            dve.wait_ge(sem("x3_out"), 16)
            for m in range(NT):
                ins = normalized(acc[:TP, m, 0:D], m)
            then(ins)
            normalized_transposed("n4", affine=True)
            dve.wait_ge(sem("n4_t_full"), 2 * NT)
            dve.memset(v_parts[:TP, :, :, HD:HD + 1], 1.0)
            for t in (p_hi, p_lo):
                dve.memset(t[:TP, :, :, QC:QC + 6], 0.0)
            dve.memset(q_b[64:96, :, :], 0.0)
            then(dve.memset(k_b[64:96, :, :], 0.0))
            signal(dve.memset(k_b[64:65, :, :], 1.0), "ones_set", 1)
            dve.wait_ge(sem("bias_in"), 16 * 5)
            dve.nop().then_inc(sem("v_low"), 2)
            dve.nop().then_inc(sem("p_low"), 2)
            dve.nop().then_inc(sem("o_free"), 2)
            dve.nop().then_inc(sem("pr_free"), 4)
            dve.nop().then_inc(sem("max_free"), 2)
            for c in range(2):
                with dve.Fori(0, NT // 2) as i:
                    for u in range(2):
                        m = 2 * i + u
                        dve.wait_ge(sem("v_full"), NT * c + m + 1)
                        v32 = p32_flat[:TP, 384 * u:384 * (u + 1)]
                        dve.wait_ge(sem("v_low"), NT * c + m + 1)
                        dve.tensor_tensor(v32, ps[:TP, u, 0:384], bias_b[:TP, 384 * c:384 * (c + 1)], ALU.add
                                          ).then_inc(sem("v_biased"), 1)
                        dve.wait_ge(sem("v_high"), NT * c + m + 1)
                        vp = lambda lo, hi: v_parts[:TP, bass.ds(m, 1), 6 * c:6 * c + 6, lo:hi].rearrange("p o h d -> p (o h) d")
                        dve.tensor_tensor(vp(HD + 1, 129), v32.rearrange("p (h d) -> p h d", d=HD), vp(0, HD), ALU.subtract
                                          ).then_inc(sem("v_low"), 1)
            job = 0
            for j in range(HEADS // 2):
                for which in range(2):
                    for c0, w in NODE_COLS:
                        job += 1
                        dve.wait_ge(sem("qk_moved"), 2 * job)
                        hi = (q_a, k_a)[which]
                        lo = q_b[0:64, :, c0:c0 + w] if which == 0 else k_a[64:128, :, c0:c0 + w]
                        dup = q_a[64:128, :, c0:c0 + w] if which == 0 else k_b[0:64, :, c0:c0 + w]
                        dve.tensor_copy(dup, hi[0:64, :, c0:c0 + w])
                        dve.tensor_tensor(lo, qk32[0:64, :, 0:w], hi[0:64, :, c0:c0 + w], ALU.subtract
                                          ).then_inc(sem("qk_parts"), 1)
                for h2 in range(2):
                    with dve.Fori(0, NT // 2) as i:
                        for u in range(2):
                            t = 2 * i + u
                            dve.wait_ge(sem("max_full"), (2 * j + h2) * NT + t + 1)
                            dve.reduce_max(row_max[:TP, h2, bass.ds(t, 1)],
                                           ps[:TP, 3 * u:3 * u + 3, :].rearrange("p a b -> p (a b)")[:, :N], AX_X
                                           ).then_inc(sem("max_free"), 1)
                def p_low_parts(qc, h2):
                    n = 10 * j + 2 * qc + h2
                    for kp in range(5):
                        dve.wait_ge(sem("exp_done"), 5 * n + kp + 6)
                        dve.tensor_tensor(p_lo[:TP, h2, 2 * kp:2 * kp + 2, 0:QC],
                                          p32[:TP, (5 * h2 + kp) % 2, :].rearrange("p (a b) -> p a b", b=QC),
                                          p_hi[:TP, h2, 2 * kp:2 * kp + 2, 0:QC],
                                          ALU.subtract).then_inc(sem("p_low"), 1)

                def o_out(qc, h2):
                    n = 10 * j + 2 * qc + h2
                    for u in range(2):
                        dve.wait_ge(sem("pv_full"), 2 * n + u + 5)
                        dve.reciprocal(recip[:TP, u:u + 1], ps[:TP, 5 + u, HD:HD + 1]).then_inc(sem("o_recip"), 1)
                        dve.wait_ge(sem("o_recip"), 2 * n + u + 1)
                        dve.tensor_scalar(row(o_pair, 2 * qc + u, 64 * h2, 64 * h2 + 64), ps[:TP, 5 + u, 0:HD],
                                          recip[:TP, u:u + 1], None, ALU.mult).then_inc(sem("o_free"), 1)

                p_low_parts(0, 0)
                with dve.Fori(0, NT // 2 - 1) as qc:
                    p_low_parts(qc, 1)
                    o_out(qc, 0)
                    p_low_parts(qc + 1, 0)
                    o_out(qc, 1)
                p_low_parts(NT // 2 - 1, 1)
                o_out(NT // 2 - 1, 0)
                o_out(NT // 2 - 1, 1)
                for t, (c0, w) in enumerate(((0, 500), (500, 500), (1000, 250))):
                    dve.wait_ge(sem("ot_high"), 3 * j + t + 1)
                    dve.tensor_tensor(ot_lo[:, c0:c0 + w], ps[:, t, 0:w], ot_hi[:, c0:c0 + w], ALU.subtract
                                      ).then_inc(sem("ot_low"), 1)
                if j:
                    dve.wait_ge(sem("pr_free"), 4 + 2 * NT * j)
                with dve.Fori(0, NT // 2) as i:
                    for u in range(2):
                        m = 2 * i + u
                        for c in range(2):
                            q = 2 * NT * j + 2 * m + c
                            dve.wait_ge(sem("pr_full"), q + 1)
                            av = row(acc, m, 384 * c, 384 * (c + 1))
                            dve.tensor_tensor(av, ps[:TP, 3 + 2 * u + c, 0:384], av, ALU.add).then_inc(sem("pr_free"), 1)
            dve.wait_ge(sem("pr_free"), 4 + 2 * NT * 6)

            dve.wait_ge(sem("bias_in"), 16 * 6)
            for m in range(NT):
                ins = dve.tensor_tensor(acc[:TP, m, 0:D], acc[:TP, m, 0:D], bias_b[:TP, 0:D], ALU.add)
            then(ins)
            normalized_transposed("n5", affine=True)
            router_parts("m1", "gate_in", 16)
            logits_in("m1")
            dve.tensor_tensor(share[:TP, 0, :], top_val[:TP, :, 1:2].rearrange("p m o -> p (m o)"),
                              top_val[:TP, :, 0:1].rearrange("p m o -> p (m o)"), ALU.subtract).then_inc(sem("m1_soft_in"), 1)
            dve.wait_ge(sem("m1_exp"), 1)
            then(dve.tensor_scalar(share[:TP, 2, :], share[:TP, 1, :], 1.0, None, ALU.add))
            then(dve.reciprocal(share[:TP, 2, :], share[:TP, 2, :]))
            then(dve.tensor_tensor(share[:TP, 3, :], share[:TP, 1, :], share[:TP, 2, :], ALU.mult))
            for m in range(NT):
                dve.tensor_scalar(gates[:TP, m, :], eye8[:TP, :], top_idx_f[:TP, m, 0:1], share[:TP, 2, m:m + 1],
                                  ALU.is_equal, ALU.mult)
                ins = dve.tensor_scalar(soft[:TP, m, :], eye8[:TP, :], top_idx_f[:TP, m, 1:2], share[:TP, 3, m:m + 1],
                                        ALU.is_equal, ALU.mult)
            then(ins)
            signal(dve.tensor_tensor(gates[:TP, :, :], gates[:TP, :, :], soft[:TP, :, :], ALU.add), "gates_ready", 1)
            for m in range(NT):
                for c in range(2):
                    dve.wait_ge(sem("gb_full"), 2 * m + c + 1)
                    av = acc[:TP, m, 384 * c:384 * (c + 1)]
                    ins = dve.tensor_tensor(av, ps[:TP, c + 2 * (m % 2), 0:384], av, ALU.add)
                    ins.then_inc(sem("gb_free"), 1)
            dve.wait_ge(sem("gb_free"), 2 * NT)
            experts("m1")
            for m in range(NT):
                dve.wait_ge(sem(f"last_in{m % 2}"), 16 * (m // 2 + 1))
                dve.tensor_tensor(acc[:TP, m, 0:D], acc[:TP, m, 0:D], again[:TP, m % 2, :], ALU.add
                                  ).then_inc(sem("last_sum"), 1)

        @block.tensor
        def _(pe):
            pe.wait_ge(sem("row_counts"), 1)
            for c in range(3):
                w = min(128, EJ - 128 * c)
                for b in range(NBUCKET):
                    pe.matmul(ps[:w, 0, c * NBUCKET + b:c * NBUCKET + b + 1], mask[:EP, b, c * 128:c * 128 + w],
                              ones16[:EP, 0:1], start=True, stop=True)
            pe.matmul(ps[:, 1, 0:NBUCKET], ones16[:EP, :128], row_cnt[:EP, :], start=True, stop=True
                      ).then_inc(sem("col_counts"), 1)
            pe.wait_ge(sem("col_counts_in"), 1)
            for b in range(NBUCKET):
                if b >= 4:
                    pe.wait_ge(sem("rank_used"), b - 3)
                p = ps[:EP, 2 + b % 4, :EJ]
                pe.matmul(p, below[:EP, 0, :EP], mask[:EP, b, :], start=True, stop=False)
                for c in range(3):
                    w = min(128, EJ - 128 * c)
                    ins = pe.matmul(p, col_cnt[:w, c, b:b + 1].to_broadcast([w, EP]), below[:w, 1 + c, :],
                                    start=False, stop=(c == 2))
                ins.then_inc(sem("ranks"), 1)
            pe.nop().then_inc(sem("onehot_free"), RING)
            pe.wait_ge(sem("starts_ready"), 1)
            pe.wait_ge(sem("rank_used"), NBUCKET)
            with pe.Fori(0, NBUCKET // 2) as bh:
                for u in range(2):
                    b = 2 * bh + u
                    lo = pe.value_load(tstart_i[0:1, bass.ds(b, 1)], min_val=0, max_val=UNITS - 1)
                    hi = pe.value_load(tstart_i[0:1, bass.ds(b + 1, 1)], min_val=1, max_val=UNITS)
                    pe.wait_ge(sem("adj_free"), b + 1)
                    for c, (c0, w) in enumerate(BANKS3):
                        pe.matmul(ps[:TP, 3 * u + c, :w], zeros[:, :TP], zeros[:, :w], start=True, stop=False,
                                  skip_group_check=True)
                    with pe.Fori(lo, hi) as t:
                        ring = UNIT * (t % (RING // UNIT))
                        for v in range(UNIT):
                            pe.wait_ge(sem("onehot_ready"), UNIT * t + v + 1)
                            for c, (c0, w) in enumerate(BANKS3):
                                ins = pe.matmul(ps[:TP, 3 * u + c, :w], row(oh_src, ring + v, 0, TP, 128),
                                                row(oh_dst, ring + v, c0, c0 + w, 128), start=False, stop=False,
                                                skip_group_check=True)
                            ins.then_inc(sem("onehot_free"), 1)
                    for c, (c0, w) in enumerate(BANKS3):
                        ins = pe.matmul(ps[:TP, 3 * u + c, :w], zeros[:, :TP], zeros[:, :w], start=False, stop=True,
                                        skip_group_check=True)
                    ins.then_inc(sem("adj_full"), 1)
            pe.wait_ge(sem("adj_free"), 2 + NBUCKET)
            pe.wait_ge(sem("ones_ready"), 1)
            for m in range(NT):
                for r in range(NREL):
                    for s in range(NT):
                        c0 = (NT * r + s) * N + m * TP
                        ins = pe.matmul(ps[:, 7, m * NREL + r:m * NREL + r + 1], adj_all[:TP, c0:c0 + 128],
                                        ones_col[:TP, 0:1], start=(s == 0), stop=(s == NT - 1))
            ins.then_inc(sem("counts"), 1)

            def weights(g):
                pe.wait_ge(sem("w_split"), g + 1)
                return w_of(g)

            def three(p, xs, ws, first=True, last=True):
                (xh, xl), (wh, wl) = xs, ws
                pe.matmul(p, xh, wh, start=first, stop=False)
                pe.matmul(p, xh, wl, start=False, stop=False)
                return pe.matmul(p, xl, wh, start=False, stop=last)

            def transposed(tag, K, src, ready):
                job = 0
                for m in range(NT):
                    ready(m)
                    for k0, k1 in ((0, 4), (4, K)):
                        if job >= 4:
                            pe.wait_ge(sem(f"{tag}_t_free"), job - 3)
                        for k in range(k0, k1):
                            ins = pe.transpose(ps[:, 4 + job % 4, (k - k0) * TP:(k - k0 + 1) * TP], src(m, k), ident[:TP, :TP])
                        ins.then_inc(sem(f"{tag}_t_full"), 1)
                        job += 1
                pe.wait_ge(sem(f"{tag}_t_free"), 2 * NT)

            def node_rows(K, m, w, p, c0=0, c1=None):
                wh, wl = w
                for k in range(K):
                    ins = three(p, (cols(hT_hi[:, k, :], m * TP, TP), cols(hT_lo[:, k, :], m * TP, TP)),
                                (wh[:, k, :], wl[:, k, :]), k == 0, k == K - 1)
                return ins

            def relational(L):
                K, O, nm = LAYERS[L]
                Oc = O // 2
                for n, (_, c, r, g) in enumerate(s for s in steps if s[0] == L):
                    w = weights(g)
                    with pe.Fori(0, NT // 2) as i:
                        for u in range(2):
                            m = 2 * i + u
                            pe.wait_ge(sem(f"y{L}_free"), NT * n + m + 1)
                            node_rows(K, m, w, ps[:TP, u, 0:Oc]).then_inc(sem(f"y{L}_full"), 1)
                    if r is None:
                        continue
                    z = 3 * c + r
                    pe.wait_ge(sem(f"y{L}_free"), 2 + NT * (n + 1))
                    with pe.Fori(0, NT // 2) as i:
                        for u in range(2):
                            m = 2 * i + u
                            pe.wait_ge(sem(f"z{L}_free"), NT * z + m + 1)
                            for s in range(NT):
                                x = cols(adj[:, NT * r + s, :], m * TP, TP, TP)
                                pe.matmul(ps[:TP, 2 + u, 0:Oc], x, y_hi[:TP, s, 0:Oc], start=(s == 0), stop=False)
                                ins = pe.matmul(ps[:TP, 2 + u, 0:Oc], x, y_lo[:TP, s, 0:Oc], start=False, stop=(s == NT - 1))
                            ins.then_inc(sem(f"z{L}_full"), 1)

            def from_acc(m, k):
                return acc[:TP, m, 128 * k:128 * (k + 1)]

            def once(*waits):
                def ready(m):
                    if m == 0:
                        for name, value in waits:
                            pe.wait_ge(sem(name), value)
                return ready

            transposed("t0", 7, from_acc, once(("h0_ready", 1)))
            relational(0)
            for L in (1, 2):
                transposed(f"t{L}", LAYERS[L][0], from_acc, once((f"z{L - 1}_free", 2 + 6 * NT)))
                relational(L)

            def staged(tag):
                transposed(tag, KD, lambda m, k: stage[:TP, m % 2, 128 * k:128 * (k + 1)],
                           lambda m: pe.wait_ge(sem(f"{tag}_staged"), m + 1))

            def logits(tag):
                pe.wait_ge(sem(f"{tag}_router"), 1)
                with pe.Fori(0, NT) as m:
                    for k in range(KD):
                        ins = three(ps[:, 3, bass.ds(m * EXPERTS, EXPERTS)],
                                    (cols(hT_hi_flat, m * TP + k * N, 128), cols(hT_lo_flat, m * TP + k * N, 128)),
                                    (router_hi[:, k, :], router_lo[:, k, :]), k == 0, k == KD - 1)
                        if k == KD - 1:
                            ins.then_inc(sem(f"{tag}_logits"), 1)

            def experts(tag):
                for x, (g1, g2) in enumerate(moe_pieces[tag]):
                    wh, wl = weights(g1)
                    for job in range(9):
                        hc, (c0, w) = job // 3, NODE_COLS[job % 3]
                        n = 9 * x + job
                        if n >= 2:
                            pe.wait_ge(sem(f"{tag}_h_low"), n - 1)
                        for k in range(KD):
                            f = slice(128 * hc, 128 * hc + 128)
                            p = ps[:, job % 2, 0:w]
                            pe.matmul(p, wh[:, k, f], hT_hi[:, k, c0:c0 + w], start=(k == 0), stop=False)
                            pe.matmul(p, wh[:, k, f], hT_lo[:, k, c0:c0 + w], start=False, stop=False)
                            ins = pe.matmul(p, wl[:, k, f], hT_hi[:, k, c0:c0 + w], start=False, stop=(k == KD - 1))
                        ins.then_inc(sem(f"{tag}_h_full"), 1)
                    wh, wl = weights(g2)
                    pe.wait_ge(sem(f"{tag}_h_low"), 9 * (x + 1))
                    with pe.Fori(0, NT // 2) as i:
                        for u in range(2):
                            m = 2 * i + u
                            pe.wait_ge(sem(f"{tag}_o_free"), NT * x + m + 1)
                            for c in range(2):
                                for k in range(KH):
                                    ins = three(ps[:TP, 2 + 2 * u + c, 0:384],
                                                (cols(ht_hi[:, k, :], m * TP, TP), cols(ht_lo[:, k, :], m * TP, TP)),
                                                (wh[:, k, 384 * c:384 * (c + 1)], wl[:, k, 384 * c:384 * (c + 1)]),
                                                k == 0, k == KH - 1)
                                ins.then_inc(sem(f"{tag}_o_full"), 1)

            staged("n1")
            logits("m0")
            experts("m0")
            staged("n2")
            pe.wait_ge(sem("adj_sum"), 1)
            for c in range(2):
                w = weights(gcn_pieces[c])
                with pe.Fori(0, NT // 2) as i:
                    for u in range(2):
                        m = 2 * i + u
                        pe.wait_ge(sem("gy_free"), NT * c + m + 1)
                        node_rows(KD, m, w, ps[:TP, u, 0:384]).then_inc(sem("gy_full"), 1)
                pe.wait_ge(sem("gy_free"), 2 + NT * (c + 1))
                with pe.Fori(0, NT // 2) as i:
                    for u in range(2):
                        m = 2 * i + u
                        pe.wait_ge(sem("gz_free"), NT * c + m + 1)
                        for s in range(NT):
                            x = cols(adj[:, s, :], m * TP, TP, TP)
                            pe.matmul(ps[:TP, 2 + u, 0:384], x, y_hi[:TP, s, 0:384], start=(s == 0), stop=False)
                            ins = pe.matmul(ps[:TP, 2 + u, 0:384], x, y_lo[:TP, s, 0:384], start=False, stop=(s == NT - 1))
                        ins.then_inc(sem("gz_full"), 1)
            staged("n4")
            for c in range(2):
                w = weights(v_pieces[c])
                with pe.Fori(0, NT // 2) as i:
                    for u in range(2):
                        m = 2 * i + u
                        pe.wait_ge(sem("v_low"), NT * c + m + 1)
                        node_rows(KD, m, w, ps[:TP, u, 0:384]).then_inc(sem("v_full"), 1)
            pe.nop().then_inc(sem("pv_full"), 4)
            pe.wait_ge(sem("v_low"), 2 + 2 * NT)
            job = 0
            for j in range(HEADS // 2):
                wh, wl = weights(qk_pieces[j])
                if j:
                    pe.wait_ge(sem("ot_low"), 3 * j)
                for which in range(2):
                    for c0, w in NODE_COLS:
                        job += 1
                        if job > 2:
                            pe.wait_ge(sem("qk_moved"), 2 * (job - 2))
                        p = ps[:, (job - 1) % 2, 0:w]
                        f = slice(128 * which, 128 * which + 128)
                        for k in range(KD):
                            pe.matmul(p, wh[:, k, f], hT_hi[:, k, c0:c0 + w], start=(k == 0), stop=False)
                            pe.matmul(p, wh[:, k, f], hT_lo[:, k, c0:c0 + w], start=False, stop=False)
                            ins = pe.matmul(p, wl[:, k, f], hT_hi[:, k, c0:c0 + w], start=False, stop=(k == KD - 1))
                        ins.then_inc(sem("qk_full"), 1)
                pe.wait_ge(sem("qk_parts"), 6 * (j + 1))
                if j:
                    pe.wait_ge(sem("pr_free"), 4 + 2 * NT * j)
                for h2 in range(2):
                    with pe.Fori(0, NT // 2) as i:
                        for u in range(2):
                            t = 2 * i + u
                            pe.wait_ge(sem("max_free"), (2 * j + h2) * NT + t + 1)
                            for c, (c0, w) in enumerate(BANKS3):
                                ins = pe.matmul(ps[:TP, 3 * u + c, :w], q_a[:, h2, bass.ds(t * TP, TP)],
                                                k_a[:, h2, c0:c0 + w], start=True, stop=True)
                            ins.then_inc(sem("max_full"), 1)
                pe.wait_ge(sem("max_free"), 2 + (2 * j + 2) * NT)
                for h2 in range(2):
                    for t in range(NT):
                        ins = pe.matmul(ps[64:65, 3 * h2 + t // 4, (t % 4) * TP:(t % 4 + 1) * TP], row_max[:TP, h2, t:t + 1],
                                        ident[:TP, :TP], start=True, stop=True)
                    ins.then_inc(sem("max_rows"), 1)
                pe.wait_ge(sem("max_set"), 2 * (j + 1))
                pe.wait_ge(sem("ones_set"), 1)
                def scores(qc, h2):
                    n = 10 * j + 2 * qc + h2
                    for kp in range(5):
                        pe.wait_ge(sem("exp_done"), 5 * n + kp + 1)
                        for e in range(2):
                            kt = 2 * kp + e
                            p = ps[:TP, kp, QC * e:QC * (e + 1)]
                            pe.matmul(p, k_a[:, h2, kt * TP:(kt + 1) * TP], q_a[:, h2, bass.ds(qc * QC, QC)],
                                      start=True, stop=False)
                            ins = pe.matmul(p, k_b[0:96, h2, kt * TP:(kt + 1) * TP], q_b[0:96, h2, bass.ds(qc * QC, QC)],
                                            start=False, stop=True)
                        ins.then_inc(sem("s_full"), 1)

                def values(qc, h2):
                    n = 10 * j + 2 * qc + h2
                    pe.wait_ge(sem("p_low"), 2 + 5 * n + 5)
                    for u in range(2):
                        pe.wait_ge(sem("o_free"), 2 * n + u + 1)
                        p = ps[:, 5 + u, 0:HD + 1]
                        for kt in range(NT):
                            ph, pl = p_hi[:TP, h2, kt, u * TP:u * TP + 128], p_lo[:TP, h2, kt, u * TP:u * TP + 128]
                            v = v_parts[:TP, kt, 2 * j + h2, :]
                            pe.matmul(p, ph, v[:, 0:HD + 1], start=(kt == 0), stop=False)
                            pe.matmul(p[:, 0:HD], ph, v[:, HD + 1:129], start=False, stop=False)
                            ins = pe.matmul(p, pl, v[:, 0:HD + 1], start=False, stop=(kt == NT - 1))
                        ins.then_inc(sem("pv_full"), 1)

                scores(0, 0)
                with pe.Fori(0, NT // 2 - 1) as qc:
                    scores(qc, 1)
                    values(qc, 0)
                    scores(qc + 1, 0)
                    values(qc, 1)
                scores(NT // 2 - 1, 1)
                values(NT // 2 - 1, 0)
                values(NT // 2 - 1, 1)
                pe.wait_ge(sem("o_free"), 2 + 2 * 5 * 2 * (j + 1))
                for t in range(3):
                    for m in range(4 * t, min(4 * t + 4, NT)):
                        ins = pe.transpose(ps[:, t, (m % 4) * TP:(m % 4 + 1) * TP], o_pair[:TP, m, :], ident[:TP, :TP])
                    ins.then_inc(sem("ot_full"), 1)
                wh, wl = weights(proj_pieces[j])
                pe.wait_ge(sem("ot_low"), 3 * (j + 1))
                with pe.Fori(0, NT // 2) as i:
                    for u in range(2):
                        m = 2 * i + u
                        for c in range(2):
                            pe.wait_ge(sem("pr_free"), 2 * NT * j + 2 * m + c + 1)
                            three(ps[:TP, 3 + 2 * u + c, 0:384], (cols(ot_hi, m * TP, TP), cols(ot_lo, m * TP, TP)),
                                  (wh[:, 0, 384 * c:384 * (c + 1)], wl[:, 0, 384 * c:384 * (c + 1)])
                                  ).then_inc(sem("pr_full"), 1)
            staged("n5")
            logits("m1")
            pe.wait_ge(sem("gates_ready"), 1)
            for q in range(3):
                for m in range(4 * q, min(4 * q + 4, NT)):
                    ins = pe.transpose(ps[0:EXPERTS, 4 + q, (m % 4) * TP:(m % 4 + 1) * TP], gates[:TP, m, :], ident[:TP, :TP])
                ins.then_inc(sem("gt_full"), 1)
            pe.wait_ge(sem("gt_done"), 3)
            pe.wait_ge(sem("b2_in"), 16)
            for m in range(NT):
                for c in range(2):
                    if m >= 2:
                        pe.wait_ge(sem("gb_free"), 2 * (m - 2) + c + 1)
                    pe.matmul(ps[:TP, c + 2 * (m % 2), 0:384], gate_t[:, m * TP:(m + 1) * TP], b2_rows[:, 384 * c:384 * (c + 1)],
                              start=True, stop=True).then_inc(sem("gb_full"), 1)
            pe.wait_ge(sem("gb_free"), 2 * NT)
            experts("m1")


def kernel(**x):
    import numpy as np
    import concourse.bacc as bacc
    from concourse.bass_utils import run_bass_kernel_spmd

    host = {k: np.asarray(v) for k, v in x.items()}
    pairs = HEADS // 2
    qkv_t = host["L1_ffn_qkv_w"].T
    w_qk = np.concatenate([qkv_t[:, 0:D].reshape(D, pairs, 128), qkv_t[:, D:2 * D].reshape(D, pairs, 128)], axis=2)
    arrays = {
        "x": host["x"], "src": host["src"], "dst": host["dst"], "typ": host["edge_type_3"],
        "node_type": host["node_type_3"].reshape(NT, TP).T,
        "emb": host["L0_gnn_node_emb"],
        "rel1": host["L0_gnn_w_rel1"], "root1": host["L0_gnn_w_root1"], "b1": host["L0_gnn_b1"],
        "rel2": host["L0_gnn_w_rel2"], "root2": host["L0_gnn_w_root2"], "b2": host["L0_gnn_b2"],
        "rel3": host["L0_gnn_w_rel3"], "root3": host["L0_gnn_w_root3"], "b3": host["L0_gnn_b3"],
        "router": host["L0_ffn_router_w"], "wi": host["L0_ffn_wi"], "wo": host["L0_ffn_wo"],
        "gcn_w": host["L1_gnn_W"], "gcn_b": host["L1_gnn_b"],
        "n1_w": host["L1_ffn_norm1_w"], "n1_b": host["L1_ffn_norm1_b"],
        "w_qk": w_qk.transpose(1, 0, 2), "w_v": qkv_t[:, 2 * D:],
        "qk_b": host["L1_ffn_qkv_b"][0:2 * D].reshape(12, 128).T, "v_b": host["L1_ffn_qkv_b"][2 * D:],
        "w_proj": host["L1_ffn_proj_w"].T, "proj_b": host["L1_ffn_proj_b"],
        "n2_w": host["L1_ffn_norm2_w"], "n2_b": host["L1_ffn_norm2_b"],
        "w_gate": host["L1_ffn_w_gate"],
        "w1": host["L1_ffn_W1"], "b1x": host["L1_ffn_b1"].reshape(EXPERTS * KH, 128).T,
        "w2": host["L1_ffn_W2"], "b2x": host["L1_ffn_b2"],
    }
    nc = bacc.Bacc("TRN2", target_bir_lowering=False, num_devices=1)
    feed, aps = {}, {}
    for name, v in arrays.items():
        v = np.ascontiguousarray(v)
        feed[f"in_{name}"] = v
        aps[name] = nc.dram_tensor(f"in_{name}", v.shape, mybir.dt.from_np(v.dtype), kind="ExternalInput").ap()
    out = nc.dram_tensor("out_nodes", (N, D), F32, kind="ExternalOutput").ap()
    build(nc, aps, out)
    return run_bass_kernel_spmd(nc, [feed], core_ids=[0]).results[0]["out_nodes"]
```

```python
from contextlib import ExitStack

import concourse.bass as bass
from concourse import mybir

F32, F16 = mybir.dt.float32, mybir.dt.float16
I32, U32 = mybir.dt.int32, mybir.dt.uint32
ALU = mybir.AluOpType
ACT = mybir.ActivationFunctionType
AX_X = mybir.AxisListType.X

N = 1250
TP = 125
NT = N // TP
D = 768
KD = D // 128
NREL = 3
EP = 125
NBUCKET = NREL * NT
EXPERTS = 8
HID = 384
KH = HID // 128
HEADS = 12
HD = 64
QC = 2 * TP
LAYERS = ((7, 896, "1"), (7, 768, "2"), (6, 768, "3"))
WMAX = 7 * 448
NODE_COLS = ((0, 418), (418, 416), (834, 416))
BANKS3 = ((0, 512), (512, 512), (1024, 226))
RING = 4
PICKS = {"m0": 1, "m1": 2}
SLOT_TILES = {tag: (n * N + 127 * EXPERTS) // 128 for tag, n in PICKS.items()}
TABLE_COLS = {tag: n + 1 for tag, n in SLOT_TILES.items()}
UNIT = 2


def build(nc, a, out):
    E = a["src"].shape[0]
    EJ = E // EP
    UNITS = E // (UNIT * 128) + NBUCKET + 1
    ETILES = UNIT * UNITS
    PAD_EDGE = (N + 50) * 128 + 127

    ctx = ExitStack()
    with ctx:
        sems = {}

        def sem(name):
            if name not in sems:
                sems[name] = ctx.enter_context(nc.semaphore(name))
            return sems[name]

        def sb(name, shape, dt=F32, scope=ctx):
            return scope.enter_context(nc.sbuf_tensor(name, shape, dt))

        ident = sb("ident", [128, 128])
        bias_b = sb("bias_b", [128, 896])
        inv_cnt = sb("inv_cnt", [128, NT, NREL])
        dinv = sb("dinv", [128, NT])
        stats = sb("stats", [128, NT, 2, 6])
        meanvar = sb("meanvar", [128, NT, 2])
        rstd = sb("rstd", [128, NT])
        minus_half = sb("minus_half", [128, NT])
        gates = sb("gates", [128, NT, EXPERTS])
        token = sb("token", [128, NT])
        ident16 = sb("ident16", [128, 128], F16)
        one_of = sb("one_of", [128, 128], F16)
        before = sb("before", [128, 128], F16)
        ones_col = sb("ones_col", [128, 2], F16)
        eye8 = sb("eye8", [128, EXPERTS])
        node_type = sb("node_type", [128, NT], I32)
        type_f = sb("type_f", [128, NT])
        top_val = sb("top_val", [128, NT, 8])
        top_idx = sb("top_idx", [128, NT, 8], U32)
        top_idx_f = sb("top_idx_f", [128, NT, 8])
        logit = sb("logit", [128, NT, EXPERTS])
        soft = sb("soft", [128, NT, EXPERTS])
        share = sb("share", [128, 4, NT])
        recip = sb("recip", [128, 2])
        router32 = sb("router32", [128, KD, EXPERTS])
        router_hi = sb("router_hi", [128, KD, EXPERTS], F16)
        router_lo = sb("router_lo", [128, KD, EXPERTS], F16)
        pidx = sb("pidx", [128, 4])
        tstart_i = sb("tstart_i", [128, NBUCKET + 1], I32)
        wraw = sb("wraw", [128, WMAX])
        whi = sb("whi", [128, 2, WMAX], F16)
        wlo = sb("wlo", [128, 2, WMAX], F16)
        qk_bias = sb("qk_bias", [128, 12])
        b1_cols = sb("b1_cols", [128, EXPERTS * KH])

        edge = ExitStack()
        iota_n = sb("iota_n", [128, N], F16, edge)
        ones16 = sb("ones16", [128, 128], F16, edge)
        e_src = sb("e_src", [128, EJ], I32, edge)
        e_dst = sb("e_dst", [128, EJ], I32, edge)
        e_typ = sb("e_typ", [128, EJ], I32, edge)
        src_tile = sb("src_tile", [128, EJ], F32, edge)
        bucket = sb("bucket", [128, EJ], F32, edge)
        src_loc = sb("src_loc", [128, EJ], F32, edge)
        packed_f = sb("packed_f", [128, EJ], F32, edge)
        packed = sb("packed", [128, EJ], I32, edge)
        mask = sb("mask", [128, NBUCKET, EJ], F16, edge)
        below = sb("below", [128, 4, EJ], F16, edge)
        col_cnt = sb("col_cnt", [128, 3, NBUCKET], F16, edge)
        row_cnt = sb("row_cnt", [128, NBUCKET], F16, edge)
        tiles_f = sb("tiles_f", [128, NBUCKET], F32, edge)
        tiles_i = sb("tiles_i", [128, NBUCKET], I32, edge)
        tstart = sb("tstart", [128, NBUCKET + 1], F32, edge)
        first_slot = sb("first_slot", [128, NBUCKET], F32, edge)
        slot = sb("slot", [128, EJ], F32, edge)
        slot_part = sb("slot_part", [128, 2, EJ], F32, edge)
        slot_i = sb("slot_i", [128, EJ], I32, edge)
        lane_i = sb("lane_i", [128, EJ], I32, edge)
        tile_i = sb("tile_i", [128, EJ], I32, edge)
        lane_f = sb("lane_f", [128, EJ], F32, edge)
        addr_f = sb("addr_f", [128, EJ], F32, edge)
        addr = sb("addr", [128, EJ], U32, edge)
        pad_fill = sb("pad_fill", [128, ETILES], I32, edge)
        sorted_p = sb("sorted_p", [128, ETILES], I32, edge)
        sorted_i = sb("sorted_i", [128, 2, ETILES], I32, edge)
        sorted_f = sb("sorted_f", [128, 2, ETILES], F32, edge)
        oh_dst = sb("oh_dst", [128, RING, N], F16, edge)
        oh_src = sb("oh_src", [128, RING, TP], F16, edge)
        zeros = sb("zeros", [128, 512], F16, edge)
        pad_records = [sb(f"pad_records{i}", [128, cols, 4], F32, edge) for i, cols in enumerate(TABLE_COLS.values())]
        edge.close()

        mt = ExitStack()
        rows_ring = sb("rows_ring", [128, 3, 2 * D], F16, mt)
        out_ring = sb("out_ring", [128, 2, D], F32, mt)
        gt_hi = sb("gt_hi", [128, KD, 128], F16, mt)
        gt_lo = sb("gt_lo", [128, KD, 128], F16, mt)
        ht_hi = sb("ht_hi", [128, KH, 128], F16, mt)
        ht_lo = sb("ht_lo", [128, KH, 128], F16, mt)
        gelu32 = sb("gelu32", [128, KH, 128], F32, mt)
        mt.close()
        yb = ExitStack()
        second_back = sb("second_back", [128, NT, D], F32, yb)
        yb.close()

        hT_hi = sb("hT_hi", [128, 7, N], F16)
        hT_lo = sb("hT_lo", [128, 7, N], F16)
        hT_hi_flat, hT_lo_flat = (t[:, :, :].rearrange("p k n -> p (k n)") for t in (hT_hi, hT_lo))
        acc = sb("acc", [128, NT, 896])
        y = ExitStack()
        y_hi = sb("y_hi", [128, NT, 448], F16, y)
        y_lo = sb("y_lo", [128, NT, 448], F16, y)
        adj_all = sb("adj", [128, NBUCKET * N + 4], F16, y)
        adj = adj_all[:, 0:NBUCKET * N].rearrange("p (b n) -> p b n", n=N)
        y.close()
        e0 = ExitStack()
        stage = sb("stage", [128, 2, D], F32, e0)
        again = sb("again", [128, 2, D], F32, e0)
        ln_w = sb("ln_w", [128, D], F32, e0)
        ln_b = sb("ln_b", [128, D], F32, e0)
        e1 = ExitStack()
        packed_rows = sb("packed_rows", [128, 3, 2, D], F16, e1)
        w2_raw = sb("w2_raw", [128, KH * D], F32, e1)
        w2_hi = sb("w2_hi", [128, 2, KH * D], F16, e1)
        w2_lo = sb("w2_lo", [128, 2, KH * D], F16, e1)
        gate_t = sb("gate_t", [EXPERTS, N], F32, e1)
        b2_rows = sb("b2_rows", [EXPERTS, D], F32, e1)
        chosen = sb("chosen", [128, 2, NT, EXPERTS], F32, e1)
        chosen16 = sb("chosen16", [128, NT, EXPERTS], F16, e1)
        expert_slot = sb("expert_slot", [128, NT, EXPERTS], F32, e1)
        picked_slot = sb("picked_slot", [128, NT, EXPERTS], F32, e1)
        token_slot = sb("token_slot", [128, 2, NT], F32, e1)
        token_slot_i = sb("token_slot_i", [128, 3, 2, NT], I32, e1)
        token_addr_f = sb("token_addr_f", [128, 2, NT], F32, e1)
        token_addr = sb("token_addr", [128, 2, NT], U32, e1)
        records = sb("records", [128, 2, NT, 4], F32, e1)
        expert_tiles_f = sb("expert_tiles_f", [128, EXPERTS], F32, e1)
        expert_tiles_i = sb("expert_tiles_i", [128, EXPERTS], I32, e1)
        expert_start = sb("expert_start", [128, EXPERTS + 1], F32, e1)
        expert_start_i = sb("expert_start_i", [128, EXPERTS + 1], I32, e1)
        expert_slot0 = sb("expert_slot0", [128, EXPERTS], F32, e1)
        table = sb("table", [128, TABLE_COLS["m1"], 4], F32, e1)
        gather_row = sb("gather_row", [128, TABLE_COLS["m1"]], U32, e1)
        scatter_row = sb("scatter_row", [128, TABLE_COLS["m1"]], U32, e1)
        slot_gate = sb("slot_gate", [128, TABLE_COLS["m1"]], F32, e1)
        e1.close()
        e2 = ExitStack()
        first_back = sb("first_back", [128, NT, D], F32, e2)
        e2.close()
        e0.close()
        at = ExitStack()
        v_parts = sb("v_parts", [128, NT, HEADS, 129], F16, at)
        qk32 = sb("qk32", [128, 2, 418], F32, at)
        q_a = sb("q_a", [128, 2, N], F16, at)
        k_a = sb("k_a", [128, 2, N], F16, at)
        q_b = sb("q_b", [128, 2, N], F16, at)
        k_b = sb("k_b", [128, 2, N], F16, at)
        p32 = sb("p32", [128, 2, 2 * QC], F32, at)
        p_hi = sb("p_hi", [128, 2, NT, QC + 6], F16, at)
        p_lo = sb("p_lo", [128, 2, NT, QC + 6], F16, at)
        o_pair = sb("o_pair", [128, NT, 128], F32, at)
        ot_hi = sb("ot_hi", [128, N], F16, at)
        ot_lo = sb("ot_lo", [128, N], F16, at)
        row_max = sb("row_max", [128, 2, NT], F32, at)
        at.close()

        ps = ctx.enter_context(nc.psum_tensor("ps", [128, 8, 512], F32))
        x3_dram = nc.dram_tensor("x3_dram", [N, D], F32, kind="Internal").ap()
        rows_dram = nc.dram_tensor("token_rows", [N, 2 * D], F16, kind="Internal").ap()
        table_dram, moe_dram = {}, {}
        for tag, cols_ in TABLE_COLS.items():
            table_dram[tag] = nc.dram_tensor(f"table_{tag}", [128 * cols_, 4], F32, kind="Internal").ap()
            moe_dram[tag] = nc.dram_tensor(f"moe_{tag}", [PICKS[tag] * N + 128 * cols_, D], F32, kind="Internal").ap()
        edge_dram = nc.dram_tensor("edge_slots", [128 * ETILES, 1], I32, kind="Internal").ap()

        pieces = []

        def piece(src, k, cols, done, value):
            pieces.append((src, k, cols, done, value))
            return len(pieces) - 1

        steps = []
        for L, (K, O, nm) in enumerate(LAYERS):
            Oc = O // 2
            for c in range(2):
                for r in (None, 0, 1, 2):
                    w = a[f"root{nm}"] if r is None else a[f"rel{nm}"][r]
                    v = w.rearrange("(k p) n -> p k n", p=128)[:, :, c * Oc:(c + 1) * Oc]
                    n = sum(1 for s in steps if s[0] == L)
                    steps.append((L, c, r, piece(v, K, Oc, "y_full", NT * (8 * L + n + 1))))
        gcn_pieces = [piece(a["gcn_w"].rearrange("(k p) n -> p k n", p=128)[:, :, c * 384:(c + 1) * 384],
                            KD, 384, "gy_full", NT * (c + 1)) for c in range(2)]
        v_pieces = [piece(a["w_v"].rearrange("(k p) n -> p k n", p=128)[:, :, c * 384:(c + 1) * 384],
                          KD, 384, "v_full", NT * (c + 1)) for c in range(2)]
        qk_pieces, proj_pieces = [], []
        for j in range(HEADS // 2):
            qk_pieces.append(piece(a["w_qk"][j].rearrange("(k p) n -> p k n", p=128), KD, 256, "qk_full", 6 * (j + 1)))
            proj_pieces.append(piece(a["w_proj"][128 * j:128 * (j + 1), :].rearrange("(k p) n -> p k n", p=128),
                                     1, D, "pr_full", 2 * NT * (j + 1)))
        expert_weights = {"m0": (a["wi"], a["wo"]), "m1": (a["w1"], a["w2"])}
        first_part = len(steps)

        def w_of(g):
            _, k, cols, _, _ = pieces[g]
            v = lambda t: t[:, g % 2, 0:k * cols].rearrange("p (k n) -> p k n", k=k)
            return v(whi), v(wlo)

        def row(reg3, i, lo, hi, parts=TP):
            return reg3[:parts, bass.ds(i, 1), lo:hi].rearrange("p o n -> p (o n)")

        def cols(t2, start, n, parts=128):
            return t2[:parts, bass.ds(start, n)]

        def row_bias(name):
            v = a[name].rearrange("(o d) -> o d", o=1)
            return v.broadcast_to([TP, v.shape[1]])

        p32_flat = p32[:, :, :].rearrange("p a b -> p (a b)")
        block = ctx.enter_context(nc.Block())

        def powers(tag):
            return ("deg", "n0", "n1", "n2", "n3", "n4", "n5").index(tag)

        def nth(tag):
            return {"m0": 1, "m1": 2}[tag]

        def block_of(tag):
            return EXPERTS * (nth(tag) - 1)

        def staged_before(tag):
            return NT * ("n1", "n2", "n4", "n5").index(tag)

        def turned_before(tag):
            return 2 * NT * ("t0", "t1", "t2", "n1", "n2", "n4", "n5").index(tag)


        @block.sync
        def _(sp):
            for t, n in ((e_src, "src"), (e_dst, "dst"), (e_typ, "typ")):
                sp.dma_start(t[:EP, :], a[n].rearrange("(p j) -> p j", p=EP)).then_inc(sem("edges_in"), 16)

            def load_pieces(first, last):
                for g in range(first, min(last, len(pieces))):
                    src, k, n, _, _ = pieces[g]
                    if g == first_part:
                        sp.wait_ge(sem("w1_split"), EXPERTS)
                    elif g >= 1:
                        sp.wait_ge(sem("w_split"), g)
                    sp.dma_start(wraw[:, 0:k * n].rearrange("p (k n) -> p k n", k=k), src).then_inc(sem("w_in"), 16)

            def load_experts(tag, split, region, value):
                w1, w2 = expert_weights[tag]
                for x in range(EXPERTS):
                    if x:
                        sp.wait_ge(sem("w1_split"), block_of(tag) + x)
                    else:
                        sp.wait_ge(sem("w_split"), split)
                    sp.dma_start(wraw[:, 0:KD * HID].rearrange("p (k n) -> p k n", k=KD),
                                 w1[x].rearrange("(k p) n -> p k n", p=128)).then_inc(sem("w1_in"), 16)
                    if x == 0:
                        for m in range(NT):
                            sp.wait_ge(sem("pack_low"), NT * nth(tag) - NT + m + 1)
                            sp.dma_start(rows_dram[m * TP:(m + 1) * TP, :],
                                         packed_rows[:TP, m % 3, :, :].rearrange("p a d -> p (a d)")
                                         ).then_inc(sem(f"{tag}_rows_out{m % 3}"), 16)
                        sp.wait_ge(sem(region), value)
                    else:
                        sp.wait_ge(sem("w2_split"), block_of(tag) + x)
                    sp.dma_start(w2_raw[:, :].rearrange("p (k n) -> p k n", k=KH),
                                 w2[x].rearrange("(k p) n -> p k n", p=128)).then_inc(sem("w2_in"), 16)

            load_pieces(0, first_part)
            load_experts("m0", first_part, "adj_sum", 1)
            load_pieces(first_part, len(pieces))
            load_experts("m1", len(pieces), "pr_free", 4 + 2 * NT * 6)

        @block.gpsimd
        def _(pool):
            pool.iota(pidx[:, 0:1], [[0, 1]], base=0, channel_multiplier=1,
                      allow_small_or_imprecise_dtypes=True).then_inc(sem("iota_ready"), 1)
            pool.iota(iota_n[:, :], [[1, N]], base=0, channel_multiplier=0,
                      allow_small_or_imprecise_dtypes=True).then_inc(sem("iota_ready"), 1)
            pool.iota(eye8[:, :], [[1, EXPERTS]], base=0, channel_multiplier=0,
                      allow_small_or_imprecise_dtypes=True).then_inc(sem("iota_ready"), 1)
            pool.iota(token[:, :], [[TP, NT]], base=0, channel_multiplier=1,
                      allow_small_or_imprecise_dtypes=True).then_inc(sem("iota_ready"), 1)
            for t, (tag, cols_) in zip(pad_records, TABLE_COLS.items()):
                pool.memset(t[:, :, 0:1], 0.0)
                pool.memset(t[:, :, 2:4], 0.0)
                pool.iota(t[:, :, 1:2].rearrange("p a o -> p (a o)"), [[1, cols_]], base=PICKS[tag] * N,
                          channel_multiplier=cols_, allow_small_or_imprecise_dtypes=True).then_inc(sem("pad_ready"), 1)
            pool.memset(pad_fill[:, :], PAD_EDGE).then_inc(sem("pad_ready"), 1)
            pool.memset(minus_half[:, :], -0.5).then_inc(sem("half_ready"), 1)
            split = [0]

            def split_to(last):
                while split[0] <= min(last, len(pieces) - 1):
                    g = split[0]
                    _, k, n, _, _ = pieces[g]
                    raw, hi, lo = wraw[:, 0:k * n], whi[:, g % 2, 0:k * n], wlo[:, g % 2, 0:k * n]
                    pool.wait_ge(sem("w_in"), 16 * (g + 1))
                    if g >= 2 and g not in (first_part, first_part + 1):
                        pool.wait_ge(sem(pieces[g - 2][3]), pieces[g - 2][4])
                    pool.tensor_copy(hi, raw).then_inc(sem("w_high"), 1)
                    pool.wait_ge(sem("w_high"), g + 1)
                    pool.tensor_tensor(lo, raw, hi, ALU.subtract).then_inc(sem("w_split"), 1)
                    split[0] += 1

            def power(tag, t):
                pool.wait_ge(sem("half_ready"), 1)
                pool.wait_ge(sem("variance"), 1 + powers(tag))
                pool.tensor_tensor(t[:TP, :], t[:TP, :], minus_half[:TP, :], ALU.pow).then_inc(sem("rstd_ready"), 1)

            split_to(1)
            pool.wait_ge(sem("padded"), 48)
            pool.wait_ge(sem("addr_ready"), 1)
            for j in range(EJ):
                pool.indirect_dma_start(edge_dram[:, :], bass.IndirectOffsetOnAxis(ap=addr[:EP, j:j + 1], axis=0),
                                        packed[:EP, j:j + 1], None).then_inc(sem("scattered"), 16)
            power("deg", dinv)
            power("n0", rstd)
            split_to(first_part - 1)
            pool.wait_ge(sem("z_full"), 18 * NT)
            for s in range(NT):
                pool.tensor_tensor(adj[:TP, 2 * NT + s, :], adj[:TP, 2 * NT + s, :], adj[:TP, s, :], ALU.add
                                   ).then_inc(sem("adj_first"), 1)
            power("n1", rstd)
            for s in range(NT):
                t = adj[:TP, 2 * NT + s, :]
                pool.wait_ge(sem("adj_first"), s + 1)
                pool.tensor_tensor(t, t, adj[:TP, NT + s, :], ALU.add).then_inc(sem("adj_second"), 1)
            for s in range(NT):
                dg = adj[:TP, 2 * NT + s, s * TP:(s + 1) * TP]
                pool.wait_ge(sem("adj_second"), s + 1)
                ins = pool.tensor_tensor(dg, dg, ident[:TP, :TP], ALU.add)
            ins.then_inc(sem("adj_sum"), 1)

            def move_rows(tag):
                pool.wait_ge(sem("padded"), 48)
                pool.wait_ge(sem("records"), nth(tag))
                for c in range(PICKS[tag]):
                    for m in range(NT):
                        pool.indirect_dma_start(table_dram[tag][:, :],
                                                bass.IndirectOffsetOnAxis(ap=token_addr[:TP, c, m:m + 1], axis=0),
                                                records[:TP, c, m, :], None).then_inc(sem(f"{tag}_records_out"), 16)
                pool.wait_ge(sem(f"{tag}_table"), 1)
                for i, n in enumerate((4, 3, 3)):
                    pool.wait_ge(sem(f"{tag}_rows_out{i}"), 16 * n)
                pool.nop().then_inc(sem(f"{tag}_out_free"), 2)

                def gather(t):
                    if t:
                        pool.wait_ge(sem(f"{tag}_gathered"), 16 * t)
                    if t >= 3:
                        pool.wait_ge(sem(f"{tag}_turned"), t - 2)
                    pool.indirect_dma_start(rows_ring[:, t % 3, :], None, rows_dram[:, :],
                                            bass.IndirectOffsetOnAxis(ap=gather_row[:, t:t + 1], axis=0)
                                            ).then_inc(sem(f"{tag}_gathered"), 16)

                gather(0)
                gather(1)
                for t in range(SLOT_TILES[tag]):
                    if t + 2 < TABLE_COLS[tag]:
                        gather(t + 2)
                    if t:
                        pool.wait_ge(sem(f"{tag}_scattered"), 16 * t)
                        pool.nop().then_inc(sem(f"{tag}_out_free"), 1)
                    pool.wait_ge(sem(f"{tag}_o_left"), t + 2)
                    pool.wait_ge(sem(f"{tag}_o_right"), t + 2)
                    pool.indirect_dma_start(moe_dram[tag][:, :],
                                            bass.IndirectOffsetOnAxis(ap=scatter_row[:, t:t + 1], axis=0),
                                            out_ring[:, t % 2, :], None).then_inc(sem(f"{tag}_scattered"), 16)
                pool.wait_ge(sem(f"{tag}_gathered"), 16 * TABLE_COLS[tag])

            move_rows("m0")
            split_to(gcn_pieces[1])
            power("n2", rstd)
            split_to(v_pieces[1])
            power("n3", rstd)
            power("n4", rstd)
            split_to(proj_pieces[0])
            for j in range(HEADS // 2 - 1):
                split_to(proj_pieces[j + 1])
            power("n5", rstd)
            move_rows("m1")

        @block.scalar
        def _(act):
            act.dma_start(qk_bias[:, :], a["qk_b"]).then_inc(sem("consts_in"), 16)
            act.dma_start(b1_cols[:, :], a["b1x"]).then_inc(sem("consts_in"), 16)
            act.dma_start(node_type[:TP, :], a["node_type"]).then_inc(sem("consts_in"), 16)
            act.dma_start(router32[:, :, :], a["router"].rearrange("(k p) n -> p k n", p=128)).then_inc(sem("consts_in"), 16)
            act.wait_ge(sem("pad_ready"), 3)
            act.dma_start(edge_dram.rearrange("(p t) o -> p (t o)", p=128), pad_fill[:, :]).then_inc(sem("padded"), 16)
            for t, d in zip(pad_records, table_dram.values()):
                act.dma_start(d.rearrange("(p t) f -> p t f", p=128), t[:, :, :]).then_inc(sem("padded"), 16)
            act.wait_ge(sem("scattered"), 16 * EJ)
            act.dma_start(sorted_p[:, :], edge_dram.rearrange("(p t) o -> p (t o)", p=128)).then_inc(sem("sorted_in"), 16)
            act.nop().then_inc(sem("adj_free"), 2)
            with act.Fori(0, NBUCKET // 2) as bh:
                for u in range(2):
                    act.wait_ge(sem("adj_full"), 2 * bh + u + 1)
                    act.activation(row(adj, 2 * bh + u, 0, N), ps[:TP, 3 * u:3 * u + 3, :].rearrange("p a b -> p (a b)")[:, :N],
                                   ACT.Copy).then_inc(sem("adj_free"), 1)
            act.wait_ge(sem("adj_full"), NBUCKET)
            act.dma_start(acc[:TP, :, 0:D], a["x"].rearrange("(t p) d -> p t d", p=TP)).then_inc(sem("x_in"), 16)
            for t in range(3):
                act.dma_start(bias_b[:TP, 128 * t:128 * (t + 1)], a["emb"][t:t + 1, :].broadcast_to([TP, 128])
                              ).then_inc(sem("x_in"), 16)

            def transposed(tag, K, func, pack=None):
                job = 0
                for m in range(NT):
                    if pack:
                        act.wait_ge(sem("staged"), staged_before(tag) + m + 1)
                        if m >= 3:
                            act.wait_ge(sem(f"{pack}_rows_out{m % 3}"), 16 * (m // 3))
                        act.activation(packed_rows[:TP, m % 3, 0, :], stage[:TP, m % 2, :], ACT.Copy
                                       ).then_inc(sem(f"pack_high"), 1)
                    for k0, k1 in ((0, 4), (4, K)):
                        act.wait_ge(sem("t_full"), turned_before(tag) + job + 1)
                        act.activation(hT_hi[:, k0:k1, m * TP:(m + 1) * TP],
                                       ps[:, 4 + job % 4, 0:(k1 - k0) * TP].rearrange("p (k n) -> p k n", n=TP),
                                       func).then_inc(sem("t_high"), 1)
                        job += 1

            def relational(L):
                K, O, nm = LAYERS[L]
                Oc = O // 2
                yj = 0
                for n, (_, c, r, g) in enumerate(s for s in steps if s[0] == L):
                    if r is not None:
                        done = NT * (6 * L + 3 * c + r)
                        if done:
                            act.wait_ge(sem("z_full"), done)
                        with act.Fori(0, NT // 2) as i:
                            for u in range(2):
                                act.wait_ge(sem("y_full"), NT * (8 * L + n) + 2 * i + u + 1)
                                act.activation(row(y_hi, 2 * i + u, 0, Oc), ps[:TP, u, 0:Oc], ACT.Copy
                                               ).then_inc(sem("y_high"), 1)

            act.wait_ge(sem("h0_ready"), 1)
            act.dma_start(bias_b[:TP, 0:896], row_bias("b1")).then_inc(sem("bias_in"), 16)
            transposed("t0", 7, ACT.Copy)
            relational(0)
            for L in (1, 2):
                act.wait_ge(sem("z_free"), 2 + 6 * NT * L)
                act.wait_ge(sem("y_free"), 2 + 8 * NT * L)
                act.dma_start(bias_b[:TP, 0:D], row_bias(f"b{L + 1}")).then_inc(sem("bias_in"), 16)
                transposed(f"t{L}", LAYERS[L][0], ACT.Relu)
                relational(L)

            def read_again(tag, src):
                for m in range(NT):
                    if m >= 2:
                        act.wait_ge(sem(f"{tag}_sum"), m - 1)
                    act.dma_start(again[:TP, m % 2, :], src[m * TP:(m + 1) * TP, :]).then_inc(sem(f"{tag}_in{m % 2}"), 16)

            act.wait_ge(sem("z_free"), 2 + 18 * NT)
            read_again("res", a["x"])

            def split_high(tag, x, done=None):
                h1, h2 = whi[:, x % 2, 0:KD * HID], w2_hi[:, x % 2, :]
                act.wait_ge(sem("w1_in"), 16 * (block_of(tag) + x + 1))
                if done is not None:
                    act.wait_ge(sem(f"{tag}_o_full"), done)
                act.activation(h1, wraw[:, 0:KD * HID], ACT.Copy).then_inc(sem("w1_high"), 1)
                act.wait_ge(sem("w2_in"), 16 * (block_of(tag) + x + 1))
                act.activation(h2, w2_raw[:, :], ACT.Copy).then_inc(sem("w2_high"), 1)

            def tokens_high(tag, t):
                act.wait_ge(sem(f"{tag}_turned"), t + 1)
                act.activation(gt_hi[:, :, :].rearrange("p k n -> p (k n)"),
                               ps[:, 0:2, :].rearrange("p a b -> p (a b)")[:, 0:D], ACT.Copy
                               ).then_inc(sem(f"{tag}_tokens_high"), 1)

            def experts(tag):
                act.wait_ge(sem(f"{tag}_records_out"), 16 * NT * PICKS[tag])
                act.dma_start(table[:, 0:TABLE_COLS[tag], :], table_dram[tag].rearrange("(p t) f -> p t f", p=128)
                              ).then_inc(sem(f"{tag}_table_in"), 16)
                tokens_high(tag, 0)
                act.wait_ge(sem(f"{tag}_table"), 1)
                for x in range(EXPERTS):
                    lo = act.value_load(expert_start_i[0:1, x:x + 1], min_val=0, max_val=SLOT_TILES[tag])
                    hi = act.value_load(expert_start_i[0:1, x + 1:x + 2], min_val=1, max_val=SLOT_TILES[tag])
                    if x + 1 < EXPERTS and x:
                        split_high(tag, x + 1, 2 * lo)
                    with act.Fori(lo, hi) as t:
                        for hc in range(KH):
                            act.wait_ge(sem(f"{tag}_h_full"), KH * t + hc + 1)
                            p = ps[:, 6 + hc % 2, 0:128]
                            if tag == "m0":
                                act.activation(ht_hi[:, hc, :], p, ACT.Relu).then_inc(sem("m0_h_high"), 1)
                            else:
                                b = b1_cols[:, x * KH + hc:x * KH + hc + 1]
                                act.activation(gelu32[:, hc, :], p, ACT.Gelu, bias=b)
                                act.activation(ht_hi[:, hc, :], p, ACT.Gelu, bias=b).then_inc(sem("m1_h_high"), 1)
                        tokens_high(tag, t + 1)
                        act.wait_ge(sem(f"{tag}_o_full"), 2 * t + 1)
                        act.wait_ge(sem(f"{tag}_out_free"), t + 1)
                        act.activation(row(out_ring, t % 2, 0, 384, 128), ps[:, 4, 0:384], ACT.Copy,
                                       scale=slot_gate[:, bass.ds(t, 1)]).then_inc(sem(f"{tag}_o_left"), 1)
                act.wait_ge(sem(f"{tag}_o_left"), hi + 1)
                act.nop().then_inc(sem(f"{tag}_o_left"), SLOT_TILES[tag])
                act.wait_ge(sem(f"{tag}_scattered"), 16 * SLOT_TILES[tag])
                for h in range(2):
                    for c, back in enumerate((first_back, second_back)[:PICKS[tag]]):
                        act.dma_start(back[:TP, 5 * h:5 * h + 5, :],
                                      moe_dram[tag][c * N + 5 * h * TP:c * N + (5 * h + 5) * TP, :]
                                      .rearrange("(t p) d -> p t d", p=TP)).then_inc(sem(f"{tag}_back{h}"), 16)

            act.wait_ge(sem("adj_first"), NT)
            transposed("n1", KD, ACT.Copy, "m0")
            for g in (first_part - 2, first_part - 1):
                act.wait_ge(sem(pieces[g][3]), pieces[g][4])
            split_high("m0", 0)
            split_high("m0", 1)
            act.wait_ge(sem("soft_in"), 1)
            act.activation(soft[:TP, :, :], logit[:TP, :, :], ACT.Exp).then_inc(sem("soft_exp"), 1)
            experts("m0")
            transposed("n2", KD, ACT.Copy)
            act.wait_ge(sem("t_high"), turned_before("n2") + 2 * NT)
            act.dma_start(bias_b[:TP, 0:D], row_bias("gcn_b")).then_inc(sem("bias_in"), 16)
            for c in range(2):
                if c:
                    act.wait_ge(sem("gz_full"), NT)
                with act.Fori(0, NT // 2) as i:
                    for u in range(2):
                        m = 2 * i + u
                        act.wait_ge(sem("gy_full"), NT * c + m + 1)
                        act.activation(row(y_hi, m, 0, 384), ps[:TP, u, 0:384], ACT.Copy,
                                       scale=dinv[:TP, bass.ds(m, 1)]).then_inc(sem("gy_high"), 1)
            act.wait_ge(sem("gz_free"), 2 + 2 * NT)
            act.dma_start(x3_dram.rearrange("(t p) d -> p t d", p=TP), acc[:TP, :, 0:D]).then_inc(sem("x3_out"), 16)
            act.dma_start(bias_b[:TP, 0:D], row_bias("v_b")).then_inc(sem("bias_in"), 16)
            act.dma_start(ln_w[:TP, :], row_bias("n1_w")).then_inc(sem("affine_in"), 16)
            act.dma_start(ln_b[:TP, :], row_bias("n1_b")).then_inc(sem("affine_in"), 16)
            transposed("n4", KD, ACT.Copy)
            for c in range(2):
                with act.Fori(0, NT // 2) as i:
                    for u in range(2):
                        m = 2 * i + u
                        act.wait_ge(sem("v_biased"), NT * c + m + 1)
                        act.activation(v_parts[:TP, bass.ds(m, 1), 6 * c:6 * c + 6, 0:HD].rearrange("p o h d -> p (o h) d"),
                                       p32_flat[:TP, 384 * u:384 * (u + 1)].rearrange("p (h d) -> p h d", d=HD),
                                       ACT.Copy).then_inc(sem("v_high"), 1)
            job = 0
            act.nop().then_inc(sem("exp_done"), 5)
            for j in range(HEADS // 2):
                for which in range(2):
                    for c0, w in NODE_COLS:
                        job += 1
                        act.wait_ge(sem("qk_full"), job)
                        if job > 1:
                            act.wait_ge(sem("qk_parts"), job - 1)
                        for hh in range(2):
                            P0 = slice(64 * hh, 64 * hh + 64)
                            p, b = ps[P0, (job - 1) % 2, 0:w], qk_bias[P0, 6 * which + j:6 * which + j + 1]
                            act.activation((q_a, k_a)[which][0:64, hh, c0:c0 + w], p, ACT.Identity, bias=b)
                            act.activation(qk32[0:64, hh, 0:w], p, ACT.Identity, bias=b).then_inc(sem("qk_moved"), 1)
                for h2 in range(2):
                    act.wait_ge(sem("max_rows"), 2 * j + h2 + 1)
                    act.activation(q_b[64:65, h2, 0:1000].rearrange("p (a b) -> p a b", b=500),
                                   ps[64:65, 3 * h2:3 * h2 + 2, 0:500], ACT.Copy, scale=-1.0)
                    act.activation(q_b[64:65, h2, 1000:N], ps[64:65, 3 * h2 + 2, 0:250], ACT.Copy,
                                   scale=-1.0).then_inc(sem("max_set"), 1)
                with act.Fori(0, NT // 2) as qc:
                    for h2 in range(2):
                        n = 10 * j + 2 * qc + h2
                        act.wait_ge(sem("pv_full"), 2 * n + 2)
                        for kp in range(5):
                            p = ps[:TP, kp, 0:2 * QC]
                            act.wait_ge(sem("s_full"), 5 * n + kp + 1)
                            act.activation(p_hi[:TP, h2, 2 * kp:2 * kp + 2, 0:QC], p.rearrange("p (a b) -> p a b", b=QC),
                                           ACT.Exp, scale=HD ** -0.5).then_inc(sem("p_high"), 1)
                            act.wait_ge(sem("p_low"), 5 * n + kp + 1)
                            act.activation(p32[:TP, (5 * h2 + kp) % 2, :], p,
                                           ACT.Exp, scale=HD ** -0.5).then_inc(sem("exp_done"), 1)
                for t, (c0, w) in enumerate(((0, 500), (500, 500), (1000, 250))):
                    act.wait_ge(sem("ot_full"), 3 * j + t + 1)
                    if j:
                        act.wait_ge(sem("pr_full"), 2 * NT * j)
                    act.activation(ot_hi[:, c0:c0 + w], ps[:, t, 0:w], ACT.Copy).then_inc(sem("ot_high"), 1)
            act.wait_ge(sem("pr_free"), 4 + 2 * NT * 6)
            act.dma_start(bias_b[:TP, 0:D], row_bias("proj_b")).then_inc(sem("bias_in"), 16)
            act.dma_start(ln_w[:TP, :], row_bias("n2_w")).then_inc(sem("affine_in"), 16)
            act.dma_start(ln_b[:TP, :], row_bias("n2_b")).then_inc(sem("affine_in"), 16)
            act.dma_start(router32[:, :, :], a["w_gate"].rearrange("(k p) n -> p k n", p=128)).then_inc(sem("gate_in"), 16)
            transposed("n5", KD, ACT.Copy, "m1")
            split_high("m1", 0)
            split_high("m1", 1)
            act.wait_ge(sem("soft_in"), 2)
            act.activation(share[:TP, 1, :], share[:TP, 0, :], ACT.Exp).then_inc(sem("soft_exp"), 1)
            act.dma_start(b2_rows[:, :], a["b2x"]).then_inc(sem("b2_in"), 16)
            for q in range(3):
                act.wait_ge(sem("gt_full"), q + 1)
                w = 500 if q < 2 else 250
                act.activation(gate_t[:, 500 * q:500 * q + w], ps[0:EXPERTS, 4 + q, 0:w], ACT.Copy).then_inc(sem("gt_done"), 1)
            read_again("last", x3_dram)
            experts("m1")
            for h in range(2):
                act.wait_ge(sem("m1_added"), h + 1)
                act.dma_start(out[5 * h * TP:(5 * h + 5) * TP, :].rearrange("(t p) d -> p t d", p=TP),
                              acc[:TP, 5 * h:5 * h + 5, 0:D]).then_inc(sem("stored"), 16)
            act.wait_ge(sem("stored"), 32)

        @block.vector
        def _(dve):
            count = [0]

            def then(ins):
                count[0] += 1
                ins.then_inc(sem("dve_step"), 1)
                dve.wait_ge(sem("dve_step"), count[0])

            def signal(ins, name, value):
                ins.then_inc(sem(name), 1)
                dve.wait_ge(sem(name), value)

            def bcast(col, n):
                return col.to_broadcast([TP, NT, n])

            dve.memset(zeros[:, :], 0.0)
            dve.memset(ones16[:, :], 1.0)
            dve.memset(slot[:EP, :], 0.0)
            dve.wait_ge(sem("iota_ready"), 4)
            for c in range(1, 3):
                dve.tensor_scalar(pidx[:, c:c + 1], pidx[:, 0:1], float(128 * c), None, ALU.add)
            then(dve.tensor_scalar(ident[:, :], iota_n[:, :128], pidx[:, 0:1], None, ALU.is_equal))
            dve.memset(one_of[:, :], 1.0)
            dve.tensor_scalar(ident16[:, :], iota_n[:, :128], pidx[:, 0:1], None, ALU.is_equal)
            dve.tensor_scalar(before[:, :], iota_n[:, :128], pidx[:, 0:1], None, ALU.is_gt)
            dve.tensor_scalar(below[:, 0, :128], iota_n[:, :128], pidx[:, 0:1], None, ALU.is_gt)
            for c in range(3):
                dve.tensor_scalar(below[:, 1 + c, :], iota_n[:, :EJ], pidx[:, c:c + 1], None, ALU.is_gt)
            dve.wait_ge(sem("edges_in"), 48)
            then(dve.tensor_scalar(src_tile[:EP, :], e_src[:EP, :], float(TP), None, ALU.is_ge))
            for k in range(2, NT):
                then(dve.scalar_tensor_tensor(src_tile[:EP, :], e_src[:EP, :], float(TP * k), src_tile[:EP, :],
                                              ALU.is_ge, ALU.add))
            dve.scalar_tensor_tensor(bucket[:EP, :], e_typ[:EP, :], float(NT), src_tile[:EP, :], ALU.mult, ALU.add)
            then(dve.scalar_tensor_tensor(src_loc[:EP, :], src_tile[:EP, :], float(-TP), e_src[:EP, :], ALU.mult, ALU.add))
            then(dve.scalar_tensor_tensor(packed_f[:EP, :], e_dst[:EP, :], 128.0, src_loc[:EP, :], ALU.mult, ALU.add))
            dve.tensor_copy(packed[:EP, :], packed_f[:EP, :])
            for b in range(NBUCKET):
                ins = dve.tensor_scalar(mask[:EP, b, :], bucket[:EP, :], float(b), None, ALU.is_equal)
            then(ins)
            then(dve.tensor_reduce(tiles_f[:EP, :], mask[:EP, :, :], AX_X, ALU.add))
            signal(dve.tensor_copy(row_cnt[:EP, :], tiles_f[:EP, :]), "row_counts", 1)
            dve.wait_ge(sem("col_counts"), 1)
            dve.tensor_copy(col_cnt[:, :2, :], ps[:, 0, 0:2 * NBUCKET].rearrange("p (c b) -> p c b", c=2))
            dve.tensor_copy(col_cnt[:64, 2, :], ps[:64, 0, 2 * NBUCKET:3 * NBUCKET])
            signal(dve.tensor_scalar(tiles_f[:, :], ps[:, 1, 0:NBUCKET], 128.0 * UNIT - 1, None, ALU.add), "col_counts_in", 1)
            then(dve.tensor_copy(tiles_i[:, :], tiles_f[:, :]))
            then(dve.tensor_scalar(tiles_i[:, :], tiles_i[:, :], 8, None, ALU.arith_shift_right))
            dve.tensor_scalar(tiles_f[:, :], tiles_i[:, :], 1.0, None, ALU.max)
            then(dve.memset(tstart[:, 0:1], 0.0))
            for b in range(NBUCKET):
                then(dve.tensor_tensor(tstart[:, b + 1:b + 2], tstart[:, b:b + 1], tiles_f[:, b:b + 1], ALU.add))
            dve.tensor_copy(tstart_i[:, :], tstart[:, :]).then_inc(sem("starts_ready"), 1)
            then(dve.tensor_scalar(first_slot[:, :], tstart[:, :NBUCKET], 128.0 * UNIT, None, ALU.mult))
            for b in range(NBUCKET):
                dve.wait_ge(sem("ranks"), b + 1)
                then(dve.scalar_tensor_tensor(slot_part[:EP, b % 2, :], ps[:EP, 2 + b % 4, :EJ], first_slot[:EP, b:b + 1],
                                              mask[:EP, b, :], ALU.add, ALU.mult))
                signal(dve.tensor_tensor(slot[:EP, :], slot[:EP, :], slot_part[:EP, b % 2, :], ALU.add), "rank_used", b + 1)
            then(dve.tensor_copy(slot_i[:EP, :], slot[:EP, :]))
            dve.tensor_scalar(tile_i[:EP, :], slot_i[:EP, :], 7, None, ALU.arith_shift_right)
            then(dve.tensor_scalar(lane_i[:EP, :], slot_i[:EP, :], 127, None, ALU.bitwise_and))
            then(dve.tensor_scalar(lane_f[:EP, :], lane_i[:EP, :], float(ETILES), None, ALU.mult))
            then(dve.tensor_tensor(addr_f[:EP, :], lane_f[:EP, :], tile_i[:EP, :], ALU.add))
            dve.tensor_copy(addr[:EP, :], addr_f[:EP, :]).then_inc(sem("addr_ready"), 1)
            dve.wait_ge(sem("sorted_in"), 16)
            dve.tensor_scalar(sorted_i[:, 0, :], sorted_p[:, :], 7, None, ALU.arith_shift_right)
            then(dve.tensor_scalar(sorted_i[:, 1, :], sorted_p[:, :], 127, None, ALU.bitwise_and))
            then(dve.tensor_copy(sorted_f[:, :, :], sorted_i[:, :, :]))
            with dve.Fori(0, NBUCKET) as b:
                lo = dve.value_load(tstart_i[0:1, bass.ds(b, 1)], min_val=0, max_val=UNITS - 1)
                hi = dve.value_load(tstart_i[0:1, bass.ds(b + 1, 1)], min_val=1, max_val=UNITS)
                with dve.Fori(lo, hi) as t:
                    ring = UNIT * (t % (RING // UNIT))
                    for u in range(UNIT):
                        dve.wait_ge(sem("onehot_free"), UNIT * t + u + 1)
                        dve.tensor_scalar(row(oh_src, ring + u, 0, TP, 128), iota_n[:, :TP],
                                          sorted_f[:, 1, bass.ds(UNIT * t + u, 1)], None, ALU.is_equal)
                        dve.tensor_scalar(row(oh_dst, ring + u, 0, N, 128), iota_n[:, :],
                                          sorted_f[:, 0, bass.ds(UNIT * t + u, 1)], None, ALU.is_equal
                                          ).then_inc(sem("onehot_ready"), 1)

            dve.wait_ge(sem("adj_full"), NBUCKET)
            dve.memset(adj_all[:, NBUCKET * N:], 0.0)
            then(dve.memset(ones_col[:, :], 1.0))
            dve.nop().then_inc(sem("ones_ready"), 1)
            dve.wait_ge(sem("counts"), 1)
            cnt = ps[:TP, 7, 0:NBUCKET].rearrange("p (m r) -> p m r", r=NREL)
            then(dve.tensor_scalar(inv_cnt[:TP, :, :], cnt, 1.0, None, ALU.max))
            then(dve.reciprocal(inv_cnt[:TP, :, :], inv_cnt[:TP, :, :]))
            then(dve.scalar_tensor_tensor(inv_cnt[:TP, :, :], cnt, 1.0, inv_cnt[:TP, :, :], ALU.min, ALU.mult))
            then(dve.tensor_reduce(dinv[:TP, :], cnt, AX_X, ALU.add))
            dve.tensor_scalar(dinv[:TP, :], dinv[:TP, :], 1.0, None, ALU.add).then_inc(sem("variance"), 1)

            def normalize_stats(tag):
                for m in range(NT):
                    for h in range(2):
                        ins = dve.bn_stats(stats[:TP, m, h, :], acc[:TP, m, 384 * h:384 * (h + 1)])
                then(ins)
                for m in range(NT):
                    ins = dve.bn_aggr(meanvar[:TP, m, :], stats[:TP, m, :, :])
                then(ins)
                dve.tensor_scalar(rstd[:TP, :], meanvar[:TP, :, 1:2].rearrange("p m o -> p (m o)"), 1e-5, None, ALU.add
                                  ).then_inc(sem("variance"), 1)
                dve.wait_ge(sem("rstd_ready"), 1 + powers(tag))

            def normalized(dst, m):
                return dve.tensor_scalar(dst, acc[:TP, m, 0:D], meanvar[:TP, m, 0:1], rstd[:TP, m:m + 1],
                                         ALU.subtract, ALU.mult)

            def low_parts(tag, m, K, relu):
                for q, (k0, k1) in enumerate(((0, 4), (4, K))):
                    job = 2 * m + q
                    dve.wait_ge(sem("t_high"), turned_before(tag) + job + 1)
                    p = ps[:, 4 + job % 4, 0:(k1 - k0) * TP].rearrange("p (k n) -> p k n", n=TP)
                    hi = hT_hi[:, k0:k1, m * TP:(m + 1) * TP]
                    lo = hT_lo[:, k0:k1, m * TP:(m + 1) * TP]
                    if relu:
                        ins = dve.scalar_tensor_tensor(lo, p, 0.0, hi, ALU.max, ALU.subtract)
                    else:
                        ins = dve.tensor_tensor(lo, p, hi, ALU.subtract)
                    ins.then_inc(sem("t_free"), 1)

            def normalized_transposed(tag, affine=False, pack=None):
                normalize_stats(tag)
                if affine:
                    dve.wait_ge(sem("affine_in"), 32 if tag == "n4" else 64)
                for m in range(NT + 1):
                    if m < NT:
                        if m >= 2:
                            dve.wait_ge(sem("t_full"), turned_before(tag) + 2 * (m - 1))
                        if m >= 2 and pack:
                            dve.wait_ge(sem("pack_low"), NT * nth(pack) - NT + m - 1)
                        s = stage[:TP, m % 2, :]
                        ins = normalized(s, m)
                        if affine:
                            then(ins)
                            then(dve.tensor_tensor(s, s, ln_w[:TP, :], ALU.mult))
                            ins = dve.tensor_tensor(s, s, ln_b[:TP, :], ALU.add)
                        ins.then_inc(sem("staged"), 1)
                    if m and pack:
                        i = m - 1
                        dve.wait_ge(sem("staged"), staged_before(tag) + i + 1)
                        dve.wait_ge(sem("pack_high"), NT * nth(pack) - NT + i + 1)
                        dve.tensor_tensor(packed_rows[:TP, i % 3, 1, :], stage[:TP, i % 2, :], packed_rows[:TP, i % 3, 0, :],
                                          ALU.subtract).then_inc(sem(f"pack_low"), 1)
                    if m:
                        low_parts(tag, m - 1, KD, False)

            dve.wait_ge(sem("x_in"), 64)
            dve.wait_ge(sem("consts_in"), 64)
            normalize_stats("n0")
            for m in range(NT):
                normalized(acc[:TP, m, 0:D], m)
            then(dve.tensor_copy(type_f[:TP, :], node_type[:TP, :]))
            for t in range(3):
                then(dve.tensor_scalar(share[:TP, t, :], type_f[:TP, :], float(t), None, ALU.is_equal))
            for m in range(NT):
                e = acc[:TP, m, D:896]
                then(dve.tensor_scalar(e, bias_b[:TP, 0:128], share[:TP, 0, m:m + 1], None, ALU.mult))
                for t in (1, 2):
                    then(dve.scalar_tensor_tensor(e, bias_b[:TP, 128 * t:128 * (t + 1)], share[:TP, t, m:m + 1], e,
                                                  ALU.mult, ALU.add))
            dve.nop().then_inc(sem("h0_ready"), 1)
            for m in range(NT):
                low_parts("t0", m, 7, False)

            def relational(L):
                K, O, nm = LAYERS[L]
                Oc = O // 2
                dve.wait_ge(sem("bias_in"), 16 * (L + 1))
                for n, (_, c, r, g) in enumerate(s for s in steps if s[0] == L):
                    c0, c1 = c * Oc, (c + 1) * Oc
                    with dve.Fori(0, NT // 2) as i:
                        for u in range(2):
                            m = 2 * i + u
                            if r is None:
                                dve.wait_ge(sem("y_full"), NT * (8 * L + n) + m + 1)
                                dve.tensor_tensor(row(acc, m, c0, c1), ps[:TP, u, 0:Oc], bias_b[:TP, c0:c1], ALU.add
                                                  ).then_inc(sem("y_free"), 1)
                            else:
                                dve.wait_ge(sem("y_high"), NT * (6 * L + 3 * c + r) + m + 1)
                                dve.tensor_tensor(row(y_lo, m, 0, Oc), ps[:TP, u, 0:Oc], row(y_hi, m, 0, Oc), ALU.subtract
                                                  ).then_inc(sem("y_free"), 1)
                    if r is not None:
                        z = 3 * c + r
                        dve.wait_ge(sem("y_free"), 2 + NT * (8 * L + n + 1))
                        dve.wait_ge(sem("z_free"), 2 + NT * (6 * L + z))
                        with dve.Fori(0, NT // 2) as i:
                            for u in range(2):
                                m = 2 * i + u
                                dve.wait_ge(sem("z_full"), NT * (6 * L + z) + m + 1)
                                dve.scalar_tensor_tensor(row(acc, m, c0, c1), ps[:TP, 2 + u, 0:Oc],
                                                         row(inv_cnt, m, r, r + 1), row(acc, m, c0, c1),
                                                         ALU.mult, ALU.add).then_inc(sem("z_free"), 1)
                dve.wait_ge(sem("z_free"), 2 + 6 * NT * (L + 1))

            dve.nop().then_inc(sem("y_free"), 2)
            dve.nop().then_inc(sem("z_free"), 2)
            relational(0)
            for L in (1, 2):
                for m in range(NT):
                    low_parts(f"t{L}", m, LAYERS[L][0], True)
                relational(L)
            for m in range(NT):
                dve.wait_ge(sem(f"res_in{m % 2}"), 16 * (m // 2 + 1))
                dve.scalar_tensor_tensor(acc[:TP, m, 0:D], acc[:TP, m, 0:D], 0.0, again[:TP, m % 2, :], ALU.max, ALU.add
                                         ).then_inc(sem("res_sum"), 1)
            dve.wait_ge(sem("res_sum"), NT)

            def logits_in(tag):
                dve.wait_ge(sem("logits"), NT * nth(tag))
                then(dve.tensor_copy(logit[:TP, :, :], ps[:TP, 3, 0:NT * EXPERTS].rearrange("p (m e) -> p m e", e=EXPERTS)))
                for m in range(NT):
                    ins = dve.max(top_val[:TP, m, :], logit[:TP, m, :])
                then(ins)
                for m in range(NT):
                    ins = dve.max_index(top_idx[:TP, m, :], top_val[:TP, m, :], logit[:TP, m, :])
                then(ins)
                then(dve.tensor_copy(top_idx_f[:TP, :, :], top_idx[:TP, :, :]))

            def router_parts(tag, name, value):
                dve.wait_ge(sem(name), value)
                for t in (hT_hi, hT_lo):
                    dve.memset(t[:, KD, 0:4], 0.0)
                then(dve.tensor_copy(router_hi[:, :, :], router32[:, :, :]))
                dve.tensor_tensor(router_lo[:, :, :], router32[:, :, :], router_hi[:, :, :], ALU.subtract
                                  ).then_inc(sem("router"), 1)

            def slots(tag):
                picks = PICKS[tag]
                for c in range(picks):
                    for m in range(NT):
                        ins = dve.tensor_scalar(chosen[:TP, c, m, :], eye8[:TP, :], top_idx_f[:TP, m, c:c + 1], None,
                                                ALU.is_equal)
                then(ins)
                if picks == 1:
                    signal(dve.tensor_copy(chosen16[:TP, :, :], chosen[:TP, 0, :, :]), "chosen", nth(tag))
                else:
                    signal(dve.tensor_tensor(chosen16[:TP, :, :], chosen[:TP, 0, :, :], chosen[:TP, 1, :, :], ALU.add),
                           "chosen", nth(tag))
                dve.wait_ge(sem("ranked"), nth(tag))
                then(dve.tensor_scalar(expert_tiles_f[:, :], ps[:, 3, 0:EXPERTS], 127.0, None, ALU.add))
                then(dve.tensor_copy(expert_tiles_i[:, :], expert_tiles_f[:, :]))
                then(dve.tensor_scalar(expert_tiles_i[:, :], expert_tiles_i[:, :], 7, None, ALU.arith_shift_right))
                dve.tensor_scalar(expert_tiles_f[:, :], expert_tiles_i[:, :], 1.0, None, ALU.max)
                then(dve.memset(expert_start[:, 0:1], 0.0))
                for x in range(EXPERTS):
                    then(dve.tensor_tensor(expert_start[:, x + 1:x + 2], expert_start[:, x:x + 1],
                                           expert_tiles_f[:, x:x + 1], ALU.add))
                dve.tensor_copy(expert_start_i[:, :], expert_start[:, :])
                then(dve.tensor_scalar(expert_slot0[:, :], expert_start[:, 0:EXPERTS], 128.0, None, ALU.mult))
                for m in range(NT):
                    ins = dve.tensor_tensor(expert_slot[:TP, m, :], ps[:TP, 2, m * EXPERTS:(m + 1) * EXPERTS],
                                            expert_slot0[:TP, :], ALU.add)
                then(ins)
                for c in range(picks):
                    then(dve.tensor_tensor(picked_slot[:TP, :, :], chosen[:TP, c, :, :], expert_slot[:TP, :, :], ALU.mult))
                    then(dve.tensor_reduce(token_slot[:TP, c, :], picked_slot[:TP, :, :], AX_X, ALU.add))
                    s, tile, lane = (token_slot_i[:TP, i, c, :] for i in range(3))
                    then(dve.tensor_copy(s, token_slot[:TP, c, :]))
                    dve.tensor_scalar(tile, s, 7, None, ALU.arith_shift_right)
                    then(dve.tensor_scalar(lane, s, 127, None, ALU.bitwise_and))
                    then(dve.tensor_copy(token_addr_f[:TP, c, :], lane))
                    then(dve.scalar_tensor_tensor(token_addr_f[:TP, c, :], token_addr_f[:TP, c, :], float(TABLE_COLS[tag]),
                                                  tile, ALU.mult, ALU.add))
                    dve.tensor_copy(token_addr[:TP, c, :], token_addr_f[:TP, c, :])
                    col = lambda f: records[:TP, c, :, f:f + 1].rearrange("p m o -> p (m o)")
                    dve.tensor_copy(col(0), token[:TP, :])
                    dve.tensor_scalar(col(1), token[:TP, :], float(c * N), None, ALU.add)
                    dve.tensor_copy(col(2), share[:TP, 0 if tag == "m0" else 2 + c, :])
                    ins = dve.memset(records[:TP, c, :, 3:4], 0.0)
                then(ins)
                dve.nop().then_inc(sem("records"), 1)

            def split_low(tag, x):
                for name, raw, hi, lo in (("w1", wraw[:, 0:KD * HID], whi[:, x % 2, 0:KD * HID], wlo[:, x % 2, 0:KD * HID]),
                                          ("w2", w2_raw[:, :], w2_hi[:, x % 2, :], w2_lo[:, x % 2, :])):
                    dve.wait_ge(sem(f"{name}_high"), block_of(tag) + x + 1)
                    dve.tensor_tensor(lo, raw, hi, ALU.subtract).then_inc(sem(f"{name}_split"), 1)

            def tokens_low(tag, t):
                dve.wait_ge(sem(f"{tag}_turned"), t + 1)
                dve.tensor_copy(gt_lo[:, :, :].rearrange("p k n -> p (k n)"),
                                ps[:, 2:4, :].rearrange("p a b -> p (a b)")[:, 0:D]
                                ).then_inc(sem(f"{tag}_tokens_low"), 1)

            def experts(tag):
                dve.wait_ge(sem(f"{tag}_table_in"), 16)
                col = lambda f: table[:, 0:TABLE_COLS[tag], f:f + 1].rearrange("p t o -> p (t o)")
                for t, f in ((gather_row, 0), (scatter_row, 1), (slot_gate, 2)):
                    ins = dve.tensor_copy(t[:, 0:TABLE_COLS[tag]], col(f))
                then(ins)
                dve.nop().then_inc(sem(f"{tag}_table"), 1)
                dve.nop().then_inc(sem(f"{tag}_o_left"), 1)
                dve.nop().then_inc(sem(f"{tag}_o_right"), 1)
                tokens_low(tag, 0)
                for x in range(EXPERTS):
                    if x + 1 < EXPERTS and x:
                        split_low(tag, x + 1)
                    lo = dve.value_load(expert_start_i[0:1, x:x + 1], min_val=0, max_val=SLOT_TILES[tag])
                    hi = dve.value_load(expert_start_i[0:1, x + 1:x + 2], min_val=1, max_val=SLOT_TILES[tag])
                    with dve.Fori(lo, hi) as t:
                        for hc in range(KH):
                            dve.wait_ge(sem(f"{tag}_h_high"), KH * t + hc + 1)
                            h = ht_hi[:, hc, :]
                            if tag == "m0":
                                ins = dve.scalar_tensor_tensor(ht_lo[:, hc, :], ps[:, 6 + hc % 2, 0:128], 0.0, h,
                                                               ALU.max, ALU.subtract)
                            else:
                                ins = dve.tensor_tensor(ht_lo[:, hc, :], gelu32[:, hc, :], h, ALU.subtract)
                            ins.then_inc(sem(f"{tag}_h_low"), 1)
                        tokens_low(tag, t + 1)
                        dve.wait_ge(sem(f"{tag}_o_full"), 2 * t + 2)
                        dve.wait_ge(sem(f"{tag}_out_free"), t + 1)
                        dve.tensor_scalar(row(out_ring, t % 2, 384, D, 128), ps[:, 5, 0:384], slot_gate[:, bass.ds(t, 1)],
                                          None, ALU.mult).then_inc(sem(f"{tag}_o_right"), 1)
                dve.wait_ge(sem(f"{tag}_o_right"), hi + 1)
                dve.nop().then_inc(sem(f"{tag}_o_right"), SLOT_TILES[tag])
                for h in range(2):
                    dve.wait_ge(sem(f"{tag}_back{h}"), 16 * PICKS[tag])
                    for c, back in enumerate((first_back, second_back)[:PICKS[tag]]):
                        if c:
                            then(ins)
                        av = acc[:TP, 5 * h:5 * h + 5, 0:D]
                        ins = dve.tensor_tensor(av, av, back[:TP, 5 * h:5 * h + 5, :], ALU.add)
                    signal(ins, f"{tag}_added", h + 1)

            dve.wait_ge(sem("adj_first"), NT)
            normalized_transposed("n1", pack="m0")
            router_parts("m0", "consts_in", 64)
            split_low("m0", 0)
            split_low("m0", 1)
            logits_in("m0")
            dve.tensor_tensor(logit[:TP, :, :], logit[:TP, :, :], top_val[:TP, :, 0:1].to_broadcast([TP, NT, EXPERTS]),
                              ALU.subtract).then_inc(sem("soft_in"), 1)
            dve.wait_ge(sem("soft_exp"), 1)
            then(dve.tensor_reduce(share[:TP, 0, :], soft[:TP, :, :], AX_X, ALU.add))
            then(dve.reciprocal(share[:TP, 0, :], share[:TP, 0, :]))
            slots("m0")
            experts("m0")

            normalized_transposed("n2")
            dve.wait_ge(sem("bias_in"), 16 * 4)
            for m in range(NT):
                ins = dve.tensor_tensor(acc[:TP, m, 0:D], acc[:TP, m, 0:D], bias_b[:TP, 0:D], ALU.add)
            then(ins)
            dve.nop().then_inc(sem("gy_free"), 2)
            dve.nop().then_inc(sem("gz_free"), 2)
            for c in range(2):
                c0, c1 = 384 * c, 384 * (c + 1)
                with dve.Fori(0, NT // 2) as i:
                    for u in range(2):
                        m = 2 * i + u
                        dve.wait_ge(sem("gy_high"), NT * c + m + 1)
                        dve.scalar_tensor_tensor(row(y_lo, m, 0, 384), ps[:TP, u, 0:384], dinv[:TP, bass.ds(m, 1)],
                                                 row(y_hi, m, 0, 384), ALU.mult, ALU.subtract).then_inc(sem("gy_free"), 1)
                with dve.Fori(0, NT // 2) as i:
                    for u in range(2):
                        m = 2 * i + u
                        dve.wait_ge(sem("gz_full"), NT * c + m + 1)
                        dve.scalar_tensor_tensor(row(acc, m, c0, c1), ps[:TP, 2 + u, 0:384], dinv[:TP, bass.ds(m, 1)],
                                                 row(acc, m, c0, c1), ALU.mult, ALU.add).then_inc(sem("gz_free"), 1)
            dve.wait_ge(sem("gz_free"), 2 + 2 * NT)

            normalize_stats("n3")
            dve.wait_ge(sem("x3_out"), 16)
            for m in range(NT):
                ins = normalized(acc[:TP, m, 0:D], m)
            then(ins)
            normalized_transposed("n4", affine=True)
            dve.wait_ge(sem("t_full"), turned_before("n4") + 2 * NT)
            dve.memset(v_parts[:TP, :, :, HD:HD + 1], 1.0)
            for t in (p_hi, p_lo):
                dve.memset(t[:TP, :, :, QC:QC + 6], 0.0)
            dve.memset(q_b[64:96, :, :], 0.0)
            then(dve.memset(k_b[64:96, :, :], 0.0))
            signal(dve.memset(k_b[64:65, :, :], 1.0), "ones_set", 1)
            dve.wait_ge(sem("bias_in"), 16 * 5)
            dve.nop().then_inc(sem("v_low"), 2)
            dve.nop().then_inc(sem("p_low"), 2)
            dve.nop().then_inc(sem("o_free"), 2)
            dve.nop().then_inc(sem("pr_free"), 4)
            dve.nop().then_inc(sem("max_free"), 2)
            for c in range(2):
                with dve.Fori(0, NT // 2) as i:
                    for u in range(2):
                        m = 2 * i + u
                        dve.wait_ge(sem("v_full"), NT * c + m + 1)
                        v32 = p32_flat[:TP, 384 * u:384 * (u + 1)]
                        dve.wait_ge(sem("v_low"), NT * c + m + 1)
                        dve.tensor_tensor(v32, ps[:TP, u, 0:384], bias_b[:TP, 384 * c:384 * (c + 1)], ALU.add
                                          ).then_inc(sem("v_biased"), 1)
                        dve.wait_ge(sem("v_high"), NT * c + m + 1)
                        vp = lambda lo, hi: v_parts[:TP, bass.ds(m, 1), 6 * c:6 * c + 6, lo:hi].rearrange("p o h d -> p (o h) d")
                        dve.tensor_tensor(vp(HD + 1, 129), v32.rearrange("p (h d) -> p h d", d=HD), vp(0, HD), ALU.subtract
                                          ).then_inc(sem("v_low"), 1)
            job = 0
            for j in range(HEADS // 2):
                for which in range(2):
                    for c0, w in NODE_COLS:
                        job += 1
                        dve.wait_ge(sem("qk_moved"), 2 * job)
                        hi = (q_a, k_a)[which]
                        lo = q_b[0:64, :, c0:c0 + w] if which == 0 else k_a[64:128, :, c0:c0 + w]
                        dup = q_a[64:128, :, c0:c0 + w] if which == 0 else k_b[0:64, :, c0:c0 + w]
                        dve.tensor_copy(dup, hi[0:64, :, c0:c0 + w])
                        dve.tensor_tensor(lo, qk32[0:64, :, 0:w], hi[0:64, :, c0:c0 + w], ALU.subtract
                                          ).then_inc(sem("qk_parts"), 1)
                for h2 in range(2):
                    with dve.Fori(0, NT // 2) as i:
                        for u in range(2):
                            t = 2 * i + u
                            dve.wait_ge(sem("max_full"), (2 * j + h2) * NT + t + 1)
                            dve.reduce_max(row_max[:TP, h2, bass.ds(t, 1)],
                                           ps[:TP, 3 * u:3 * u + 3, :].rearrange("p a b -> p (a b)")[:, :N], AX_X
                                           ).then_inc(sem("max_free"), 1)
                def p_low_parts(qc, h2):
                    n = 10 * j + 2 * qc + h2
                    for kp in range(5):
                        dve.wait_ge(sem("exp_done"), 5 * n + kp + 6)
                        dve.tensor_tensor(p_lo[:TP, h2, 2 * kp:2 * kp + 2, 0:QC],
                                          p32[:TP, (5 * h2 + kp) % 2, :].rearrange("p (a b) -> p a b", b=QC),
                                          p_hi[:TP, h2, 2 * kp:2 * kp + 2, 0:QC],
                                          ALU.subtract).then_inc(sem("p_low"), 1)

                def o_out(qc, h2):
                    n = 10 * j + 2 * qc + h2
                    for u in range(2):
                        dve.wait_ge(sem("pv_full"), 2 * n + u + 5)
                        dve.reciprocal(recip[:TP, u:u + 1], ps[:TP, 5 + u, HD:HD + 1]).then_inc(sem("o_recip"), 1)
                        dve.wait_ge(sem("o_recip"), 2 * n + u + 1)
                        dve.tensor_scalar(row(o_pair, 2 * qc + u, 64 * h2, 64 * h2 + 64), ps[:TP, 5 + u, 0:HD],
                                          recip[:TP, u:u + 1], None, ALU.mult).then_inc(sem("o_free"), 1)

                p_low_parts(0, 0)
                with dve.Fori(0, NT // 2 - 1) as qc:
                    p_low_parts(qc, 1)
                    o_out(qc, 0)
                    p_low_parts(qc + 1, 0)
                    o_out(qc, 1)
                p_low_parts(NT // 2 - 1, 1)
                o_out(NT // 2 - 1, 0)
                o_out(NT // 2 - 1, 1)
                for t, (c0, w) in enumerate(((0, 500), (500, 500), (1000, 250))):
                    dve.wait_ge(sem("ot_high"), 3 * j + t + 1)
                    dve.tensor_tensor(ot_lo[:, c0:c0 + w], ps[:, t, 0:w], ot_hi[:, c0:c0 + w], ALU.subtract
                                      ).then_inc(sem("ot_low"), 1)
                if j:
                    dve.wait_ge(sem("pr_free"), 4 + 2 * NT * j)
                with dve.Fori(0, NT // 2) as i:
                    for u in range(2):
                        m = 2 * i + u
                        for c in range(2):
                            q = 2 * NT * j + 2 * m + c
                            dve.wait_ge(sem("pr_full"), q + 1)
                            av = row(acc, m, 384 * c, 384 * (c + 1))
                            dve.tensor_tensor(av, ps[:TP, 3 + 2 * u + c, 0:384], av, ALU.add).then_inc(sem("pr_free"), 1)
            dve.wait_ge(sem("pr_free"), 4 + 2 * NT * 6)

            dve.wait_ge(sem("bias_in"), 16 * 6)
            for m in range(NT):
                ins = dve.tensor_tensor(acc[:TP, m, 0:D], acc[:TP, m, 0:D], bias_b[:TP, 0:D], ALU.add)
            then(ins)
            normalized_transposed("n5", affine=True, pack="m1")
            router_parts("m1", "gate_in", 16)
            split_low("m1", 0)
            split_low("m1", 1)
            logits_in("m1")
            dve.tensor_tensor(share[:TP, 0, :], top_val[:TP, :, 1:2].rearrange("p m o -> p (m o)"),
                              top_val[:TP, :, 0:1].rearrange("p m o -> p (m o)"), ALU.subtract).then_inc(sem("soft_in"), 1)
            dve.wait_ge(sem("soft_exp"), 2)
            then(dve.tensor_scalar(share[:TP, 2, :], share[:TP, 1, :], 1.0, None, ALU.add))
            then(dve.reciprocal(share[:TP, 2, :], share[:TP, 2, :]))
            then(dve.tensor_tensor(share[:TP, 3, :], share[:TP, 1, :], share[:TP, 2, :], ALU.mult))
            for m in range(NT):
                dve.tensor_scalar(gates[:TP, m, :], eye8[:TP, :], top_idx_f[:TP, m, 0:1], share[:TP, 2, m:m + 1],
                                  ALU.is_equal, ALU.mult)
                ins = dve.tensor_scalar(soft[:TP, m, :], eye8[:TP, :], top_idx_f[:TP, m, 1:2], share[:TP, 3, m:m + 1],
                                        ALU.is_equal, ALU.mult)
            then(ins)
            signal(dve.tensor_tensor(gates[:TP, :, :], gates[:TP, :, :], soft[:TP, :, :], ALU.add), "gates_ready", 1)
            slots("m1")
            for m in range(NT):
                for c in range(2):
                    dve.wait_ge(sem("gb_full"), 2 * m + c + 1)
                    av = acc[:TP, m, 384 * c:384 * (c + 1)]
                    ins = dve.tensor_tensor(av, ps[:TP, c + 4 * (m % 2), 0:384], av, ALU.add)
                    ins.then_inc(sem("gb_free"), 1)
            dve.wait_ge(sem("gb_free"), 2 * NT)
            for m in range(NT):
                dve.wait_ge(sem(f"last_in{m % 2}"), 16 * (m // 2 + 1))
                dve.tensor_tensor(acc[:TP, m, 0:D], acc[:TP, m, 0:D], again[:TP, m % 2, :], ALU.add
                                  ).then_inc(sem("last_sum"), 1)
            dve.wait_ge(sem("last_sum"), NT)
            experts("m1")

        @block.tensor
        def _(pe):
            pe.wait_ge(sem("row_counts"), 1)
            for c in range(3):
                w = min(128, EJ - 128 * c)
                for b in range(NBUCKET):
                    pe.matmul(ps[:w, 0, c * NBUCKET + b:c * NBUCKET + b + 1], mask[:EP, b, c * 128:c * 128 + w],
                              ones16[:EP, 0:1], start=True, stop=True)
            pe.matmul(ps[:, 1, 0:NBUCKET], ones16[:EP, :128], row_cnt[:EP, :], start=True, stop=True
                      ).then_inc(sem("col_counts"), 1)
            pe.wait_ge(sem("col_counts_in"), 1)
            for b in range(NBUCKET):
                if b >= 4:
                    pe.wait_ge(sem("rank_used"), b - 3)
                p = ps[:EP, 2 + b % 4, :EJ]
                pe.matmul(p, below[:EP, 0, :EP], mask[:EP, b, :], start=True, stop=False)
                for c in range(3):
                    w = min(128, EJ - 128 * c)
                    ins = pe.matmul(p, col_cnt[:w, c, b:b + 1].to_broadcast([w, EP]), below[:w, 1 + c, :],
                                    start=False, stop=(c == 2))
                ins.then_inc(sem("ranks"), 1)
            pe.nop().then_inc(sem("onehot_free"), RING)
            pe.wait_ge(sem("starts_ready"), 1)
            pe.wait_ge(sem("rank_used"), NBUCKET)
            with pe.Fori(0, NBUCKET // 2) as bh:
                for u in range(2):
                    b = 2 * bh + u
                    lo = pe.value_load(tstart_i[0:1, bass.ds(b, 1)], min_val=0, max_val=UNITS - 1)
                    hi = pe.value_load(tstart_i[0:1, bass.ds(b + 1, 1)], min_val=1, max_val=UNITS)
                    pe.wait_ge(sem("adj_free"), b + 1)
                    for c, (c0, w) in enumerate(BANKS3):
                        pe.matmul(ps[:TP, 3 * u + c, :w], zeros[:, :TP], zeros[:, :w], start=True, stop=False,
                                  skip_group_check=True)
                    with pe.Fori(lo, hi) as t:
                        ring = UNIT * (t % (RING // UNIT))
                        for v in range(UNIT):
                            pe.wait_ge(sem("onehot_ready"), UNIT * t + v + 1)
                            for c, (c0, w) in enumerate(BANKS3):
                                ins = pe.matmul(ps[:TP, 3 * u + c, :w], row(oh_src, ring + v, 0, TP, 128),
                                                row(oh_dst, ring + v, c0, c0 + w, 128), start=False, stop=False,
                                                skip_group_check=True)
                            ins.then_inc(sem("onehot_free"), 1)
                    for c, (c0, w) in enumerate(BANKS3):
                        ins = pe.matmul(ps[:TP, 3 * u + c, :w], zeros[:, :TP], zeros[:, :w], start=False, stop=True,
                                        skip_group_check=True)
                    ins.then_inc(sem("adj_full"), 1)
            pe.wait_ge(sem("adj_free"), 2 + NBUCKET)
            pe.wait_ge(sem("ones_ready"), 1)
            for m in range(NT):
                for r in range(NREL):
                    for s in range(NT):
                        c0 = (NT * r + s) * N + m * TP
                        ins = pe.matmul(ps[:, 7, m * NREL + r:m * NREL + r + 1], adj_all[:TP, c0:c0 + 128],
                                        ones_col[:TP, 0:1], start=(s == 0), stop=(s == NT - 1))
            ins.then_inc(sem("counts"), 1)

            def weights(g):
                pe.wait_ge(sem("w_split"), g + 1)
                return w_of(g)

            def three(p, xs, ws, first=True, last=True):
                (xh, xl), (wh, wl) = xs, ws
                pe.matmul(p, xh, wh, start=first, stop=False)
                pe.matmul(p, xh, wl, start=False, stop=False)
                return pe.matmul(p, xl, wh, start=False, stop=last)

            def transposed(tag, K, src, ready):
                job = 0
                for m in range(NT):
                    ready(m)
                    for k0, k1 in ((0, 4), (4, K)):
                        if job >= 4:
                            pe.wait_ge(sem("t_free"), turned_before(tag) + job - 3)
                        for k in range(k0, k1):
                            ins = pe.transpose(ps[:, 4 + job % 4, (k - k0) * TP:(k - k0 + 1) * TP], src(m, k), ident[:TP, :TP])
                        ins.then_inc(sem("t_full"), 1)
                        job += 1
                pe.wait_ge(sem("t_free"), turned_before(tag) + 2 * NT)

            def node_rows(K, m, w, p, c0=0, c1=None):
                wh, wl = w
                for k in range(K):
                    ins = three(p, (cols(hT_hi[:, k, :], m * TP, TP), cols(hT_lo[:, k, :], m * TP, TP)),
                                (wh[:, k, :], wl[:, k, :]), k == 0, k == K - 1)
                return ins

            def relational(L):
                K, O, nm = LAYERS[L]
                Oc = O // 2
                for n, (_, c, r, g) in enumerate(s for s in steps if s[0] == L):
                    w = weights(g)
                    with pe.Fori(0, NT // 2) as i:
                        for u in range(2):
                            m = 2 * i + u
                            pe.wait_ge(sem("y_free"), NT * (8 * L + n) + m + 1)
                            node_rows(K, m, w, ps[:TP, u, 0:Oc]).then_inc(sem("y_full"), 1)
                    if r is None:
                        continue
                    z = 3 * c + r
                    pe.wait_ge(sem("y_free"), 2 + NT * (8 * L + n + 1))
                    with pe.Fori(0, NT // 2) as i:
                        for u in range(2):
                            m = 2 * i + u
                            pe.wait_ge(sem("z_free"), NT * (6 * L + z) + m + 1)
                            for s in range(NT):
                                x = cols(adj[:, NT * r + s, :], m * TP, TP, TP)
                                pe.matmul(ps[:TP, 2 + u, 0:Oc], x, y_hi[:TP, s, 0:Oc], start=(s == 0), stop=False)
                                ins = pe.matmul(ps[:TP, 2 + u, 0:Oc], x, y_lo[:TP, s, 0:Oc], start=False, stop=(s == NT - 1))
                            ins.then_inc(sem("z_full"), 1)

            def from_acc(m, k):
                return acc[:TP, m, 128 * k:128 * (k + 1)]

            def once(*waits):
                def ready(m):
                    if m == 0:
                        for name, value in waits:
                            pe.wait_ge(sem(name), value)
                return ready

            transposed("t0", 7, from_acc, once(("h0_ready", 1)))
            relational(0)
            for L in (1, 2):
                transposed(f"t{L}", LAYERS[L][0], from_acc, once(("z_free", 2 + 6 * NT * L)))
                relational(L)

            def staged(tag):
                transposed(tag, KD, lambda m, k: stage[:TP, m % 2, 128 * k:128 * (k + 1)],
                           lambda m: pe.wait_ge(sem("staged"), staged_before(tag) + m + 1))

            def logits(tag):
                pe.wait_ge(sem("router"), nth(tag))
                with pe.Fori(0, NT) as m:
                    for k in range(KD):
                        ins = three(ps[:, 3, bass.ds(m * EXPERTS, EXPERTS)],
                                    (cols(hT_hi_flat, m * TP + k * N, 128), cols(hT_lo_flat, m * TP + k * N, 128)),
                                    (router_hi[:, k, :], router_lo[:, k, :]), k == 0, k == KD - 1)
                        if k == KD - 1:
                            ins.then_inc(sem("logits"), 1)

            def ranks(tag):
                pe.wait_ge(sem("chosen"), nth(tag))
                flat = chosen16[:TP, :, :].rearrange("p m e -> p (m e)")
                pe.matmul(ps[:TP, 2, 0:NT * EXPERTS], before[:TP, 0:TP], flat, start=True, stop=False)
                for d in range(1, NT):
                    pe.matmul(ps[:TP, 2, d * EXPERTS:NT * EXPERTS], one_of[:TP, 0:TP], flat[:, 0:(NT - d) * EXPERTS],
                              start=False, stop=(d == NT - 1))
                for m in range(NT):
                    ins = pe.matmul(ps[:, 3, 0:EXPERTS], one_of[:TP, :], chosen16[:TP, m, :], start=(m == 0), stop=(m == NT - 1))
                ins.then_inc(sem("ranked"), 1)

            def turn_tokens(tag, t):
                pe.wait_ge(sem(f"{tag}_gathered"), 16 * (t + 1))
                for k in range(2 * KD):
                    lhs = row(rows_ring, t % 3, 128 * k, 128 * (k + 1), 128)
                    q = k % KD
                    ins = pe.matmul(ps[:, 2 * (k // KD) + q // 4, (q % 4) * 128:(q % 4 + 1) * 128], lhs, ident16[:, :], start=True, stop=True)
                ins.then_inc(sem(f"{tag}_turned"), 1)

            def experts(tag):
                turn_tokens(tag, 0)
                for x in range(EXPERTS):
                    w1h, w1l = (w[:, x % 2, 0:KD * HID].rearrange("p (k n) -> p k n", k=KD) for w in (whi, wlo))
                    w2h, w2l = (w[:, x % 2, :].rearrange("p (k n) -> p k n", k=KH) for w in (w2_hi, w2_lo))
                    lo = pe.value_load(expert_start_i[0:1, x:x + 1], min_val=0, max_val=SLOT_TILES[tag])
                    hi = pe.value_load(expert_start_i[0:1, x + 1:x + 2], min_val=1, max_val=SLOT_TILES[tag])
                    pe.wait_ge(sem("w1_split"), block_of(tag) + x + 1)
                    pe.wait_ge(sem("w2_split"), block_of(tag) + x + 1)
                    with pe.Fori(lo, hi) as t:
                        pe.wait_ge(sem(f"{tag}_tokens_high"), t + 1)
                        pe.wait_ge(sem(f"{tag}_tokens_low"), t + 1)
                        for hc in range(KH):
                            f = slice(128 * hc, 128 * hc + 128)
                            if hc == 2:
                                pe.wait_ge(sem(f"{tag}_h_low"), KH * t + 1)
                            for k in range(KD):
                                p = ps[:, 6 + hc % 2, 0:128]
                                pe.matmul(p, w1h[:, k, f], gt_hi[:, k, :], start=(k == 0), stop=False)
                                pe.matmul(p, w1h[:, k, f], gt_lo[:, k, :], start=False, stop=False)
                                ins = pe.matmul(p, w1l[:, k, f], gt_hi[:, k, :], start=False, stop=(k == KD - 1))
                            ins.then_inc(sem(f"{tag}_h_full"), 1)
                        turn_tokens(tag, t + 1)
                        pe.wait_ge(sem(f"{tag}_h_low"), KH * (t + 1))
                        pe.wait_ge(sem(f"{tag}_o_left"), t + 1)
                        pe.wait_ge(sem(f"{tag}_o_right"), t + 1)
                        for c in range(2):
                            for k in range(KH):
                                ins = three(ps[:, 4 + c, 0:384], (ht_hi[:, k, :], ht_lo[:, k, :]),
                                            (w2h[:, k, 384 * c:384 * (c + 1)], w2l[:, k, 384 * c:384 * (c + 1)]),
                                            k == 0, k == KH - 1)
                            ins.then_inc(sem(f"{tag}_o_full"), 1)
                pe.wait_ge(sem(f"{tag}_tokens_high"), hi + 1)
                pe.wait_ge(sem(f"{tag}_tokens_low"), hi + 1)
                pe.nop().then_inc(sem(f"{tag}_turned"), TABLE_COLS[tag])

            staged("n1")
            logits("m0")
            ranks("m0")
            experts("m0")
            staged("n2")
            pe.wait_ge(sem("adj_sum"), 1)
            for c in range(2):
                w = weights(gcn_pieces[c])
                with pe.Fori(0, NT // 2) as i:
                    for u in range(2):
                        m = 2 * i + u
                        pe.wait_ge(sem("gy_free"), NT * c + m + 1)
                        node_rows(KD, m, w, ps[:TP, u, 0:384]).then_inc(sem("gy_full"), 1)
                pe.wait_ge(sem("gy_free"), 2 + NT * (c + 1))
                with pe.Fori(0, NT // 2) as i:
                    for u in range(2):
                        m = 2 * i + u
                        pe.wait_ge(sem("gz_free"), NT * c + m + 1)
                        for s in range(NT):
                            x = cols(adj[:, 2 * NT + s, :], m * TP, TP, TP)
                            pe.matmul(ps[:TP, 2 + u, 0:384], x, y_hi[:TP, s, 0:384], start=(s == 0), stop=False)
                            ins = pe.matmul(ps[:TP, 2 + u, 0:384], x, y_lo[:TP, s, 0:384], start=False, stop=(s == NT - 1))
                        ins.then_inc(sem("gz_full"), 1)
            staged("n4")
            for c in range(2):
                w = weights(v_pieces[c])
                with pe.Fori(0, NT // 2) as i:
                    for u in range(2):
                        m = 2 * i + u
                        pe.wait_ge(sem("v_low"), NT * c + m + 1)
                        node_rows(KD, m, w, ps[:TP, u, 0:384]).then_inc(sem("v_full"), 1)
            pe.nop().then_inc(sem("pv_full"), 4)
            pe.wait_ge(sem("v_low"), 2 + 2 * NT)
            job = 0
            for j in range(HEADS // 2):
                wh, wl = weights(qk_pieces[j])
                if j:
                    pe.wait_ge(sem("ot_low"), 3 * j)
                for which in range(2):
                    for c0, w in NODE_COLS:
                        job += 1
                        if job > 2:
                            pe.wait_ge(sem("qk_moved"), 2 * (job - 2))
                        p = ps[:, (job - 1) % 2, 0:w]
                        f = slice(128 * which, 128 * which + 128)
                        for k in range(KD):
                            pe.matmul(p, wh[:, k, f], hT_hi[:, k, c0:c0 + w], start=(k == 0), stop=False)
                            pe.matmul(p, wh[:, k, f], hT_lo[:, k, c0:c0 + w], start=False, stop=False)
                            ins = pe.matmul(p, wl[:, k, f], hT_hi[:, k, c0:c0 + w], start=False, stop=(k == KD - 1))
                        ins.then_inc(sem("qk_full"), 1)
                pe.wait_ge(sem("qk_parts"), 6 * (j + 1))
                if j:
                    pe.wait_ge(sem("pr_free"), 4 + 2 * NT * j)
                for h2 in range(2):
                    with pe.Fori(0, NT // 2) as i:
                        for u in range(2):
                            t = 2 * i + u
                            pe.wait_ge(sem("max_free"), (2 * j + h2) * NT + t + 1)
                            for c, (c0, w) in enumerate(BANKS3):
                                ins = pe.matmul(ps[:TP, 3 * u + c, :w], q_a[:, h2, bass.ds(t * TP, TP)],
                                                k_a[:, h2, c0:c0 + w], start=True, stop=True)
                            ins.then_inc(sem("max_full"), 1)
                pe.wait_ge(sem("max_free"), 2 + (2 * j + 2) * NT)
                for h2 in range(2):
                    for t in range(NT):
                        ins = pe.matmul(ps[64:65, 3 * h2 + t // 4, (t % 4) * TP:(t % 4 + 1) * TP], row_max[:TP, h2, t:t + 1],
                                        ident[:TP, :TP], start=True, stop=True)
                    ins.then_inc(sem("max_rows"), 1)
                pe.wait_ge(sem("max_set"), 2 * (j + 1))
                pe.wait_ge(sem("ones_set"), 1)
                def scores(qc, h2):
                    n = 10 * j + 2 * qc + h2
                    for kp in range(5):
                        pe.wait_ge(sem("exp_done"), 5 * n + kp + 1)
                        for e in range(2):
                            kt = 2 * kp + e
                            p = ps[:TP, kp, QC * e:QC * (e + 1)]
                            pe.matmul(p, k_a[:, h2, kt * TP:(kt + 1) * TP], q_a[:, h2, bass.ds(qc * QC, QC)],
                                      start=True, stop=False)
                            ins = pe.matmul(p, k_b[0:96, h2, kt * TP:(kt + 1) * TP], q_b[0:96, h2, bass.ds(qc * QC, QC)],
                                            start=False, stop=True)
                        ins.then_inc(sem("s_full"), 1)

                def values(qc, h2):
                    n = 10 * j + 2 * qc + h2
                    pe.wait_ge(sem("p_low"), 2 + 5 * n + 5)
                    for u in range(2):
                        pe.wait_ge(sem("o_free"), 2 * n + u + 1)
                        p = ps[:, 5 + u, 0:HD + 1]
                        for kt in range(NT):
                            ph, pl = p_hi[:TP, h2, kt, u * TP:u * TP + 128], p_lo[:TP, h2, kt, u * TP:u * TP + 128]
                            v = v_parts[:TP, kt, 2 * j + h2, :]
                            pe.matmul(p, ph, v[:, 0:HD + 1], start=(kt == 0), stop=False)
                            pe.matmul(p[:, 0:HD], ph, v[:, HD + 1:129], start=False, stop=False)
                            ins = pe.matmul(p, pl, v[:, 0:HD + 1], start=False, stop=(kt == NT - 1))
                        ins.then_inc(sem("pv_full"), 1)

                scores(0, 0)
                with pe.Fori(0, NT // 2 - 1) as qc:
                    scores(qc, 1)
                    values(qc, 0)
                    scores(qc + 1, 0)
                    values(qc, 1)
                scores(NT // 2 - 1, 1)
                values(NT // 2 - 1, 0)
                values(NT // 2 - 1, 1)
                pe.wait_ge(sem("o_free"), 2 + 2 * 5 * 2 * (j + 1))
                for t in range(3):
                    for m in range(4 * t, min(4 * t + 4, NT)):
                        ins = pe.transpose(ps[:, t, (m % 4) * TP:(m % 4 + 1) * TP], o_pair[:TP, m, :], ident[:TP, :TP])
                    ins.then_inc(sem("ot_full"), 1)
                wh, wl = weights(proj_pieces[j])
                pe.wait_ge(sem("ot_low"), 3 * (j + 1))
                with pe.Fori(0, NT // 2) as i:
                    for u in range(2):
                        m = 2 * i + u
                        for c in range(2):
                            pe.wait_ge(sem("pr_free"), 2 * NT * j + 2 * m + c + 1)
                            three(ps[:TP, 3 + 2 * u + c, 0:384], (cols(ot_hi, m * TP, TP), cols(ot_lo, m * TP, TP)),
                                  (wh[:, 0, 384 * c:384 * (c + 1)], wl[:, 0, 384 * c:384 * (c + 1)])
                                  ).then_inc(sem("pr_full"), 1)
            staged("n5")
            logits("m1")
            ranks("m1")
            pe.wait_ge(sem("gates_ready"), 1)
            for q in range(3):
                for m in range(4 * q, min(4 * q + 4, NT)):
                    ins = pe.transpose(ps[0:EXPERTS, 4 + q, (m % 4) * TP:(m % 4 + 1) * TP], gates[:TP, m, :], ident[:TP, :TP])
                ins.then_inc(sem("gt_full"), 1)
            pe.wait_ge(sem("gt_done"), 3)
            pe.wait_ge(sem("b2_in"), 16)
            for m in range(NT):
                for c in range(2):
                    if m >= 2:
                        pe.wait_ge(sem("gb_free"), 2 * (m - 2) + c + 1)
                    pe.matmul(ps[:TP, c + 4 * (m % 2), 0:384], gate_t[:, m * TP:(m + 1) * TP], b2_rows[:, 384 * c:384 * (c + 1)],
                              start=True, stop=True).then_inc(sem("gb_full"), 1)
            pe.wait_ge(sem("gb_free"), 2 * NT)
            experts("m1")


def kernel(**x):
    import numpy as np
    import concourse.bacc as bacc
    from concourse.bass_utils import run_bass_kernel_spmd

    host = {k: np.asarray(v) for k, v in x.items()}
    pairs = HEADS // 2
    qkv_t = host["L1_ffn_qkv_w"].T
    w_qk = np.concatenate([qkv_t[:, 0:D].reshape(D, pairs, 128), qkv_t[:, D:2 * D].reshape(D, pairs, 128)], axis=2)
    arrays = {
        "x": host["x"], "src": host["src"], "dst": host["dst"], "typ": host["edge_type_3"],
        "node_type": host["node_type_3"].reshape(NT, TP).T,
        "emb": host["L0_gnn_node_emb"],
        "rel1": host["L0_gnn_w_rel1"], "root1": host["L0_gnn_w_root1"], "b1": host["L0_gnn_b1"],
        "rel2": host["L0_gnn_w_rel2"], "root2": host["L0_gnn_w_root2"], "b2": host["L0_gnn_b2"],
        "rel3": host["L0_gnn_w_rel3"], "root3": host["L0_gnn_w_root3"], "b3": host["L0_gnn_b3"],
        "router": host["L0_ffn_router_w"], "wi": host["L0_ffn_wi"], "wo": host["L0_ffn_wo"],
        "gcn_w": host["L1_gnn_W"], "gcn_b": host["L1_gnn_b"],
        "n1_w": host["L1_ffn_norm1_w"], "n1_b": host["L1_ffn_norm1_b"],
        "w_qk": w_qk.transpose(1, 0, 2), "w_v": qkv_t[:, 2 * D:],
        "qk_b": host["L1_ffn_qkv_b"][0:2 * D].reshape(12, 128).T, "v_b": host["L1_ffn_qkv_b"][2 * D:],
        "w_proj": host["L1_ffn_proj_w"].T, "proj_b": host["L1_ffn_proj_b"],
        "n2_w": host["L1_ffn_norm2_w"], "n2_b": host["L1_ffn_norm2_b"],
        "w_gate": host["L1_ffn_w_gate"],
        "w1": host["L1_ffn_W1"], "b1x": host["L1_ffn_b1"].reshape(EXPERTS * KH, 128).T,
        "w2": host["L1_ffn_W2"], "b2x": host["L1_ffn_b2"],
    }
    nc = bacc.Bacc("TRN2", target_bir_lowering=False, num_devices=1)
    feed, aps = {}, {}
    for name, v in arrays.items():
        v = np.ascontiguousarray(v)
        feed[f"in_{name}"] = v
        aps[name] = nc.dram_tensor(f"in_{name}", v.shape, mybir.dt.from_np(v.dtype), kind="ExternalInput").ap()
    out = nc.dram_tensor("out_nodes", (N, D), F32, kind="ExternalOutput").ap()
    build(nc, aps, out)
    return run_bass_kernel_spmd(nc, [feed], core_ids=[0]).results[0]["out_nodes"]
```

```python
from contextlib import ExitStack

import concourse.bass as bass
from concourse import mybir

F32, F16 = mybir.dt.float32, mybir.dt.float16
I32, U32 = mybir.dt.int32, mybir.dt.uint32
ALU = mybir.AluOpType
ACT = mybir.ActivationFunctionType
AX_X = mybir.AxisListType.X

N = 1250
TP = 125
NT = N // TP
D = 768
KD = D // 128
NREL = 3
EP = 125
NBUCKET = NREL * NT
EXPERTS = 8
HID = 384
KH = HID // 128
HEADS = 12
HD = 64
QC = 2 * TP
LAYERS = ((7, 896, "1"), (7, 768, "2"), (6, 768, "3"))
WMAX = 7 * 448
NODE_COLS = ((0, 418), (418, 416), (834, 416))
BANKS3 = ((0, 512), (512, 512), (1024, 226))
PICKS = {"m0": 1, "m1": 2}
SLOT_TILES = {tag: (n * N + 127 * EXPERTS) // 128 for tag, n in PICKS.items()}
TABLE_COLS = {tag: n + 1 for tag, n in SLOT_TILES.items()}
PACKED_OVER = 4
UNIT = 3


def build(nc, a, out):
    E = a["src"].shape[0]
    EJ = E // EP
    UNITS = E // (UNIT * 128) + NBUCKET + 1
    ETILES = UNIT * UNITS
    PAD_EDGE = (N + 50) * 128 + 127

    ctx = ExitStack()
    with ctx:
        sems = {}

        def sem(name):
            if name not in sems:
                sems[name] = ctx.enter_context(nc.semaphore(name))
            return sems[name]

        def sb(name, shape, dt=F32, scope=ctx):
            return scope.enter_context(nc.sbuf_tensor(name, shape, dt))

        ident = sb("ident", [128, 128])
        bias_b = sb("bias_b", [128, 896])
        inv_cnt = sb("inv_cnt", [128, NT, NREL])
        dinv = sb("dinv", [128, NT])
        stats = sb("stats", [128, NT, 2, 6])
        meanvar = sb("meanvar", [128, NT, 2])
        rstd = sb("rstd", [128, NT])
        minus_half = sb("minus_half", [128, NT])
        gates = sb("gates", [128, NT, EXPERTS])
        token = sb("token", [128, NT])
        ident16 = sb("ident16", [128, 128], F16)
        one_of = sb("one_of", [128, 128], F16)
        before = sb("before", [128, 128], F16)
        ones_col = sb("ones_col", [128, 2], F16)
        eye8 = sb("eye8", [128, EXPERTS])
        node_type = sb("node_type", [128, NT], I32)
        type_f = sb("type_f", [128, NT])
        top_val = sb("top_val", [128, NT, 8])
        top_idx = sb("top_idx", [128, NT, 8], U32)
        top_idx_f = sb("top_idx_f", [128, NT, 8])
        logit = sb("logit", [128, NT, EXPERTS])
        row_max = sb("row_max", [128, 2, NT])
        soft = sb("soft", [128, NT, EXPERTS])
        share = sb("share", [128, 4, NT])
        recip = sb("recip", [128, 2])
        router32 = sb("router32", [128, KD, EXPERTS])
        router_hi = sb("router_hi", [128, KD, EXPERTS], F16)
        router_lo = sb("router_lo", [128, KD, EXPERTS], F16)
        pidx = sb("pidx", [128, 4])
        tstart_i = sb("tstart_i", [128, NBUCKET + 1], I32)
        wraw = sb("wraw", [128, WMAX])
        whi = sb("whi", [128, 2, WMAX], F16)
        wlo = sb("wlo", [128, 2, WMAX], F16)
        qk_bias = sb("qk_bias", [128, 12])
        b1_cols = sb("b1_cols", [128, EXPERTS * KH])

        mt = ExitStack()
        rows_ring = sb("rows_ring", [128, 3, 2 * D], F16, mt)
        out_ring = sb("out_ring", [128, 2, D], F32, mt)
        gt_hi = sb("gt_hi", [128, KD, 128], F16, mt)
        gt_lo = sb("gt_lo", [128, KD, 128], F16, mt)
        ht_hi = sb("ht_hi", [128, KH, 128], F16, mt)
        ht_lo = sb("ht_lo", [128, KH, 128], F16, mt)
        gelu32 = sb("gelu32", [128, KH, 128], F32, mt)
        chosen = sb("chosen", [128, 2, NT, EXPERTS], F32, mt)
        chosen16 = sb("chosen16", [128, NT, EXPERTS], F16, mt)
        expert_slot = sb("expert_slot", [128, NT, EXPERTS], F32, mt)
        picked_slot = sb("picked_slot", [128, NT, EXPERTS], F32, mt)
        token_slot = sb("token_slot", [128, 2, NT], F32, mt)
        token_slot_i = sb("token_slot_i", [128, 3, 2, NT], I32, mt)
        token_addr_f = sb("token_addr_f", [128, 2, NT], F32, mt)
        token_addr = sb("token_addr", [128, 2, NT], U32, mt)
        records = sb("records", [128, 2, NT, 4], F32, mt)
        expert_tiles_f = sb("expert_tiles_f", [128, EXPERTS], F32, mt)
        expert_tiles_i = sb("expert_tiles_i", [128, EXPERTS], I32, mt)
        expert_start = sb("expert_start", [128, EXPERTS + 1], F32, mt)
        expert_start_i = sb("expert_start_i", [128, EXPERTS + 1], I32, mt)
        expert_slot0 = sb("expert_slot0", [128, EXPERTS], F32, mt)
        table = sb("table", [128, TABLE_COLS["m1"], 4], F32, mt)
        gather_row = sb("gather_row", [128, TABLE_COLS["m1"]], U32, mt)
        scatter_row = sb("scatter_row", [128, TABLE_COLS["m1"]], U32, mt)
        slot_gate = sb("slot_gate", [128, TABLE_COLS["m1"]], F32, mt)
        mt.close()
        yb = ExitStack()
        second_back = sb("second_back", [128, NT, D], F32, yb)
        yb.close()

        hT_hi = sb("hT_hi", [128, 7, N], F16)
        hT_lo = sb("hT_lo", [128, 7, N], F16)
        hT_hi_flat, hT_lo_flat = (t[:, :, :].rearrange("p k n -> p (k n)") for t in (hT_hi, hT_lo))
        acc = sb("acc", [128, NT, 896])
        onehot = ExitStack()
        iota_n = sb("iota_n", [128, N], F16, onehot)
        sorted_f = sb("sorted_f", [128, 2, ETILES], F32, onehot)
        oh_dst = sb("oh_dst", [128, UNIT, N], F16, onehot)
        oh_src = sb("oh_src", [128, UNIT, TP], F16, onehot)
        zeros = sb("zeros", [128, 512], F16, onehot)
        onehot.close()
        y = ExitStack()
        y_hi = sb("y_hi", [128, NT, 448], F16, y)
        y_lo = sb("y_lo", [128, NT, 448], F16, y)
        edge = ExitStack()
        packed = sb("packed", [128, EJ], I32, edge)
        addr = sb("addr", [128, EJ], U32, edge)
        pad_fill = sb("pad_fill", [128, ETILES], I32, edge)
        sorted_p = sb("sorted_p", [128, ETILES], I32, edge)
        sorted_i = sb("sorted_i", [128, 2, ETILES], I32, edge)
        pad_records = [sb(f"pad_records{i}", [128, cols, 4], F32, edge) for i, cols in enumerate(TABLE_COLS.values())]
        early = ExitStack()
        early_hi = [sb(f"early_hi{r}", [128, NT, 448], F16, early) for r in range(NREL)]
        early_lo = [sb(f"early_lo{r}", [128, NT, 448], F16, early) for r in range(NREL)]
        early.close()
        ones16 = sb("ones16", [128, 128], F16, edge)
        e_src = sb("e_src", [128, EJ], I32, edge)
        e_dst = sb("e_dst", [128, EJ], I32, edge)
        e_typ = sb("e_typ", [128, EJ], I32, edge)
        src_tile = sb("src_tile", [128, EJ], F32, edge)
        bucket = sb("bucket", [128, EJ], F32, edge)
        src_loc = sb("src_loc", [128, EJ], F32, edge)
        packed_f = sb("packed_f", [128, EJ], F32, edge)
        mask = sb("mask", [128, NBUCKET, EJ], F16, edge)
        below = sb("below", [128, 4, EJ], F16, edge)
        col_cnt = sb("col_cnt", [128, 3, NBUCKET], F16, edge)
        row_cnt = sb("row_cnt", [128, NBUCKET], F16, edge)
        tiles_f = sb("tiles_f", [128, NBUCKET], F32, edge)
        tiles_i = sb("tiles_i", [128, NBUCKET], I32, edge)
        tstart = sb("tstart", [128, NBUCKET + 1], F32, edge)
        first_slot = sb("first_slot", [128, NBUCKET], F32, edge)
        slot = sb("slot", [128, EJ], F32, edge)
        slot_part = sb("slot_part", [128, 2, EJ], F32, edge)
        slot_i = sb("slot_i", [128, EJ], I32, edge)
        lane_i = sb("lane_i", [128, EJ], I32, edge)
        tile_i = sb("tile_i", [128, EJ], I32, edge)
        lane_f = sb("lane_f", [128, EJ], F32, edge)
        addr_f = sb("addr_f", [128, EJ], F32, edge)
        edge.close()
        adj_all = sb("adj", [128, NBUCKET * N + 4], F16, y)
        adj = adj_all[:, 0:NBUCKET * N].rearrange("p (b n) -> p b n", n=N)
        y.close()
        e0 = ExitStack()
        stage = sb("stage", [128, 2, D], F32, e0)
        again = sb("again", [128, 2, D], F32, e0)
        ln_w = sb("ln_w", [128, D], F32, e0)
        ln_b = sb("ln_b", [128, D], F32, e0)
        e1 = ExitStack()
        packed_rows = sb("packed_rows", [128, 3, 2, D], F16, e1)
        w2_raw = sb("w2_raw", [128, KH * D], F32, e1)
        w2_hi = sb("w2_hi", [128, 2, KH * D], F16, e1)
        w2_lo = sb("w2_lo", [128, 2, KH * D], F16, e1)
        gate_t = sb("gate_t", [EXPERTS, N], F32, e1)
        b2_rows = sb("b2_rows", [EXPERTS, D], F32, e1)
        e1.close()
        e2 = ExitStack()
        first_back = sb("first_back", [128, NT, D], F32, e2)
        e2.close()
        e0.close()
        at = ExitStack()
        v_parts = sb("v_parts", [128, NT, HEADS, 129], F16, at)
        qk32 = sb("qk32", [128, 2, 418], F32, at)
        q_a = sb("q_a", [128, 2, N], F16, at)
        k_a = sb("k_a", [128, 2, N], F16, at)
        q_b = sb("q_b", [128, 2, N], F16, at)
        k_b = sb("k_b", [128, 2, N], F16, at)
        p32 = sb("p32", [128, 4, 2 * QC], F32, at)
        p_hi = sb("p_hi", [128, 2, NT, QC + 6], F16, at)
        p_lo = sb("p_lo", [128, 2, NT, QC + 6], F16, at)
        o_pair = sb("o_pair", [128, NT, 128], F32, at)
        ot_hi = sb("ot_hi", [128, N], F16, at)
        ot_lo = sb("ot_lo", [128, N], F16, at)
        at.close()

        ps = ctx.enter_context(nc.psum_tensor("ps", [128, 8, 512], F32))
        x3_dram = nc.dram_tensor("x3_dram", [N, D], F32, kind="Internal").ap()
        early_dram = nc.dram_tensor("early_products", [NREL, 2, TP, NT * 448], F16, kind="Internal").ap()
        rows_dram = nc.dram_tensor("token_rows", [N, 2 * D], F16, kind="Internal").ap()
        table_dram, moe_dram = {}, {}
        for tag, cols_ in TABLE_COLS.items():
            table_dram[tag] = nc.dram_tensor(f"table_{tag}", [128 * cols_, 4], F32, kind="Internal").ap()
            moe_dram[tag] = nc.dram_tensor(f"moe_{tag}", [PICKS[tag] * N + 128 * cols_, D], F32, kind="Internal").ap()
        edge_dram = nc.dram_tensor("edge_slots", [128 * ETILES, 1], I32, kind="Internal").ap()

        pieces = []

        def piece(src, k, cols, done, value):
            pieces.append((src, k, cols, done, value))
            return len(pieces) - 1

        steps = []
        for L, (K, O, nm) in enumerate(LAYERS):
            Oc = O // 2
            order = [(c, r) for c in range(2) for r in (None, 0, 1, 2)]
            if L == 0:
                order.sort(key=lambda s: s[1] is not None)
            for n, (c, r) in enumerate(order):
                w = a[f"root{nm}"] if r is None else a[f"rel{nm}"][r]
                v = w.rearrange("(k p) n -> p k n", p=128)[:, :, c * Oc:(c + 1) * Oc]
                steps.append((L, c, r, piece(v, K, Oc, "y_full", NT * (8 * L + n + 1))))
        gcn_pieces = [piece(a["gcn_w"].rearrange("(k p) n -> p k n", p=128)[:, :, c * 384:(c + 1) * 384],
                            KD, 384, "gy_full", NT * (c + 1)) for c in range(2)]
        v_pieces = [piece(a["w_v"].rearrange("(k p) n -> p k n", p=128)[:, :, c * 384:(c + 1) * 384],
                          KD, 384, "v_full", NT * (c + 1)) for c in range(2)]
        qk_pieces, proj_pieces = [], []
        for j in range(HEADS // 2):
            qk_pieces.append(piece(a["w_qk"][j].rearrange("(k p) n -> p k n", p=128), KD, 256, "qk_full", 6 * (j + 1)))
            proj_pieces.append(piece(a["w_proj"][128 * j:128 * (j + 1), :].rearrange("(k p) n -> p k n", p=128),
                                     1, D, "pr_full", 2 * NT * (j + 1)))
        expert_weights = {"m0": (a["wi"], a["wo"]), "m1": (a["w1"], a["w2"])}
        first_part = len(steps)

        def w_of(g):
            _, k, cols, _, _ = pieces[g]
            v = lambda t: t[:, g % 2, 0:k * cols].rearrange("p (k n) -> p k n", k=k)
            return v(whi), v(wlo)

        def row(reg3, i, lo, hi, parts=TP):
            return reg3[:parts, bass.ds(i, 1), lo:hi].rearrange("p o n -> p (o n)")

        def cols(t2, start, n, parts=128):
            return t2[:parts, bass.ds(start, n)]

        def row_bias(name):
            v = a[name].rearrange("(o d) -> o d", o=1)
            return v.broadcast_to([TP, v.shape[1]])

        p32_flat = p32[:, :, :].rearrange("p a b -> p (a b)")
        block = ctx.enter_context(nc.Block())

        FIRST_LATE = 2 + NREL

        def parts_of(L, when):
            for n, (_, c, r, g) in enumerate(s for s in steps if s[0] == L):
                ahead = L == 0 and (r is None or c == 0)
                product = ahead == (when == "early")
                aggregation = r is not None and when == "late"
                if product or aggregation:
                    yield n, c, r, g, product, aggregation, ahead and r is not None

        def powers(tag):
            return ("n0", "deg", "n1", "n2", "n3", "n4", "n5").index(tag)

        def nth(tag):
            return {"m0": 1, "m1": 2}[tag]

        def block_of(tag):
            return EXPERTS * (nth(tag) - 1)

        def staged_before(tag):
            return NT * ("n1", "n2", "n4", "n5").index(tag)

        def turned_before(tag):
            return 2 * NT * ("t0", "t1", "t2", "n1", "n2", "n4", "n5").index(tag)


        @block.sync
        def _(sp):
            for t, n in ((e_src, "src"), (e_dst, "dst"), (e_typ, "typ")):
                sp.dma_start(t[:EP, :], a[n].rearrange("(p j) -> p j", p=EP)).then_inc(sem("edges_in"), 16)

            def load_pieces(first, last):
                for g in range(first, min(last, len(pieces))):
                    src, k, n, _, _ = pieces[g]
                    if g == first_part:
                        sp.wait_ge(sem("w1_split"), 3 * EXPERTS)
                    elif g >= 1:
                        sp.wait_ge(sem("w_split"), g)
                    sp.dma_start(wraw[:, 0:k * n].rearrange("p (k n) -> p k n", k=k), src).then_inc(sem("w_in"), 16)

            def load_experts(tag, split, region, value):
                w1, w2 = expert_weights[tag]
                for x in range(EXPERTS):
                    if x:
                        sp.wait_ge(sem("w1_split"), 3 * (block_of(tag) + x))
                    else:
                        sp.wait_ge(sem("w_split"), split)
                    sp.dma_start(wraw[:, 0:KD * HID].rearrange("p (k n) -> p k n", k=KD),
                                 w1[x].rearrange("(k p) n -> p k n", p=128)).then_inc(sem("w1_in"), 16)
                    if x == 0:
                        for m in range(NT):
                            sp.wait_ge(sem("pack_low"), NT * nth(tag) - NT + m + 1)
                            sp.dma_start(rows_dram[m * TP:(m + 1) * TP, :],
                                         packed_rows[:TP, m % 3, :, :].rearrange("p a d -> p (a d)")
                                         ).then_inc(sem(f"{tag}_rows_out{m % 3}"), 16)
                        sp.wait_ge(sem(region), value)
                    else:
                        sp.wait_ge(sem("w2_split"), 3 * (block_of(tag) + x))
                    sp.dma_start(w2_raw[:, :].rearrange("p (k n) -> p k n", k=KH),
                                 w2[x].rearrange("(k p) n -> p k n", p=128)).then_inc(sem("w2_in"), 16)
                    if x == 0 and tag == "m1":
                        for m in range(NT):
                            if m >= 2:
                                sp.wait_ge(sem("last_sum"), m - 1)
                            sp.dma_start(again[:TP, m % 2, :], x3_dram[m * TP:(m + 1) * TP, :]
                                         ).then_inc(sem(f"last_in{m % 2}"), 16)

            load_pieces(0, first_part)
            load_experts("m0", first_part, "adj_sum", 1)
            load_pieces(first_part, len(pieces))
            load_experts("m1", len(pieces), "pr_free", 4 + 2 * NT * 6)

        @block.gpsimd
        def _(pool):
            pool.iota(pidx[:, 0:1], [[0, 1]], base=0, channel_multiplier=1,
                      allow_small_or_imprecise_dtypes=True).then_inc(sem("iota_ready"), 1)
            pool.iota(iota_n[:, :], [[1, N]], base=0, channel_multiplier=0,
                      allow_small_or_imprecise_dtypes=True).then_inc(sem("iota_ready"), 1)
            pool.iota(eye8[:, :], [[1, EXPERTS]], base=0, channel_multiplier=0,
                      allow_small_or_imprecise_dtypes=True).then_inc(sem("iota_ready"), 1)
            pool.iota(token[:, :], [[TP, NT]], base=0, channel_multiplier=1,
                      allow_small_or_imprecise_dtypes=True).then_inc(sem("iota_ready"), 1)
            for t, (tag, cols_) in zip(pad_records, TABLE_COLS.items()):
                pool.memset(t[:, :, 0:1], 0.0)
                pool.memset(t[:, :, 2:4], 0.0)
                pool.iota(t[:, :, 1:2].rearrange("p a o -> p (a o)"), [[1, cols_]], base=PICKS[tag] * N,
                          channel_multiplier=cols_, allow_small_or_imprecise_dtypes=True).then_inc(sem("pad_ready"), 1)
            pool.memset(pad_fill[:, :], PAD_EDGE).then_inc(sem("pad_ready"), 1)
            pool.memset(minus_half[:, :], -0.5).then_inc(sem("half_ready"), 1)
            split = [0]

            def split_to(last):
                while split[0] <= min(last, len(pieces) - 1):
                    g = split[0]
                    _, k, n, _, _ = pieces[g]
                    raw, hi, lo = wraw[:, 0:k * n], whi[:, g % 2, 0:k * n], wlo[:, g % 2, 0:k * n]
                    pool.wait_ge(sem("w_in"), 16 * (g + 1))
                    if g >= 2 and g not in (first_part, first_part + 1):
                        pool.wait_ge(sem(pieces[g - 2][3]), pieces[g - 2][4])
                    pool.tensor_copy(hi, raw).then_inc(sem("w_high"), 1)
                    pool.wait_ge(sem("w_high"), g + 1)
                    pool.tensor_tensor(lo, raw, hi, ALU.subtract).then_inc(sem("w_split"), 1)
                    split[0] += 1

            def power(tag, t):
                pool.wait_ge(sem("half_ready"), 1)
                pool.wait_ge(sem("variance"), 1 + powers(tag))
                pool.tensor_tensor(t[:TP, :], t[:TP, :], minus_half[:TP, :], ALU.pow).then_inc(sem("rstd_ready"), 1)

            split_to(1)
            pool.wait_ge(sem("padded"), 48)
            pool.wait_ge(sem("addr_ready"), 1)
            for j in range(EJ):
                if j == 30:
                    power("n0", rstd)
                pool.indirect_dma_start(edge_dram[:, :], bass.IndirectOffsetOnAxis(ap=addr[:EP, j:j + 1], axis=0),
                                        packed[:EP, j:j + 1], None).then_inc(sem("scattered"), 16)
            split[0] = FIRST_LATE
            split_to(FIRST_LATE + 1)
            power("deg", dinv)
            split_to(first_part - 1)
            pool.wait_ge(sem("z_full"), 18 * NT)
            def add_first(tiles):
                for s in tiles:
                    pool.tensor_tensor(adj[:TP, 2 * NT + s, :], adj[:TP, 2 * NT + s, :], adj[:TP, s, :], ALU.add
                                       ).then_inc(sem("adj_first"), 1)

            add_first(range(PACKED_OVER))
            power("n1", rstd)
            add_first(range(PACKED_OVER, NT))
            for s in range(NT):
                t = adj[:TP, 2 * NT + s, :]
                pool.wait_ge(sem("adj_first"), s + 1)
                pool.tensor_tensor(t, t, adj[:TP, NT + s, :], ALU.add).then_inc(sem("adj_second"), 1)
            for s in range(NT):
                dg = adj[:TP, 2 * NT + s, s * TP:(s + 1) * TP]
                pool.wait_ge(sem("adj_second"), s + 1)
                ins = pool.tensor_tensor(dg, dg, ident[:TP, :TP], ALU.add)
            ins.then_inc(sem("adj_sum"), 1)

            def move_rows(tag):
                pool.wait_ge(sem("padded"), 48)
                pool.wait_ge(sem("records"), nth(tag))
                for c in range(PICKS[tag]):
                    for m in range(NT):
                        pool.indirect_dma_start(table_dram[tag][:, :],
                                                bass.IndirectOffsetOnAxis(ap=token_addr[:TP, c, m:m + 1], axis=0),
                                                records[:TP, c, m, :], None).then_inc(sem(f"{tag}_records_out"), 16)
                pool.wait_ge(sem(f"{tag}_table"), 1)
                for i, n in enumerate((4, 3, 3)):
                    pool.wait_ge(sem(f"{tag}_rows_out{i}"), 16 * n)
                pool.nop().then_inc(sem(f"{tag}_out_free"), 2)

                def gather(t):
                    if t:
                        pool.wait_ge(sem(f"{tag}_gathered"), 16 * t)
                    if t >= 3:
                        pool.wait_ge(sem(f"{tag}_turned"), t - 2)
                    pool.indirect_dma_start(rows_ring[:, t % 3, :], None, rows_dram[:, :],
                                            bass.IndirectOffsetOnAxis(ap=gather_row[:, t:t + 1], axis=0)
                                            ).then_inc(sem(f"{tag}_gathered"), 16)

                gather(0)
                gather(1)
                for t in range(SLOT_TILES[tag]):
                    if t + 2 < TABLE_COLS[tag]:
                        gather(t + 2)
                    if t:
                        pool.wait_ge(sem(f"{tag}_scattered"), 16 * t)
                        pool.nop().then_inc(sem(f"{tag}_out_free"), 1)
                    pool.wait_ge(sem(f"{tag}_o_left"), t + 2)
                    pool.wait_ge(sem(f"{tag}_o_right"), t + 2)
                    pool.indirect_dma_start(moe_dram[tag][:, :],
                                            bass.IndirectOffsetOnAxis(ap=scatter_row[:, t:t + 1], axis=0),
                                            out_ring[:, t % 2, :], None).then_inc(sem(f"{tag}_scattered"), 16)
                pool.wait_ge(sem(f"{tag}_gathered"), 16 * TABLE_COLS[tag])

            move_rows("m0")
            split_to(gcn_pieces[1])
            power("n2", rstd)
            split_to(v_pieces[1])
            power("n3", rstd)
            power("n4", rstd)
            split_to(proj_pieces[0])
            for j in range(HEADS // 2 - 1):
                split_to(proj_pieces[j + 1])
            power("n5", rstd)
            move_rows("m1")

        @block.scalar
        def _(act):
            act.dma_start(qk_bias[:, :], a["qk_b"]).then_inc(sem("consts_in"), 16)
            act.dma_start(b1_cols[:, :], a["b1x"]).then_inc(sem("consts_in"), 16)
            act.dma_start(node_type[:TP, :], a["node_type"]).then_inc(sem("consts_in"), 16)
            act.dma_start(router32[:, :, :], a["router"].rearrange("(k p) n -> p k n", p=128)).then_inc(sem("consts_in"), 16)
            act.dma_start(acc[:TP, :, 0:D], a["x"].rearrange("(t p) d -> p t d", p=TP)).then_inc(sem("x_in"), 16)
            for t in range(3):
                act.dma_start(bias_b[:TP, 128 * t:128 * (t + 1)], a["emb"][t:t + 1, :].broadcast_to([TP, 128])
                              ).then_inc(sem("x_in"), 16)
            act.wait_ge(sem("pad_ready"), 3)
            act.dma_start(edge_dram.rearrange("(p t) o -> p (t o)", p=128), pad_fill[:, :]).then_inc(sem("padded"), 16)
            for t, d in zip(pad_records, table_dram.values()):
                act.dma_start(d.rearrange("(p t) f -> p t f", p=128), t[:, :, :]).then_inc(sem("padded"), 16)
            def transposed(tag, K, func, pack=None):
                job = 0
                for m in range(NT):
                    if pack:
                        act.wait_ge(sem("staged"), staged_before(tag) + m + 1)
                        if m >= 3:
                            act.wait_ge(sem(f"{pack}_rows_out{m % 3}"), 16 * (m // 3))
                        act.activation(packed_rows[:TP, m % 3, 0, :], stage[:TP, m % 2, :], ACT.Copy
                                       ).then_inc(sem(f"pack_high"), 1)
                    for k0, k1 in ((0, 4), (4, K)):
                        act.wait_ge(sem("t_full"), turned_before(tag) + job + 1)
                        act.activation(hT_hi[:, k0:k1, m * TP:(m + 1) * TP],
                                       ps[:, 4 + job % 4, 0:(k1 - k0) * TP].rearrange("p (k n) -> p k n", n=TP),
                                       func).then_inc(sem("t_high"), 1)
                        job += 1

            def relational(L, when="late"):
                K, O, nm = LAYERS[L]
                Oc = O // 2
                for n, c, r, g, product, aggregation, stored in parts_of(L, when):
                    if r is None:
                        continue
                    dst = early_hi[r] if stored else y_hi
                    done = NT * (6 * L + 3 * c + r)
                    if stored and when == "early":
                        if r == 0:
                            early_split(2)
                        if r < 2:
                            early_split(3 + r)
                    elif done:
                        act.wait_ge(sem("z_full"), done)
                    if product:
                        with act.Fori(0, NT // 2) as i:
                            for u in range(2):
                                act.wait_ge(sem("y_full"), NT * (8 * L + n) + 2 * i + u + 1)
                                act.activation(row(dst, 2 * i + u, 0, Oc), ps[:TP, u, 0:Oc], ACT.Copy
                                               ).then_inc(sem("y_high"), 1)
                        if stored:
                            act.wait_ge(sem("y_free"), 2 + NT * (8 * L + n + 1))
                            for q, t in enumerate((early_hi[r], early_lo[r])):
                                act.dma_start(early_dram[r, q], t[:TP, :, :].rearrange("p m n -> p (m n)")
                                              ).then_inc(sem("early_out"), 16)
                    else:
                        for q, t in enumerate((y_hi, y_lo)):
                            act.dma_start(t[:TP, :, :].rearrange("p m n -> p (m n)"), early_dram[r, q]
                                          ).then_inc(sem("early_back"), 16)

            def early_split(g):
                _, k, n, _, _ = pieces[g]
                act.wait_ge(sem("w_in"), 16 * (g + 1))
                act.wait_ge(sem(pieces[g - 2][3]), pieces[g - 2][4])
                act.activation(whi[:, g % 2, 0:k * n], wraw[:, 0:k * n], ACT.Copy).then_inc(sem("w_high"), 1)

            act.wait_ge(sem("h0_ready"), 1)
            act.dma_start(bias_b[:TP, 0:896], row_bias("b1")).then_inc(sem("bias_in"), 16)
            transposed("t0", 7, ACT.Copy)
            relational(0, "early")
            act.wait_ge(sem("scattered"), 16 * EJ)
            act.dma_start(sorted_p[:, :], edge_dram.rearrange("(p t) o -> p (t o)", p=128)).then_inc(sem("sorted_in"), 16)
            act.wait_ge(sem("early_out"), 16 * 2 * NREL)
            act.nop().then_inc(sem("adj_free"), 2)
            with act.Fori(0, NBUCKET // 2) as bh:
                for u in range(2):
                    act.wait_ge(sem("adj_full"), 2 * bh + u + 1)
                    act.activation(row(adj, 2 * bh + u, 0, N), ps[:TP, 3 * u:3 * u + 3, :].rearrange("p a b -> p (a b)")[:, :N],
                                   ACT.Copy).then_inc(sem("adj_free"), 1)
            relational(0)
            for L in (1, 2):
                act.wait_ge(sem("z_free"), 2 + 6 * NT * L)
                act.wait_ge(sem("y_free"), 2 + 8 * NT * L)
                act.dma_start(bias_b[:TP, 0:D], row_bias(f"b{L + 1}")).then_inc(sem("bias_in"), 16)
                transposed(f"t{L}", LAYERS[L][0], ACT.Relu)
                relational(L)

            act.wait_ge(sem("y_full"), 24 * NT)
            for h in range(2):
                act.dma_start(second_back[:TP, 5 * h:5 * h + 5, :],
                              a["x"][5 * h * TP:(5 * h + 5) * TP, :].rearrange("(t p) d -> p t d", p=TP)
                              ).then_inc(sem(f"res_in{h}"), 16)

            def split_high(tag, x, parts):
                for i in parts:
                    name = ("w1", "w2")[i // 3]
                    c = slice(D * (i % 3), D * (i % 3 + 1))
                    if i % 3 == 0:
                        act.wait_ge(sem(f"{name}_in"), 16 * (block_of(tag) + x + 1))
                    raw, hi = ((wraw, whi), (w2_raw, w2_hi))[i // 3]
                    act.activation(hi[:, x % 2, c], raw[:, c], ACT.Copy).then_inc(sem(f"{name}_high"), 1)

            def tokens_high(tag, t):
                act.wait_ge(sem(f"{tag}_turned"), t + 1)
                act.activation(gt_hi[:, :, :].rearrange("p k n -> p (k n)"),
                               ps[:, 0:2, :].rearrange("p a b -> p (a b)")[:, 0:D], ACT.Copy
                               ).then_inc(sem(f"{tag}_tokens_high"), 1)

            def experts(tag):
                act.wait_ge(sem(f"{tag}_records_out"), 16 * NT * PICKS[tag])
                act.dma_start(table[:, 0:TABLE_COLS[tag], :], table_dram[tag].rearrange("(p t) f -> p t f", p=128)
                              ).then_inc(sem(f"{tag}_table_in"), 16)
                tokens_high(tag, 0)
                act.wait_ge(sem(f"{tag}_table"), 1)

                def tile(x, t, nxt=lambda *parts: None):
                    for hc in range(KH):
                        act.wait_ge(sem(f"{tag}_h_full"), KH * t + hc + 1)
                        p = ps[:, 6 + hc % 2, 0:128]
                        if tag == "m0":
                            act.activation(ht_hi[:, hc, :], p, ACT.Relu).then_inc(sem("m0_h_high"), 1)
                        else:
                            b = b1_cols[:, x * KH + hc:x * KH + hc + 1]
                            act.activation(gelu32[:, hc, :], p, ACT.Gelu, bias=b)
                            act.activation(ht_hi[:, hc, :], p, ACT.Gelu, bias=b).then_inc(sem("m1_h_high"), 1)
                        if hc < 2:
                            nxt(hc)
                    tokens_high(tag, t + 1)
                    nxt(2)
                    act.wait_ge(sem(f"{tag}_o_full"), 2 * t + 1)
                    act.wait_ge(sem(f"{tag}_out_free"), t + 1)
                    act.activation(row(out_ring, t % 2, 0, 384, 128), ps[:, 4, 0:384], ACT.Copy,
                                   scale=slot_gate[:, bass.ds(t, 1)]).then_inc(sem(f"{tag}_o_left"), 1)
                    nxt(3, 4, 5)

                for x in range(EXPERTS):
                    lo = act.value_load(expert_start_i[0:1, x:x + 1], min_val=0, max_val=SLOT_TILES[tag])
                    hi = act.value_load(expert_start_i[0:1, x + 1:x + 2], min_val=1, max_val=SLOT_TILES[tag])
                    with act.Fori(lo, lo + 1) as t:
                        if x + 1 < EXPERTS:
                            tile(x, t, lambda *parts: split_high(tag, x + 1, parts))
                        else:
                            tile(x, t)
                    with act.If(lo + 1 < hi):
                        with act.Fori(lo + 1, hi) as t:
                            tile(x, t)
                act.wait_ge(sem(f"{tag}_o_left"), hi + 1)
                act.nop().then_inc(sem(f"{tag}_o_left"), SLOT_TILES[tag])
                act.wait_ge(sem(f"{tag}_scattered"), 16 * SLOT_TILES[tag])
                for h in range(2):
                    for c, back in enumerate((first_back, second_back)[:PICKS[tag]]):
                        act.dma_start(back[:TP, 5 * h:5 * h + 5, :],
                                      moe_dram[tag][c * N + 5 * h * TP:c * N + (5 * h + 5) * TP, :]
                                      .rearrange("(t p) d -> p t d", p=TP)).then_inc(sem(f"{tag}_back{h}"), 16)

            act.wait_ge(sem("adj_first"), PACKED_OVER)
            transposed("n1", KD, ACT.Copy, "m0")
            for g in (first_part - 2, first_part - 1):
                act.wait_ge(sem(pieces[g][3]), pieces[g][4])
            act.wait_ge(sem("soft_in"), 1)
            act.activation(soft[:TP, :, :], logit[:TP, :, :], ACT.Exp).then_inc(sem("soft_exp"), 1)
            split_high("m0", 0, range(6))
            experts("m0")
            transposed("n2", KD, ACT.Copy)
            act.wait_ge(sem("t_high"), turned_before("n2") + 2 * NT)
            act.dma_start(bias_b[:TP, 0:D], row_bias("gcn_b")).then_inc(sem("bias_in"), 16)
            for c in range(2):
                if c:
                    act.wait_ge(sem("gz_full"), NT)
                with act.Fori(0, NT // 2) as i:
                    for u in range(2):
                        m = 2 * i + u
                        act.wait_ge(sem("gy_full"), NT * c + m + 1)
                        act.activation(row(y_hi, m, 0, 384), ps[:TP, u, 0:384], ACT.Copy,
                                       scale=dinv[:TP, bass.ds(m, 1)]).then_inc(sem("gy_high"), 1)
            act.wait_ge(sem("gz_free"), 2 + 2 * NT)
            act.dma_start(x3_dram.rearrange("(t p) d -> p t d", p=TP), acc[:TP, :, 0:D]).then_inc(sem("x3_out"), 16)
            act.dma_start(bias_b[:TP, 0:D], row_bias("v_b")).then_inc(sem("bias_in"), 16)
            act.dma_start(ln_w[:TP, :], row_bias("n1_w")).then_inc(sem("affine_in"), 16)
            act.dma_start(ln_b[:TP, :], row_bias("n1_b")).then_inc(sem("affine_in"), 16)
            transposed("n4", KD, ACT.Copy)
            for c in range(2):
                with act.Fori(0, NT // 2) as i:
                    for u in range(2):
                        m = 2 * i + u
                        act.wait_ge(sem("v_biased"), NT * c + m + 1)
                        act.activation(v_parts[:TP, bass.ds(m, 1), 6 * c:6 * c + 6, 0:HD].rearrange("p o h d -> p (o h) d"),
                                       p32_flat[:TP, 384 * u:384 * (u + 1)].rearrange("p (h d) -> p h d", d=HD),
                                       ACT.Copy).then_inc(sem("v_high"), 1)
            act.wait_ge(sem("v_low"), 2 + 2 * NT)
            act.dma_start(bias_b[:TP, 0:D], row_bias("proj_b")).then_inc(sem("bias_in"), 16)
            act.nop().then_inc(sem("exp_done"), 5)

            def queries_keys(j):
                job = 6 * j
                for which in range(2):
                    for c0, w in NODE_COLS:
                        job += 1
                        act.wait_ge(sem("qk_full"), job)
                        if job > 1:
                            act.wait_ge(sem("qk_parts"), job - 1)
                        for hh in range(2):
                            P0 = slice(64 * hh, 64 * hh + 64)
                            p, b = ps[P0, (job - 1) % 2, 0:w], qk_bias[P0, 6 * which + j:6 * which + j + 1]
                            act.activation((q_a, k_a)[which][0:64, hh, c0:c0 + w], p, ACT.Identity, bias=b)
                            act.activation(qk32[0:64, hh, 0:w], p, ACT.Identity, bias=b).then_inc(sem("qk_moved"), 1)

            queries_keys(0)
            for j in range(HEADS // 2):
                for h2 in range(2):
                    act.wait_ge(sem("max_rows"), 2 * j + h2 + 1)
                    act.activation(q_b[64:65, h2, 0:1000].rearrange("p (a b) -> p a b", b=500),
                                   ps[64:65, 3 * h2:3 * h2 + 2, 0:500], ACT.Copy, scale=-1.0)
                    act.activation(q_b[64:65, h2, 1000:N], ps[64:65, 3 * h2 + 2, 0:250], ACT.Copy,
                                   scale=-1.0).then_inc(sem("max_set"), 1)
                with act.Fori(0, NT // 2) as qc:
                    for h2 in range(2):
                        n = 10 * j + 2 * qc + h2
                        act.wait_ge(sem("pv_full"), 2 * n + 2)
                        for kp in range(5):
                            p = ps[:TP, kp, 0:2 * QC]
                            act.wait_ge(sem("s_full"), 5 * n + kp + 1)
                            act.activation(p_hi[:TP, h2, 2 * kp:2 * kp + 2, 0:QC], p.rearrange("p (a b) -> p a b", b=QC),
                                           ACT.Exp, scale=HD ** -0.5).then_inc(sem("p_high"), 1)
                            act.wait_ge(sem("p_low"), 5 * n + kp + (1 if 5 * h2 + kp < 2 else -1))
                            act.activation(p32[:TP, (5 * h2 + kp) % 4, :], p,
                                           ACT.Exp, scale=HD ** -0.5).then_inc(sem("exp_done"), 1)
                if j + 1 < HEADS // 2:
                    queries_keys(j + 1)
                for t, (c0, w) in enumerate(((0, 500), (500, 500), (1000, 250))):
                    act.wait_ge(sem("ot_full"), 3 * j + t + 1)
                    if j:
                        act.wait_ge(sem("pr_full"), 2 * NT * j)
                    act.activation(ot_hi[:, c0:c0 + w], ps[:, 5 + t, 0:w], ACT.Copy).then_inc(sem("ot_high"), 1)
            act.wait_ge(sem("pr_free"), 4 + 2 * NT * 6)
            act.dma_start(ln_w[:TP, :], row_bias("n2_w")).then_inc(sem("affine_in"), 16)
            act.dma_start(ln_b[:TP, :], row_bias("n2_b")).then_inc(sem("affine_in"), 16)
            act.dma_start(router32[:, :, :], a["w_gate"].rearrange("(k p) n -> p k n", p=128)).then_inc(sem("gate_in"), 16)
            transposed("n5", KD, ACT.Copy, "m1")
            act.wait_ge(sem("soft_in"), 2)
            act.activation(share[:TP, 1, :], share[:TP, 0, :], ACT.Exp).then_inc(sem("soft_exp"), 1)
            split_high("m1", 0, range(6))
            act.dma_start(b2_rows[:, :], a["b2x"]).then_inc(sem("b2_in"), 16)
            for q in range(3):
                act.wait_ge(sem("gt_full"), q + 1)
                w = 500 if q < 2 else 250
                act.activation(gate_t[:, 500 * q:500 * q + w], ps[0:EXPERTS, 4 + q, 0:w], ACT.Copy).then_inc(sem("gt_done"), 1)
            experts("m1")
            for h in range(2):
                act.wait_ge(sem("m1_added"), h + 1)
                act.dma_start(out[5 * h * TP:(5 * h + 5) * TP, :].rearrange("(t p) d -> p t d", p=TP),
                              acc[:TP, 5 * h:5 * h + 5, 0:D]).then_inc(sem("stored"), 16)
            act.wait_ge(sem("stored"), 32)

        @block.vector
        def _(dve):
            count = [0]

            def then(ins):
                count[0] += 1
                ins.then_inc(sem("dve_step"), 1)
                dve.wait_ge(sem("dve_step"), count[0])

            def signal(ins, name, value):
                ins.then_inc(sem(name), 1)
                dve.wait_ge(sem(name), value)

            def bcast(col, n):
                return col.to_broadcast([TP, NT, n])

            dve.memset(zeros[:, :], 0.0)
            dve.memset(ones16[:, :], 1.0)
            dve.memset(slot[:EP, :], 0.0)
            dve.wait_ge(sem("iota_ready"), 4)
            for c in range(1, 3):
                dve.tensor_scalar(pidx[:, c:c + 1], pidx[:, 0:1], float(128 * c), None, ALU.add)
            then(dve.tensor_scalar(ident[:, :], iota_n[:, :128], pidx[:, 0:1], None, ALU.is_equal))
            dve.memset(one_of[:, :], 1.0)
            dve.tensor_scalar(ident16[:, :], iota_n[:, :128], pidx[:, 0:1], None, ALU.is_equal)
            dve.tensor_scalar(before[:, :], iota_n[:, :128], pidx[:, 0:1], None, ALU.is_gt)
            dve.tensor_scalar(below[:, 0, :128], iota_n[:, :128], pidx[:, 0:1], None, ALU.is_gt)
            for c in range(3):
                dve.tensor_scalar(below[:, 1 + c, :], iota_n[:, :EJ], pidx[:, c:c + 1], None, ALU.is_gt)
            dve.wait_ge(sem("edges_in"), 48)
            then(dve.tensor_scalar(src_tile[:EP, :], e_src[:EP, :], float(TP), None, ALU.is_ge))
            for k in range(2, NT):
                then(dve.scalar_tensor_tensor(src_tile[:EP, :], e_src[:EP, :], float(TP * k), src_tile[:EP, :],
                                              ALU.is_ge, ALU.add))
            dve.scalar_tensor_tensor(bucket[:EP, :], e_typ[:EP, :], float(NT), src_tile[:EP, :], ALU.mult, ALU.add)
            then(dve.scalar_tensor_tensor(src_loc[:EP, :], src_tile[:EP, :], float(-TP), e_src[:EP, :], ALU.mult, ALU.add))
            then(dve.scalar_tensor_tensor(packed_f[:EP, :], e_dst[:EP, :], 128.0, src_loc[:EP, :], ALU.mult, ALU.add))
            dve.tensor_copy(packed[:EP, :], packed_f[:EP, :])
            for b in range(NBUCKET):
                ins = dve.tensor_scalar(mask[:EP, b, :], bucket[:EP, :], float(b), None, ALU.is_equal)
            then(ins)
            then(dve.tensor_reduce(tiles_f[:EP, :], mask[:EP, :, :], AX_X, ALU.add))
            signal(dve.tensor_copy(row_cnt[:EP, :], tiles_f[:EP, :]), "row_counts", 1)
            dve.wait_ge(sem("col_counts"), 1)
            dve.tensor_copy(col_cnt[:, :2, :], ps[:, 0, 0:2 * NBUCKET].rearrange("p (c b) -> p c b", c=2))
            dve.tensor_copy(col_cnt[:64, 2, :], ps[:64, 0, 2 * NBUCKET:3 * NBUCKET])
            signal(dve.tensor_scalar(tiles_f[:, :], ps[:, 1, 0:NBUCKET], 127.0, None, ALU.add), "col_counts_in", 1)
            then(dve.tensor_copy(tiles_i[:, :], tiles_f[:, :]))
            then(dve.tensor_scalar(tiles_i[:, :], tiles_i[:, :], 7, None, ALU.arith_shift_right))
            then(dve.tensor_copy(tiles_f[:, :], tiles_i[:, :]))
            then(dve.tensor_scalar(tiles_f[:, :], tiles_f[:, :], float(UNIT - 1), 683.0, ALU.add, ALU.mult))
            then(dve.tensor_copy(tiles_i[:, :], tiles_f[:, :]))
            then(dve.tensor_scalar(tiles_i[:, :], tiles_i[:, :], 11, None, ALU.arith_shift_right))
            dve.tensor_scalar(tiles_f[:, :], tiles_i[:, :], 1.0, None, ALU.max)
            then(dve.memset(tstart[:, 0:1], 0.0))
            for b in range(NBUCKET):
                then(dve.tensor_tensor(tstart[:, b + 1:b + 2], tstart[:, b:b + 1], tiles_f[:, b:b + 1], ALU.add))
            dve.tensor_copy(tstart_i[:, :], tstart[:, :]).then_inc(sem("starts_ready"), 1)
            then(dve.tensor_scalar(first_slot[:, :], tstart[:, :NBUCKET], 128.0 * UNIT, None, ALU.mult))
            for b in range(NBUCKET):
                dve.wait_ge(sem("ranks"), b + 1)
                then(dve.scalar_tensor_tensor(slot_part[:EP, b % 2, :], ps[:EP, 2 + b % 4, :EJ], first_slot[:EP, b:b + 1],
                                              mask[:EP, b, :], ALU.add, ALU.mult))
                signal(dve.tensor_tensor(slot[:EP, :], slot[:EP, :], slot_part[:EP, b % 2, :], ALU.add), "rank_used", b + 1)
            then(dve.tensor_copy(slot_i[:EP, :], slot[:EP, :]))
            dve.tensor_scalar(tile_i[:EP, :], slot_i[:EP, :], 7, None, ALU.arith_shift_right)
            then(dve.tensor_scalar(lane_i[:EP, :], slot_i[:EP, :], 127, None, ALU.bitwise_and))
            then(dve.tensor_scalar(lane_f[:EP, :], lane_i[:EP, :], float(ETILES), None, ALU.mult))
            then(dve.tensor_tensor(addr_f[:EP, :], lane_f[:EP, :], tile_i[:EP, :], ALU.add))
            dve.tensor_copy(addr[:EP, :], addr_f[:EP, :]).then_inc(sem("addr_ready"), 1)
            def normalize_stats(tag):
                for m in range(NT):
                    for h in range(2):
                        ins = dve.bn_stats(stats[:TP, m, h, :], acc[:TP, m, 384 * h:384 * (h + 1)])
                then(ins)
                for m in range(NT):
                    ins = dve.bn_aggr(meanvar[:TP, m, :], stats[:TP, m, :, :])
                then(ins)
                dve.tensor_scalar(rstd[:TP, :], meanvar[:TP, :, 1:2].rearrange("p m o -> p (m o)"), 1e-5, None, ALU.add
                                  ).then_inc(sem("variance"), 1)
                dve.wait_ge(sem("rstd_ready"), 1 + powers(tag))

            def normalized(dst, m):
                return dve.tensor_scalar(dst, acc[:TP, m, 0:D], meanvar[:TP, m, 0:1], rstd[:TP, m:m + 1],
                                         ALU.subtract, ALU.mult)

            def low_parts(tag, m, K, relu):
                for q, (k0, k1) in enumerate(((0, 4), (4, K))):
                    job = 2 * m + q
                    dve.wait_ge(sem("t_high"), turned_before(tag) + job + 1)
                    p = ps[:, 4 + job % 4, 0:(k1 - k0) * TP].rearrange("p (k n) -> p k n", n=TP)
                    hi = hT_hi[:, k0:k1, m * TP:(m + 1) * TP]
                    lo = hT_lo[:, k0:k1, m * TP:(m + 1) * TP]
                    if relu:
                        ins = dve.scalar_tensor_tensor(lo, p, 0.0, hi, ALU.max, ALU.subtract)
                    else:
                        ins = dve.tensor_tensor(lo, p, hi, ALU.subtract)
                    ins.then_inc(sem("t_free"), 1)

            def normalized_transposed(tag, affine=False, pack=None):
                normalize_stats(tag)
                if affine:
                    dve.wait_ge(sem("affine_in"), 32 if tag == "n4" else 64)
                for m in range(NT + 1):
                    if m < NT:
                        if m >= 2:
                            dve.wait_ge(sem("t_full"), turned_before(tag) + 2 * (m - 1))
                        if m >= 2 and pack:
                            dve.wait_ge(sem("pack_low"), NT * nth(pack) - NT + m - 1)
                        s = stage[:TP, m % 2, :]
                        ins = normalized(s, m)
                        if affine:
                            then(ins)
                            then(dve.tensor_tensor(s, s, ln_w[:TP, :], ALU.mult))
                            ins = dve.tensor_tensor(s, s, ln_b[:TP, :], ALU.add)
                        ins.then_inc(sem("staged"), 1)
                    if m and pack:
                        i = m - 1
                        dve.wait_ge(sem("staged"), staged_before(tag) + i + 1)
                        dve.wait_ge(sem("pack_high"), NT * nth(pack) - NT + i + 1)
                        dve.tensor_tensor(packed_rows[:TP, i % 3, 1, :], stage[:TP, i % 2, :], packed_rows[:TP, i % 3, 0, :],
                                          ALU.subtract).then_inc(sem(f"pack_low"), 1)
                    if m:
                        low_parts(tag, m - 1, KD, False)

            dve.wait_ge(sem("x_in"), 64)
            dve.wait_ge(sem("consts_in"), 64)
            normalize_stats("n0")
            for m in range(NT):
                normalized(acc[:TP, m, 0:D], m)
            then(dve.tensor_copy(type_f[:TP, :], node_type[:TP, :]))
            for t in range(3):
                then(dve.tensor_scalar(share[:TP, t, :], type_f[:TP, :], float(t), None, ALU.is_equal))
            for m in range(NT):
                e = acc[:TP, m, D:896]
                then(dve.tensor_scalar(e, bias_b[:TP, 0:128], share[:TP, 0, m:m + 1], None, ALU.mult))
                for t in (1, 2):
                    then(dve.scalar_tensor_tensor(e, bias_b[:TP, 128 * t:128 * (t + 1)], share[:TP, t, m:m + 1], e,
                                                  ALU.mult, ALU.add))
            dve.nop().then_inc(sem("h0_ready"), 1)
            for m in range(NT):
                low_parts("t0", m, 7, False)

            def early_split(g):
                _, k, n, _, _ = pieces[g]
                dve.wait_ge(sem("w_high"), g + 1)
                dve.tensor_tensor(wlo[:, g % 2, 0:k * n], wraw[:, 0:k * n], whi[:, g % 2, 0:k * n], ALU.subtract
                                  ).then_inc(sem("w_split"), 1)

            def relational(L, when="late"):
                K, O, nm = LAYERS[L]
                Oc = O // 2
                dve.wait_ge(sem("bias_in"), 16 * (L + 1))
                for n, c, r, g, product, aggregation, stored in parts_of(L, when):
                    c0, c1 = c * Oc, (c + 1) * Oc
                    y_hi_, y_lo_ = (early_hi[r], early_lo[r]) if stored else (y_hi, y_lo)
                    if stored and product:
                        if r == 0:
                            early_split(2)
                        if r < 2:
                            early_split(3 + r)
                    with dve.Fori(0, NT // 2) if product else ExitStack() as i:
                        for u in range(2 if product else 0):
                            m = 2 * i + u
                            if r is None:
                                dve.wait_ge(sem("y_full"), NT * (8 * L + n) + m + 1)
                                dve.tensor_tensor(row(acc, m, c0, c1), ps[:TP, u, 0:Oc], bias_b[:TP, c0:c1], ALU.add
                                                  ).then_inc(sem("y_free"), 1)
                            else:
                                dve.wait_ge(sem("y_high"), NT * (6 * L + 3 * c + r) + m + 1)
                                dve.tensor_tensor(row(y_lo_, m, 0, Oc), ps[:TP, u, 0:Oc], row(y_hi_, m, 0, Oc), ALU.subtract
                                                  ).then_inc(sem("y_free"), 1)
                    if aggregation:
                        z = 3 * c + r
                        dve.wait_ge(sem("y_free"), 2 + NT * (8 * L + n + 1))
                        dve.wait_ge(sem("z_free"), 2 + NT * (6 * L + z))
                        with dve.Fori(0, NT // 2) as i:
                            for u in range(2):
                                m = 2 * i + u
                                dve.wait_ge(sem("z_full"), NT * (6 * L + z) + m + 1)
                                dve.scalar_tensor_tensor(row(acc, m, c0, c1), ps[:TP, 2 + u, 0:Oc],
                                                         row(inv_cnt, m, r, r + 1), row(acc, m, c0, c1),
                                                         ALU.mult, ALU.add).then_inc(sem("z_free"), 1)
                if when == "late":
                    dve.wait_ge(sem("z_free"), 2 + 6 * NT * (L + 1))

            dve.nop().then_inc(sem("y_free"), 2)
            dve.nop().then_inc(sem("z_free"), 2)
            relational(0, "early")
            dve.wait_ge(sem("sorted_in"), 16)
            dve.tensor_scalar(sorted_i[:, 0, :], sorted_p[:, :], 7, None, ALU.arith_shift_right)
            then(dve.tensor_scalar(sorted_i[:, 1, :], sorted_p[:, :], 127, None, ALU.bitwise_and))
            then(dve.tensor_copy(sorted_f[:, :, :], sorted_i[:, :, :]))
            with dve.Fori(0, NBUCKET) as b:
                lo = dve.value_load(tstart_i[0:1, bass.ds(b, 1)], min_val=0, max_val=UNITS - 1)
                hi = dve.value_load(tstart_i[0:1, bass.ds(b + 1, 1)], min_val=1, max_val=UNITS)
                with dve.Fori(lo, hi) as t:
                    for u in range(UNIT):
                        dve.wait_ge(sem("onehot_free"), UNIT * t + u + 1)
                        dve.tensor_scalar(oh_src[:, u, :], iota_n[:, :TP],
                                          sorted_f[:, 1, bass.ds(UNIT * t + u, 1)], None, ALU.is_equal)
                        dve.tensor_scalar(oh_dst[:, u, :], iota_n[:, :],
                                          sorted_f[:, 0, bass.ds(UNIT * t + u, 1)], None, ALU.is_equal
                                          ).then_inc(sem("onehot_ready"), 1)

            dve.wait_ge(sem("adj_full"), NBUCKET)
            dve.memset(adj_all[:, NBUCKET * N:], 0.0)
            then(dve.memset(ones_col[:, :], 1.0))
            dve.nop().then_inc(sem("ones_ready"), 1)
            dve.wait_ge(sem("counts"), 1)
            cnt = ps[:TP, 7, 0:NBUCKET].rearrange("p (m r) -> p m r", r=NREL)
            then(dve.tensor_scalar(inv_cnt[:TP, :, :], cnt, 1.0, None, ALU.max))
            then(dve.reciprocal(inv_cnt[:TP, :, :], inv_cnt[:TP, :, :]))
            then(dve.scalar_tensor_tensor(inv_cnt[:TP, :, :], cnt, 1.0, inv_cnt[:TP, :, :], ALU.min, ALU.mult))
            then(dve.tensor_reduce(dinv[:TP, :], cnt, AX_X, ALU.add))
            dve.tensor_scalar(dinv[:TP, :], dinv[:TP, :], 1.0, None, ALU.add).then_inc(sem("variance"), 1)

            relational(0)
            for L in (1, 2):
                for m in range(NT):
                    low_parts(f"t{L}", m, LAYERS[L][0], True)
                relational(L)
            for m in range(NT):
                dve.wait_ge(sem(f"res_in{m // 5}"), 16)
                dve.scalar_tensor_tensor(acc[:TP, m, 0:D], acc[:TP, m, 0:D], 0.0, second_back[:TP, m, :], ALU.max, ALU.add
                                         ).then_inc(sem("res_sum"), 1)
            dve.wait_ge(sem("res_sum"), NT)

            def logits_in(tag):
                dve.wait_ge(sem("logits"), NT * nth(tag))
                then(dve.tensor_copy(logit[:TP, :, :], ps[:TP, 3, 0:NT * EXPERTS].rearrange("p (m e) -> p m e", e=EXPERTS)))
                for m in range(NT):
                    ins = dve.max(top_val[:TP, m, :], logit[:TP, m, :])
                then(ins)
                for m in range(NT):
                    ins = dve.max_index(top_idx[:TP, m, :], top_val[:TP, m, :], logit[:TP, m, :])
                then(ins)
                then(dve.tensor_copy(top_idx_f[:TP, :, :], top_idx[:TP, :, :]))

            def router_parts(tag, name, value):
                dve.wait_ge(sem(name), value)
                then(dve.tensor_copy(router_hi[:, :, :], router32[:, :, :]))
                dve.tensor_tensor(router_lo[:, :, :], router32[:, :, :], router_hi[:, :, :], ALU.subtract
                                  ).then_inc(sem("router"), 1)

            def slots(tag):
                picks = PICKS[tag]
                for c in range(picks):
                    for m in range(NT):
                        ins = dve.tensor_scalar(chosen[:TP, c, m, :], eye8[:TP, :], top_idx_f[:TP, m, c:c + 1], None,
                                                ALU.is_equal)
                then(ins)
                if picks == 1:
                    signal(dve.tensor_copy(chosen16[:TP, :, :], chosen[:TP, 0, :, :]), "chosen", nth(tag))
                else:
                    signal(dve.tensor_tensor(chosen16[:TP, :, :], chosen[:TP, 0, :, :], chosen[:TP, 1, :, :], ALU.add),
                           "chosen", nth(tag))
                dve.wait_ge(sem("ranked"), nth(tag))
                then(dve.tensor_scalar(expert_tiles_f[:, :], ps[:, 3, 0:EXPERTS], 127.0, None, ALU.add))
                then(dve.tensor_copy(expert_tiles_i[:, :], expert_tiles_f[:, :]))
                then(dve.tensor_scalar(expert_tiles_i[:, :], expert_tiles_i[:, :], 7, None, ALU.arith_shift_right))
                dve.tensor_scalar(expert_tiles_f[:, :], expert_tiles_i[:, :], 1.0, None, ALU.max)
                then(dve.memset(expert_start[:, 0:1], 0.0))
                for x in range(EXPERTS):
                    then(dve.tensor_tensor(expert_start[:, x + 1:x + 2], expert_start[:, x:x + 1],
                                           expert_tiles_f[:, x:x + 1], ALU.add))
                dve.tensor_copy(expert_start_i[:, :], expert_start[:, :])
                then(dve.tensor_scalar(expert_slot0[:, :], expert_start[:, 0:EXPERTS], 128.0, None, ALU.mult))
                for m in range(NT):
                    ins = dve.tensor_tensor(expert_slot[:TP, m, :], ps[:TP, 2, m * EXPERTS:(m + 1) * EXPERTS],
                                            expert_slot0[:TP, :], ALU.add)
                then(ins)
                for c in range(picks):
                    then(dve.tensor_tensor(picked_slot[:TP, :, :], chosen[:TP, c, :, :], expert_slot[:TP, :, :], ALU.mult))
                    then(dve.tensor_reduce(token_slot[:TP, c, :], picked_slot[:TP, :, :], AX_X, ALU.add))
                    s, tile, lane = (token_slot_i[:TP, i, c, :] for i in range(3))
                    then(dve.tensor_copy(s, token_slot[:TP, c, :]))
                    dve.tensor_scalar(tile, s, 7, None, ALU.arith_shift_right)
                    then(dve.tensor_scalar(lane, s, 127, None, ALU.bitwise_and))
                    then(dve.tensor_copy(token_addr_f[:TP, c, :], lane))
                    then(dve.scalar_tensor_tensor(token_addr_f[:TP, c, :], token_addr_f[:TP, c, :], float(TABLE_COLS[tag]),
                                                  tile, ALU.mult, ALU.add))
                    dve.tensor_copy(token_addr[:TP, c, :], token_addr_f[:TP, c, :])
                    col = lambda f: records[:TP, c, :, f:f + 1].rearrange("p m o -> p (m o)")
                    dve.tensor_copy(col(0), token[:TP, :])
                    dve.tensor_scalar(col(1), token[:TP, :], float(c * N), None, ALU.add)
                    dve.tensor_copy(col(2), share[:TP, 0 if tag == "m0" else 2 + c, :])
                    ins = dve.memset(records[:TP, c, :, 3:4], 0.0)
                then(ins)
                dve.nop().then_inc(sem("records"), 1)

            def split_low(tag, x, parts):
                for i in parts:
                    name = ("w1", "w2")[i // 3]
                    c = slice(D * (i % 3), D * (i % 3 + 1))
                    raw, hi, lo = ((wraw, whi, wlo), (w2_raw, w2_hi, w2_lo))[i // 3]
                    dve.wait_ge(sem(f"{name}_high"), 3 * (block_of(tag) + x) + i % 3 + 1)
                    dve.tensor_tensor(lo[:, x % 2, c], raw[:, c], hi[:, x % 2, c], ALU.subtract
                                      ).then_inc(sem(f"{name}_split"), 1)

            def tokens_low(tag, t):
                dve.wait_ge(sem(f"{tag}_turned"), t + 1)
                dve.tensor_copy(gt_lo[:, :, :].rearrange("p k n -> p (k n)"),
                                ps[:, 2:4, :].rearrange("p a b -> p (a b)")[:, 0:D]
                                ).then_inc(sem(f"{tag}_tokens_low"), 1)

            def experts(tag):
                dve.wait_ge(sem(f"{tag}_table_in"), 16)
                col = lambda f: table[:, 0:TABLE_COLS[tag], f:f + 1].rearrange("p t o -> p (t o)")
                for t, f in ((gather_row, 0), (scatter_row, 1), (slot_gate, 2)):
                    ins = dve.tensor_copy(t[:, 0:TABLE_COLS[tag]], col(f))
                then(ins)
                dve.nop().then_inc(sem(f"{tag}_table"), 1)
                dve.nop().then_inc(sem(f"{tag}_o_left"), 1)
                dve.nop().then_inc(sem(f"{tag}_o_right"), 1)
                tokens_low(tag, 0)

                def tile(t, nxt=lambda *parts: None):
                    for hc in range(KH):
                        dve.wait_ge(sem(f"{tag}_h_high"), KH * t + hc + 1)
                        h = ht_hi[:, hc, :]
                        if tag == "m0":
                            ins = dve.scalar_tensor_tensor(ht_lo[:, hc, :], ps[:, 6 + hc % 2, 0:128], 0.0, h,
                                                           ALU.max, ALU.subtract)
                        else:
                            ins = dve.tensor_tensor(ht_lo[:, hc, :], gelu32[:, hc, :], h, ALU.subtract)
                        ins.then_inc(sem(f"{tag}_h_low"), 1)
                        if hc < 2:
                            nxt(hc)
                    tokens_low(tag, t + 1)
                    nxt(2)
                    dve.wait_ge(sem(f"{tag}_o_full"), 2 * t + 2)
                    dve.wait_ge(sem(f"{tag}_out_free"), t + 1)
                    dve.tensor_scalar(row(out_ring, t % 2, 384, D, 128), ps[:, 5, 0:384], slot_gate[:, bass.ds(t, 1)],
                                      None, ALU.mult).then_inc(sem(f"{tag}_o_right"), 1)
                    nxt(3, 4, 5)

                for x in range(EXPERTS):
                    lo = dve.value_load(expert_start_i[0:1, x:x + 1], min_val=0, max_val=SLOT_TILES[tag])
                    hi = dve.value_load(expert_start_i[0:1, x + 1:x + 2], min_val=1, max_val=SLOT_TILES[tag])
                    with dve.Fori(lo, lo + 1) as t:
                        if x + 1 < EXPERTS:
                            tile(t, lambda *parts: split_low(tag, x + 1, parts))
                        else:
                            tile(t)
                    with dve.If(lo + 1 < hi):
                        with dve.Fori(lo + 1, hi) as t:
                            tile(t)
                dve.wait_ge(sem(f"{tag}_o_right"), hi + 1)
                dve.nop().then_inc(sem(f"{tag}_o_right"), SLOT_TILES[tag])
                if tag == "m1":
                    for m in range(NT):
                        for c in range(2):
                            dve.wait_ge(sem("gb_full"), 2 * m + c + 1)
                            av = acc[:TP, m, 384 * c:384 * (c + 1)]
                            dve.tensor_tensor(av, ps[:TP, c + 4 * (m % 2), 0:384], av, ALU.add).then_inc(sem("gb_free"), 1)
                    dve.wait_ge(sem("gb_free"), 2 * NT)
                for h in range(2):
                    dve.wait_ge(sem(f"{tag}_back{h}"), 16 * PICKS[tag])
                    for c, back in enumerate((first_back, second_back)[:PICKS[tag]]):
                        if c:
                            then(ins)
                        av = acc[:TP, 5 * h:5 * h + 5, 0:D]
                        ins = dve.tensor_tensor(av, av, back[:TP, 5 * h:5 * h + 5, :], ALU.add)
                    signal(ins, f"{tag}_added", h + 1)

            dve.wait_ge(sem("adj_first"), PACKED_OVER)
            router_parts("m0", "consts_in", 64)
            normalized_transposed("n1", pack="m0")
            logits_in("m0")
            dve.tensor_tensor(logit[:TP, :, :], logit[:TP, :, :], top_val[:TP, :, 0:1].to_broadcast([TP, NT, EXPERTS]),
                              ALU.subtract).then_inc(sem("soft_in"), 1)
            dve.wait_ge(sem("soft_exp"), 1)
            then(dve.tensor_reduce(share[:TP, 0, :], soft[:TP, :, :], AX_X, ALU.add))
            then(dve.reciprocal(share[:TP, 0, :], share[:TP, 0, :]))
            slots("m0")
            split_low("m0", 0, range(6))
            experts("m0")

            normalized_transposed("n2")
            dve.wait_ge(sem("bias_in"), 16 * 4)
            for m in range(NT):
                ins = dve.tensor_tensor(acc[:TP, m, 0:D], acc[:TP, m, 0:D], bias_b[:TP, 0:D], ALU.add)
            then(ins)
            dve.nop().then_inc(sem("gy_free"), 2)
            dve.nop().then_inc(sem("gz_free"), 2)
            for c in range(2):
                c0, c1 = 384 * c, 384 * (c + 1)
                with dve.Fori(0, NT // 2) as i:
                    for u in range(2):
                        m = 2 * i + u
                        dve.wait_ge(sem("gy_high"), NT * c + m + 1)
                        dve.scalar_tensor_tensor(row(y_lo, m, 0, 384), ps[:TP, u, 0:384], dinv[:TP, bass.ds(m, 1)],
                                                 row(y_hi, m, 0, 384), ALU.mult, ALU.subtract).then_inc(sem("gy_free"), 1)
                with dve.Fori(0, NT // 2) as i:
                    for u in range(2):
                        m = 2 * i + u
                        dve.wait_ge(sem("gz_full"), NT * c + m + 1)
                        dve.scalar_tensor_tensor(row(acc, m, c0, c1), ps[:TP, 2 + u, 0:384], dinv[:TP, bass.ds(m, 1)],
                                                 row(acc, m, c0, c1), ALU.mult, ALU.add).then_inc(sem("gz_free"), 1)
            dve.wait_ge(sem("gz_free"), 2 + 2 * NT)

            normalize_stats("n3")
            dve.wait_ge(sem("x3_out"), 16)
            for m in range(NT):
                ins = normalized(acc[:TP, m, 0:D], m)
            then(ins)
            normalized_transposed("n4", affine=True)
            dve.wait_ge(sem("t_full"), turned_before("n4") + 2 * NT)
            dve.memset(v_parts[:TP, :, :, HD:HD + 1], 1.0)
            for t in (p_hi, p_lo):
                dve.memset(t[:TP, :, :, QC:QC + 6], 0.0)
            dve.memset(q_b[64:96, :, :], 0.0)
            then(dve.memset(k_b[64:96, :, :], 0.0))
            signal(dve.memset(k_b[64:65, :, :], 1.0), "ones_set", 1)
            dve.wait_ge(sem("bias_in"), 16 * 5)
            dve.nop().then_inc(sem("v_low"), 2)
            dve.nop().then_inc(sem("p_low"), 2)
            dve.nop().then_inc(sem("o_free"), 2)
            dve.nop().then_inc(sem("pr_free"), 4)
            dve.nop().then_inc(sem("max_free"), 2)
            for c in range(2):
                with dve.Fori(0, NT // 2) as i:
                    for u in range(2):
                        m = 2 * i + u
                        dve.wait_ge(sem("v_full"), NT * c + m + 1)
                        v32 = p32_flat[:TP, 384 * u:384 * (u + 1)]
                        dve.wait_ge(sem("v_low"), NT * c + m + 1)
                        dve.tensor_tensor(v32, ps[:TP, u, 0:384], bias_b[:TP, 384 * c:384 * (c + 1)], ALU.add
                                          ).then_inc(sem("v_biased"), 1)
                        dve.wait_ge(sem("v_high"), NT * c + m + 1)
                        vp = lambda lo, hi: v_parts[:TP, bass.ds(m, 1), 6 * c:6 * c + 6, lo:hi].rearrange("p o h d -> p (o h) d")
                        dve.tensor_tensor(vp(HD + 1, 129), v32.rearrange("p (h d) -> p h d", d=HD), vp(0, HD), ALU.subtract
                                          ).then_inc(sem("v_low"), 1)
            def queries_keys(j):
                job = 6 * j
                for which in range(2):
                    for c0, w in NODE_COLS:
                        job += 1
                        dve.wait_ge(sem("qk_moved"), 2 * job)
                        hi = (q_a, k_a)[which]
                        lo = q_b[0:64, :, c0:c0 + w] if which == 0 else k_a[64:128, :, c0:c0 + w]
                        dup = q_a[64:128, :, c0:c0 + w] if which == 0 else k_b[0:64, :, c0:c0 + w]
                        dve.tensor_copy(dup, hi[0:64, :, c0:c0 + w])
                        dve.tensor_tensor(lo, qk32[0:64, :, 0:w], hi[0:64, :, c0:c0 + w], ALU.subtract
                                          ).then_inc(sem("qk_parts"), 1)

            dve.wait_ge(sem("bias_in"), 16 * 6)
            for m in range(NT):
                ins = dve.tensor_tensor(acc[:TP, m, 0:D], acc[:TP, m, 0:D], bias_b[:TP, 0:D], ALU.add)
            then(ins)
            queries_keys(0)
            for j in range(HEADS // 2):
                for h2 in range(2):
                    with dve.Fori(0, NT // 2) as i:
                        for u in range(2):
                            t = 2 * i + u
                            dve.wait_ge(sem("max_full"), (2 * j + h2) * NT + t + 1)
                            dve.reduce_max(row_max[:TP, h2, bass.ds(t, 1)],
                                           ps[:TP, 3 * u:3 * u + 3, :].rearrange("p a b -> p (a b)")[:, :N], AX_X
                                           ).then_inc(sem("max_free"), 1)
                def p_low_parts(qc, h2):
                    n = 10 * j + 2 * qc + h2
                    for kp in range(5):
                        dve.wait_ge(sem("exp_done"), 5 * n + kp + 6)
                        dve.tensor_tensor(p_lo[:TP, h2, 2 * kp:2 * kp + 2, 0:QC],
                                          p32[:TP, (5 * h2 + kp) % 4, :].rearrange("p (a b) -> p a b", b=QC),
                                          p_hi[:TP, h2, 2 * kp:2 * kp + 2, 0:QC],
                                          ALU.subtract).then_inc(sem("p_low"), 1)

                def o_out(qc, h2):
                    n = 10 * j + 2 * qc + h2
                    for u in range(2):
                        dve.wait_ge(sem("pv_full"), 2 * n + u + 5)
                        dve.reciprocal(recip[:TP, u:u + 1], ps[:TP, 5 + u, HD:HD + 1]).then_inc(sem("o_recip"), 1)
                        dve.wait_ge(sem("o_recip"), 2 * n + u + 1)
                        dve.tensor_scalar(row(o_pair, 2 * qc + u, 64 * h2, 64 * h2 + 64), ps[:TP, 5 + u, 0:HD],
                                          recip[:TP, u:u + 1], None, ALU.mult).then_inc(sem("o_free"), 1)

                p_low_parts(0, 0)
                with dve.Fori(0, NT // 2 - 1) as qc:
                    p_low_parts(qc, 1)
                    o_out(qc, 0)
                    p_low_parts(qc + 1, 0)
                    o_out(qc, 1)
                p_low_parts(NT // 2 - 1, 1)
                o_out(NT // 2 - 1, 0)
                o_out(NT // 2 - 1, 1)
                if j + 1 < HEADS // 2:
                    queries_keys(j + 1)
                for t, (c0, w) in enumerate(((0, 500), (500, 500), (1000, 250))):
                    dve.wait_ge(sem("ot_high"), 3 * j + t + 1)
                    dve.tensor_tensor(ot_lo[:, c0:c0 + w], ps[:, 5 + t, 0:w], ot_hi[:, c0:c0 + w], ALU.subtract
                                      ).then_inc(sem("ot_low"), 1)
                if j:
                    dve.wait_ge(sem("pr_free"), 4 + 2 * NT * j)
                with dve.Fori(0, NT // 2) as i:
                    for u in range(2):
                        m = 2 * i + u
                        for c in range(2):
                            q = 2 * NT * j + 2 * m + c
                            dve.wait_ge(sem("pr_full"), q + 1)
                            av = row(acc, m, 384 * c, 384 * (c + 1))
                            dve.tensor_tensor(av, ps[:TP, 3 + 2 * u + c, 0:384], av, ALU.add).then_inc(sem("pr_free"), 1)
            dve.wait_ge(sem("pr_free"), 4 + 2 * NT * 6)

            router_parts("m1", "gate_in", 16)
            normalized_transposed("n5", affine=True, pack="m1")
            logits_in("m1")
            dve.tensor_tensor(share[:TP, 0, :], top_val[:TP, :, 1:2].rearrange("p m o -> p (m o)"),
                              top_val[:TP, :, 0:1].rearrange("p m o -> p (m o)"), ALU.subtract).then_inc(sem("soft_in"), 1)
            dve.wait_ge(sem("soft_exp"), 2)
            then(dve.tensor_scalar(share[:TP, 2, :], share[:TP, 1, :], 1.0, None, ALU.add))
            then(dve.reciprocal(share[:TP, 2, :], share[:TP, 2, :]))
            then(dve.tensor_tensor(share[:TP, 3, :], share[:TP, 1, :], share[:TP, 2, :], ALU.mult))
            for m in range(NT):
                dve.tensor_scalar(gates[:TP, m, :], eye8[:TP, :], top_idx_f[:TP, m, 0:1], share[:TP, 2, m:m + 1],
                                  ALU.is_equal, ALU.mult)
                ins = dve.tensor_scalar(soft[:TP, m, :], eye8[:TP, :], top_idx_f[:TP, m, 1:2], share[:TP, 3, m:m + 1],
                                        ALU.is_equal, ALU.mult)
            then(ins)
            signal(dve.tensor_tensor(gates[:TP, :, :], gates[:TP, :, :], soft[:TP, :, :], ALU.add), "gates_ready", 1)
            slots("m1")
            split_low("m1", 0, range(6))
            for m in range(NT):
                dve.wait_ge(sem(f"last_in{m % 2}"), 16 * (m // 2 + 1))
                dve.tensor_tensor(acc[:TP, m, 0:D], acc[:TP, m, 0:D], again[:TP, m % 2, :], ALU.add
                                  ).then_inc(sem("last_sum"), 1)
            dve.wait_ge(sem("last_sum"), NT)
            experts("m1")

        @block.tensor
        def _(pe):
            pe.wait_ge(sem("row_counts"), 1)
            for c in range(3):
                w = min(128, EJ - 128 * c)
                for b in range(NBUCKET):
                    pe.matmul(ps[:w, 0, c * NBUCKET + b:c * NBUCKET + b + 1], mask[:EP, b, c * 128:c * 128 + w],
                              ones16[:EP, 0:1], start=True, stop=True)
            pe.matmul(ps[:, 1, 0:NBUCKET], ones16[:EP, :128], row_cnt[:EP, :], start=True, stop=True
                      ).then_inc(sem("col_counts"), 1)
            pe.wait_ge(sem("col_counts_in"), 1)
            for b in range(NBUCKET):
                if b >= 4:
                    pe.wait_ge(sem("rank_used"), b - 3)
                p = ps[:EP, 2 + b % 4, :EJ]
                pe.matmul(p, below[:EP, 0, :EP], mask[:EP, b, :], start=True, stop=False)
                for c in range(3):
                    w = min(128, EJ - 128 * c)
                    ins = pe.matmul(p, col_cnt[:w, c, b:b + 1].to_broadcast([w, EP]), below[:w, 1 + c, :],
                                    start=False, stop=(c == 2))
                ins.then_inc(sem("ranks"), 1)
            pe.wait_ge(sem("rank_used"), NBUCKET)

            def weights(g):
                pe.wait_ge(sem("w_split"), g + 1)
                return w_of(g)

            def three(p, xs, ws, first=True, last=True):
                (xh, xl), (wh, wl) = xs, ws
                pe.matmul(p, xh, wh, start=first, stop=False)
                pe.matmul(p, xh, wl, start=False, stop=False)
                return pe.matmul(p, xl, wh, start=False, stop=last)

            def logits(tag, m):
                pe.wait_ge(sem("t_free"), turned_before(tag) + 2 * (m + 1))
                for k in range(KD):
                    c = slice(m * TP, (m + 1) * TP)
                    ins = three(ps[:TP, 3, m * EXPERTS:(m + 1) * EXPERTS], (hT_hi[:, k, c], hT_lo[:, k, c]),
                                (router_hi[:, k, :], router_lo[:, k, :]), k == 0, k == KD - 1)
                ins.then_inc(sem("logits"), 1)

            def transposed(tag, K, src, ready, router=None):
                job = 0
                for m in range(NT):
                    ready(m)
                    for k0, k1 in ((0, 4), (4, K)):
                        if job >= 4:
                            pe.wait_ge(sem("t_free"), turned_before(tag) + job - 3)
                        for k in range(k0, k1):
                            ins = pe.transpose(ps[:, 4 + job % 4, (k - k0) * TP:(k - k0 + 1) * TP], src(m, k), ident[:TP, :TP])
                        ins.then_inc(sem("t_full"), 1)
                        job += 1
                    if router and m:
                        logits(tag, m - 1)
                if router:
                    logits(tag, NT - 1)
                pe.wait_ge(sem("t_free"), turned_before(tag) + 2 * NT)

            def node_rows(K, m, w, p):
                wh, wl = w
                for k in range(K):
                    ins = three(p, (cols(hT_hi[:, k, :], m * TP, TP), cols(hT_lo[:, k, :], m * TP, TP)),
                                (wh[:, k, :], wl[:, k, :]), k == 0, k == K - 1)
                return ins

            def relational(L, when="late"):
                K, O, nm = LAYERS[L]
                Oc = O // 2
                for n, c, r, g, product, aggregation, stored in parts_of(L, when):
                    if product:
                        w = weights(g)
                    with pe.Fori(0, NT // 2) if product else ExitStack() as i:
                        for u in range(2 if product else 0):
                            m = 2 * i + u
                            pe.wait_ge(sem("y_free"), NT * (8 * L + n) + m + 1)
                            node_rows(K, m, w, ps[:TP, u, 0:Oc]).then_inc(sem("y_full"), 1)
                    if not aggregation:
                        continue
                    z = 3 * c + r
                    if stored:
                        pe.wait_ge(sem("early_back"), 32 * (r + 1))
                    else:
                        pe.wait_ge(sem("y_free"), 2 + NT * (8 * L + n + 1))
                    with pe.Fori(0, NT // 2) as i:
                        for u in range(2):
                            m = 2 * i + u
                            pe.wait_ge(sem("z_free"), NT * (6 * L + z) + m + 1)
                            for s in range(NT):
                                x = cols(adj[:, NT * r + s, :], m * TP, TP, TP)
                                pe.matmul(ps[:TP, 2 + u, 0:Oc], x, y_hi[:TP, s, 0:Oc], start=(s == 0), stop=False)
                                ins = pe.matmul(ps[:TP, 2 + u, 0:Oc], x, y_lo[:TP, s, 0:Oc], start=False, stop=(s == NT - 1))
                            ins.then_inc(sem("z_full"), 1)

            def from_acc(m, k):
                return acc[:TP, m, 128 * k:128 * (k + 1)]

            def once(*waits):
                def ready(m):
                    if m == 0:
                        for name, value in waits:
                            pe.wait_ge(sem(name), value)
                return ready

            transposed("t0", 7, from_acc, once(("h0_ready", 1)))
            relational(0, "early")
            pe.wait_ge(sem("y_free"), 2 + (2 + NREL) * NT)
            pe.nop().then_inc(sem("onehot_free"), UNIT)
            pe.wait_ge(sem("starts_ready"), 1)
            pe.wait_ge(sem("rank_used"), NBUCKET)
            with pe.Fori(0, NBUCKET // 2) as bh:
                for u in range(2):
                    b = 2 * bh + u
                    lo = pe.value_load(tstart_i[0:1, bass.ds(b, 1)], min_val=0, max_val=UNITS - 1)
                    hi = pe.value_load(tstart_i[0:1, bass.ds(b + 1, 1)], min_val=1, max_val=UNITS)
                    pe.wait_ge(sem("adj_free"), b + 1)
                    for c, (c0, w) in enumerate(BANKS3):
                        pe.matmul(ps[:TP, 3 * u + c, :w], zeros[:, :TP], zeros[:, :w], start=True, stop=False,
                                  skip_group_check=True)
                    with pe.Fori(lo, hi) as t:
                        for v in range(UNIT):
                            pe.wait_ge(sem("onehot_ready"), UNIT * t + v + 1)
                            for c, (c0, w) in enumerate(BANKS3):
                                ins = pe.matmul(ps[:TP, 3 * u + c, :w], oh_src[:, v, :],
                                                oh_dst[:, v, c0:c0 + w], start=False, stop=False,
                                                skip_group_check=True)
                            ins.then_inc(sem("onehot_free"), 1)
                    for c, (c0, w) in enumerate(BANKS3):
                        ins = pe.matmul(ps[:TP, 3 * u + c, :w], zeros[:, :TP], zeros[:, :w], start=False, stop=True,
                                        skip_group_check=True)
                    ins.then_inc(sem("adj_full"), 1)
            pe.wait_ge(sem("adj_free"), 2 + NBUCKET)
            pe.wait_ge(sem("ones_ready"), 1)
            for m in range(NT):
                for r in range(NREL):
                    for s in range(NT):
                        c0 = (NT * r + s) * N + m * TP
                        ins = pe.matmul(ps[:, 7, m * NREL + r:m * NREL + r + 1], adj_all[:TP, c0:c0 + 128],
                                        ones_col[:TP, 0:1], start=(s == 0), stop=(s == NT - 1))
            ins.then_inc(sem("counts"), 1)

            relational(0)
            for L in (1, 2):
                transposed(f"t{L}", LAYERS[L][0], from_acc, once(("z_free", 2 + 6 * NT * L)))
                relational(L)

            def staged(tag, router=None):
                def ready(m):
                    pe.wait_ge(sem("staged"), staged_before(tag) + m + 1)
                if router:
                    pe.wait_ge(sem("router"), nth(router))
                transposed(tag, KD, lambda m, k: stage[:TP, m % 2, 128 * k:128 * (k + 1)], ready, router)

            def ranks(tag):
                pe.wait_ge(sem("chosen"), nth(tag))
                flat = chosen16[:TP, :, :].rearrange("p m e -> p (m e)")
                pe.matmul(ps[:TP, 2, 0:NT * EXPERTS], before[:TP, 0:TP], flat, start=True, stop=False)
                for d in range(1, NT):
                    pe.matmul(ps[:TP, 2, d * EXPERTS:NT * EXPERTS], one_of[:TP, 0:TP], flat[:, 0:(NT - d) * EXPERTS],
                              start=False, stop=(d == NT - 1))
                for m in range(NT):
                    ins = pe.matmul(ps[:, 3, 0:EXPERTS], one_of[:TP, :], chosen16[:TP, m, :], start=(m == 0), stop=(m == NT - 1))
                ins.then_inc(sem("ranked"), 1)

            def turn_tokens(tag, t):
                pe.wait_ge(sem(f"{tag}_gathered"), 16 * (t + 1))
                for k in range(2 * KD):
                    lhs = row(rows_ring, t % 3, 128 * k, 128 * (k + 1), 128)
                    q = k % KD
                    ins = pe.matmul(ps[:, 2 * (k // KD) + q // 4, (q % 4) * 128:(q % 4 + 1) * 128], lhs, ident16[:, :], start=True, stop=True)
                ins.then_inc(sem(f"{tag}_turned"), 1)

            def experts(tag):
                turn_tokens(tag, 0)
                for x in range(EXPERTS):
                    w1h, w1l = (w[:, x % 2, 0:KD * HID].rearrange("p (k n) -> p k n", k=KD) for w in (whi, wlo))
                    w2h, w2l = (w[:, x % 2, :].rearrange("p (k n) -> p k n", k=KH) for w in (w2_hi, w2_lo))
                    lo = pe.value_load(expert_start_i[0:1, x:x + 1], min_val=0, max_val=SLOT_TILES[tag])
                    hi = pe.value_load(expert_start_i[0:1, x + 1:x + 2], min_val=1, max_val=SLOT_TILES[tag])
                    pe.wait_ge(sem("w1_split"), 3 * (block_of(tag) + x + 1))
                    pe.wait_ge(sem("w2_split"), 3 * (block_of(tag) + x + 1))
                    with pe.Fori(lo, hi) as t:
                        pe.wait_ge(sem(f"{tag}_tokens_high"), t + 1)
                        pe.wait_ge(sem(f"{tag}_tokens_low"), t + 1)
                        for hc in range(KH):
                            f = slice(128 * hc, 128 * hc + 128)
                            if hc == 2:
                                pe.wait_ge(sem(f"{tag}_h_low"), KH * t + 1)
                            for k in range(KD):
                                p = ps[:, 6 + hc % 2, 0:128]
                                pe.matmul(p, w1h[:, k, f], gt_hi[:, k, :], start=(k == 0), stop=False)
                                pe.matmul(p, w1h[:, k, f], gt_lo[:, k, :], start=False, stop=False)
                                ins = pe.matmul(p, w1l[:, k, f], gt_hi[:, k, :], start=False, stop=(k == KD - 1))
                            ins.then_inc(sem(f"{tag}_h_full"), 1)
                        turn_tokens(tag, t + 1)
                        pe.wait_ge(sem(f"{tag}_h_low"), KH * (t + 1))
                        pe.wait_ge(sem(f"{tag}_o_left"), t + 1)
                        pe.wait_ge(sem(f"{tag}_o_right"), t + 1)
                        for c in range(2):
                            for k in range(KH):
                                ins = three(ps[:, 4 + c, 0:384], (ht_hi[:, k, :], ht_lo[:, k, :]),
                                            (w2h[:, k, 384 * c:384 * (c + 1)], w2l[:, k, 384 * c:384 * (c + 1)]),
                                            k == 0, k == KH - 1)
                            ins.then_inc(sem(f"{tag}_o_full"), 1)
                pe.wait_ge(sem(f"{tag}_tokens_high"), hi + 1)
                pe.wait_ge(sem(f"{tag}_tokens_low"), hi + 1)
                pe.nop().then_inc(sem(f"{tag}_turned"), TABLE_COLS[tag])

            staged("n1", "m0")
            ranks("m0")
            experts("m0")
            staged("n2")
            pe.wait_ge(sem("adj_sum"), 1)
            for c in range(2):
                w = weights(gcn_pieces[c])
                with pe.Fori(0, NT // 2) as i:
                    for u in range(2):
                        m = 2 * i + u
                        pe.wait_ge(sem("gy_free"), NT * c + m + 1)
                        node_rows(KD, m, w, ps[:TP, u, 0:384]).then_inc(sem("gy_full"), 1)
                pe.wait_ge(sem("gy_free"), 2 + NT * (c + 1))
                with pe.Fori(0, NT // 2) as i:
                    for u in range(2):
                        m = 2 * i + u
                        pe.wait_ge(sem("gz_free"), NT * c + m + 1)
                        for s in range(NT):
                            x = cols(adj[:, 2 * NT + s, :], m * TP, TP, TP)
                            pe.matmul(ps[:TP, 2 + u, 0:384], x, y_hi[:TP, s, 0:384], start=(s == 0), stop=False)
                            ins = pe.matmul(ps[:TP, 2 + u, 0:384], x, y_lo[:TP, s, 0:384], start=False, stop=(s == NT - 1))
                        ins.then_inc(sem("gz_full"), 1)
            staged("n4")
            for c in range(2):
                w = weights(v_pieces[c])
                with pe.Fori(0, NT // 2) as i:
                    for u in range(2):
                        m = 2 * i + u
                        pe.wait_ge(sem("v_low"), NT * c + m + 1)
                        node_rows(KD, m, w, ps[:TP, u, 0:384]).then_inc(sem("v_full"), 1)
            pe.nop().then_inc(sem("pv_full"), 4)
            pe.wait_ge(sem("v_low"), 2 + 2 * NT)
            def queries_keys(j):
                wh, wl = weights(qk_pieces[j])
                if j:
                    pe.wait_ge(sem("exp_done"), 5 + 50 * j)
                job = 6 * j
                for which in range(2):
                    for c0, w in NODE_COLS:
                        job += 1
                        if job > 2:
                            pe.wait_ge(sem("qk_moved"), 2 * (job - 2))
                        p = ps[:, (job - 1) % 2, 0:w]
                        f = slice(128 * which, 128 * which + 128)
                        for k in range(KD):
                            pe.matmul(p, wh[:, k, f], hT_hi[:, k, c0:c0 + w], start=(k == 0), stop=False)
                            pe.matmul(p, wh[:, k, f], hT_lo[:, k, c0:c0 + w], start=False, stop=False)
                            ins = pe.matmul(p, wl[:, k, f], hT_hi[:, k, c0:c0 + w], start=False, stop=(k == KD - 1))
                        ins.then_inc(sem("qk_full"), 1)

            queries_keys(0)
            for j in range(HEADS // 2):
                pe.wait_ge(sem("qk_parts"), 6 * (j + 1))
                if j:
                    pe.wait_ge(sem("pr_free"), 4 + 2 * NT * j)
                for h2 in range(2):
                    with pe.Fori(0, NT // 2) as i:
                        for u in range(2):
                            t = 2 * i + u
                            pe.wait_ge(sem("max_free"), (2 * j + h2) * NT + t + 1)
                            for c, (c0, w) in enumerate(BANKS3):
                                ins = pe.matmul(ps[:TP, 3 * u + c, :w], q_a[:, h2, bass.ds(t * TP, TP)],
                                                k_a[:, h2, c0:c0 + w], start=True, stop=True)
                            ins.then_inc(sem("max_full"), 1)
                pe.wait_ge(sem("max_free"), 2 + (2 * j + 2) * NT)
                for h2 in range(2):
                    for t in range(NT):
                        ins = pe.matmul(ps[64:65, 3 * h2 + t // 4, (t % 4) * TP:(t % 4 + 1) * TP], row_max[:TP, h2, t:t + 1],
                                        ident[:TP, :TP], start=True, stop=True)
                    ins.then_inc(sem("max_rows"), 1)
                pe.wait_ge(sem("max_set"), 2 * (j + 1))
                pe.wait_ge(sem("ones_set"), 1)
                def scores(qc, h2):
                    n = 10 * j + 2 * qc + h2
                    for kp in range(5):
                        pe.wait_ge(sem("exp_done"), 5 * n + kp + 1)
                        for e in range(2):
                            kt = 2 * kp + e
                            p = ps[:TP, kp, QC * e:QC * (e + 1)]
                            pe.matmul(p, k_a[:, h2, kt * TP:(kt + 1) * TP], q_a[:, h2, bass.ds(qc * QC, QC)],
                                      start=True, stop=False)
                            ins = pe.matmul(p, k_b[0:96, h2, kt * TP:(kt + 1) * TP], q_b[0:96, h2, bass.ds(qc * QC, QC)],
                                            start=False, stop=True)
                        ins.then_inc(sem("s_full"), 1)

                def values(qc, h2):
                    n = 10 * j + 2 * qc + h2
                    pe.wait_ge(sem("p_low"), 2 + 5 * n + 5)
                    for u in range(2):
                        pe.wait_ge(sem("o_free"), 2 * n + u + 1)
                        p = ps[:, 5 + u, 0:HD + 1]
                        for kt in range(NT):
                            ph, pl = p_hi[:TP, h2, kt, u * TP:u * TP + 128], p_lo[:TP, h2, kt, u * TP:u * TP + 128]
                            v = v_parts[:TP, kt, 2 * j + h2, :]
                            pe.matmul(p, ph, v[:, 0:HD + 1], start=(kt == 0), stop=False)
                            pe.matmul(p[:, 0:HD], ph, v[:, HD + 1:129], start=False, stop=False)
                            ins = pe.matmul(p, pl, v[:, 0:HD + 1], start=False, stop=(kt == NT - 1))
                        ins.then_inc(sem("pv_full"), 1)

                scores(0, 0)
                with pe.Fori(0, NT // 2 - 1) as qc:
                    scores(qc, 1)
                    values(qc, 0)
                    scores(qc + 1, 0)
                    values(qc, 1)
                scores(NT // 2 - 1, 1)
                values(NT // 2 - 1, 0)
                values(NT // 2 - 1, 1)
                if j + 1 < HEADS // 2:
                    queries_keys(j + 1)
                pe.wait_ge(sem("o_free"), 2 + 2 * 5 * 2 * (j + 1))
                for t in range(3):
                    for m in range(4 * t, min(4 * t + 4, NT)):
                        ins = pe.transpose(ps[:, 5 + t, (m % 4) * TP:(m % 4 + 1) * TP], o_pair[:TP, m, :], ident[:TP, :TP])
                    ins.then_inc(sem("ot_full"), 1)
                wh, wl = weights(proj_pieces[j])
                pe.wait_ge(sem("ot_low"), 3 * (j + 1))
                with pe.Fori(0, NT // 2) as i:
                    for u in range(2):
                        m = 2 * i + u
                        for c in range(2):
                            pe.wait_ge(sem("pr_free"), 2 * NT * j + 2 * m + c + 1)
                            three(ps[:TP, 3 + 2 * u + c, 0:384], (cols(ot_hi, m * TP, TP), cols(ot_lo, m * TP, TP)),
                                  (wh[:, 0, 384 * c:384 * (c + 1)], wl[:, 0, 384 * c:384 * (c + 1)])
                                  ).then_inc(sem("pr_full"), 1)
            staged("n5", "m1")
            ranks("m1")
            pe.wait_ge(sem("gates_ready"), 1)
            for q in range(3):
                for m in range(4 * q, min(4 * q + 4, NT)):
                    ins = pe.transpose(ps[0:EXPERTS, 4 + q, (m % 4) * TP:(m % 4 + 1) * TP], gates[:TP, m, :], ident[:TP, :TP])
                ins.then_inc(sem("gt_full"), 1)
            pe.wait_ge(sem("gt_done"), 3)
            pe.wait_ge(sem("b2_in"), 16)
            experts("m1")
            pe.wait_ge(sem("m1_o_left"), 1 + SLOT_TILES["m1"])
            pe.wait_ge(sem("m1_o_right"), 1 + SLOT_TILES["m1"])
            for m in range(NT):
                for c in range(2):
                    if m >= 2:
                        pe.wait_ge(sem("gb_free"), 2 * (m - 2) + c + 1)
                    pe.matmul(ps[:TP, c + 4 * (m % 2), 0:384], gate_t[:, m * TP:(m + 1) * TP], b2_rows[:, 384 * c:384 * (c + 1)],
                              start=True, stop=True).then_inc(sem("gb_full"), 1)


def kernel(**x):
    import numpy as np
    import concourse.bacc as bacc
    from concourse.bass_utils import run_bass_kernel_spmd

    host = {k: np.asarray(v) for k, v in x.items()}
    pairs = HEADS // 2
    qkv_t = host["L1_ffn_qkv_w"].T
    w_qk = np.concatenate([qkv_t[:, 0:D].reshape(D, pairs, 128), qkv_t[:, D:2 * D].reshape(D, pairs, 128)], axis=2)
    arrays = {
        "x": host["x"], "src": host["src"], "dst": host["dst"], "typ": host["edge_type_3"],
        "node_type": host["node_type_3"].reshape(NT, TP).T,
        "emb": host["L0_gnn_node_emb"],
        "rel1": host["L0_gnn_w_rel1"], "root1": host["L0_gnn_w_root1"], "b1": host["L0_gnn_b1"],
        "rel2": host["L0_gnn_w_rel2"], "root2": host["L0_gnn_w_root2"], "b2": host["L0_gnn_b2"],
        "rel3": host["L0_gnn_w_rel3"], "root3": host["L0_gnn_w_root3"], "b3": host["L0_gnn_b3"],
        "router": host["L0_ffn_router_w"], "wi": host["L0_ffn_wi"], "wo": host["L0_ffn_wo"],
        "gcn_w": host["L1_gnn_W"], "gcn_b": host["L1_gnn_b"],
        "n1_w": host["L1_ffn_norm1_w"], "n1_b": host["L1_ffn_norm1_b"],
        "w_qk": w_qk.transpose(1, 0, 2), "w_v": qkv_t[:, 2 * D:],
        "qk_b": host["L1_ffn_qkv_b"][0:2 * D].reshape(12, 128).T, "v_b": host["L1_ffn_qkv_b"][2 * D:],
        "w_proj": host["L1_ffn_proj_w"].T, "proj_b": host["L1_ffn_proj_b"],
        "n2_w": host["L1_ffn_norm2_w"], "n2_b": host["L1_ffn_norm2_b"],
        "w_gate": host["L1_ffn_w_gate"],
        "w1": host["L1_ffn_W1"], "b1x": host["L1_ffn_b1"].reshape(EXPERTS * KH, 128).T,
        "w2": host["L1_ffn_W2"], "b2x": host["L1_ffn_b2"],
    }
    nc = bacc.Bacc("TRN2", target_bir_lowering=False, num_devices=1)
    feed, aps = {}, {}
    for name, v in arrays.items():
        v = np.ascontiguousarray(v)
        feed[f"in_{name}"] = v
        aps[name] = nc.dram_tensor(f"in_{name}", v.shape, mybir.dt.from_np(v.dtype), kind="ExternalInput").ap()
    out = nc.dram_tensor("out_nodes", (N, D), F32, kind="ExternalOutput").ap()
    build(nc, aps, out)
    return run_bass_kernel_spmd(nc, [feed], core_ids=[0]).results[0]["out_nodes"]
```
